# Optimizing a Trainium2 kernel written in Bass

```python
import numpy as np
import jax
import jax.numpy as jnp

def _softmax(x, axis=-1):
    return jax.nn.softmax(x, axis=axis)

def _gelu(x):
    return jax.nn.gelu(x, approximate=True)

def _silu(x):
    return jax.nn.silu(x)

def _sigmoid(x):
    return jax.nn.sigmoid(x)

def _layernorm(x, axis=-1, eps=1e-05):
    m = jnp.mean(x, axis=axis, keepdims=True)
    v = jnp.var(x, axis=axis, keepdims=True)
    return (x - m) / jnp.sqrt(v + eps)

def _scatter_add(tgt, idx, src, axis=0):
    return tgt.at[idx].add(src)

def _segment_sum(src, seg, n):
    return jax.ops.segment_sum(src, seg, n)
kernel_name = 'mk_adaln_d2_jaxref_r8_8990a8'

def setup_inputs(seed: int=0):
    np.random.seed(seed)
    _w = jnp.asarray

    def _L0_attn_setup():
        import jax, jax.numpy as jnp
        import numpy as np
        B, S, HID = (1, 256, 128)
        H, HKV, D = (16, 4, 64)
        THETA = 10000.0

        def _rope_tables(seq_len, head_dim):
            inv_freq = 1.0 / THETA ** (jnp.arange(0, head_dim, 2, dtype=jnp.float32) / head_dim)
            freqs = jnp.arange(seq_len, dtype=jnp.float32)[:, None] * inv_freq[None, :]
            emb = jnp.concatenate([freqs, freqs], axis=-1)
            return (jnp.cos(emb)[:, 0::2], jnp.sin(emb)[:, 0::2])

        def _apply_rope(x, cos, sin):
            xe, xo = (x[..., 0::2], x[..., 1::2])
            re = xe * cos - xo * sin
            ro = xe * sin + xo * cos
            return jnp.stack([re, ro], axis=-1).reshape(x.shape)
        key = jax.random.key(seed)
        k0, k1, k2, k3, k4 = jax.random.split(key, 5)
        return {'hidden_states': jax.random.normal(k0, (B, S, HID), dtype=jnp.float32), 'Wq': jax.random.normal(k1, (HID, H * D), dtype=jnp.float32) * 0.02, 'Wk': jax.random.normal(k2, (HID, HKV * D), dtype=jnp.float32) * 0.02, 'Wv': jax.random.normal(k3, (HID, HKV * D), dtype=jnp.float32) * 0.02, 'Wo': jax.random.normal(k4, (H * D, HID), dtype=jnp.float32) * 0.02}
    _L0_attn_in = _L0_attn_setup()

    def _L0_ffn_setup():
        import jax, jax.numpy as jnp
        import numpy as np
        TOP_K = 2
        ROUTED_SCALING = 1.0
        key = jax.random.key(seed)
        k1, k2, k3, k4 = jax.random.split(key, 4)
        S, B, H = (128, 2, 128)
        E, FFN = (8, 176)
        return {'hidden_states': jax.random.normal(k1, (S, B, H), dtype=jnp.float32), 'gate_w': jax.random.normal(k2, (E, H), dtype=jnp.float32) * 0.02, 'w1': jax.random.normal(k3, (E, H, 2 * FFN), dtype=jnp.float32) * 0.02, 'w2': jax.random.normal(k4, (E, FFN, H), dtype=jnp.float32) * 0.02}
    _L0_ffn_in = _L0_ffn_setup()
    _L0_c = _w((lambda *s: np.random.randn(*s).astype(np.float32) * 0.05)(4, 128))
    _L0_wmod = _w((lambda *s: np.random.randn(*s).astype(np.float32) * 0.05)(128, 6 * 128) * 128 ** (-0.5))

    def _L1_attn_setup():
        import jax, jax.numpy as jnp
        import numpy as np
        D_MODEL, D_STATE, D_CONV = (128, 16, 4)
        BATCH, SEQ_LEN = (2, 256)

        def _selective_scan(u, A, B_sel, C_sel, delta):
            deltaA = jnp.exp(delta[..., None, None] * A[None, None])
            deltaB_u = delta[..., None, None] * B_sel[:, :, None, :] * u[..., None]

            def step(h, inp):
                a_t, bu_t, c_t = inp
                h = a_t * h + bu_t
                y_t = jnp.einsum('bdn,bn->bd', h, c_t)
                return (h, y_t)
            h0 = jnp.zeros((u.shape[0], u.shape[2], A.shape[1]), dtype=u.dtype)
            xs = (jnp.swapaxes(deltaA, 0, 1), jnp.swapaxes(deltaB_u, 0, 1), jnp.swapaxes(C_sel, 0, 1))
            _, ys = jax.lax.scan(step, h0, xs)
            return jnp.swapaxes(ys, 0, 1)
        key = jax.random.key(seed)
        ks = jax.random.split(key, 6)
        x = jax.random.normal(ks[0], (BATCH, SEQ_LEN, D_MODEL), dtype=jnp.float32)
        W_in = jax.random.normal(ks[1], (D_MODEL, 2 * D_MODEL), dtype=jnp.float32) * 0.02
        conv_w = jax.random.normal(ks[2], (D_MODEL, 1, D_CONV), dtype=jnp.float32) * 0.1
        conv_b = jax.random.normal(ks[3], (D_MODEL,), dtype=jnp.float32) * 0.01
        W_xproj = jax.random.normal(ks[4], (D_MODEL, 2 * D_STATE + 1), dtype=jnp.float32) * 0.02
        log_A = jnp.broadcast_to(jnp.log(jnp.arange(1, D_STATE + 1, dtype=jnp.float32))[None, :], (D_MODEL, D_STATE))
        D_param = jnp.ones((D_MODEL,), dtype=jnp.float32)
        W_out = jax.random.normal(ks[5], (D_MODEL, D_MODEL), dtype=jnp.float32) * 0.02
        return {'x': x, 'W_in': W_in, 'conv_w': conv_w, 'conv_b': conv_b, 'W_xproj': W_xproj, 'log_A': log_A, 'D_param': D_param, 'W_out': W_out}
    _L1_attn_in = _L1_attn_setup()

    def _L1_ffn_setup():
        import jax, jax.numpy as jnp
        import numpy as np
        NUM_EXPERTS = 8
        TOP_K = 2
        CAPACITY_FACTOR = 1.0

        def _dispatch_compute(xf, top_expert, w1, w2, capacity):
            tokens, hs = xf.shape
            tpe = jnp.bincount(top_expert, length=NUM_EXPERTS)
            indices = jnp.argsort(top_expert)
            offsets = jnp.concatenate([jnp.zeros((1,), tpe.dtype), jnp.cumsum(tpe)[:-1]])
            slot = jnp.arange(capacity)
            pos = offsets[:, None] + slot[None, :]
            valid = slot[None, :] < tpe[:, None]
            tok_idx = indices[jnp.minimum(pos, tokens - 1)]
            xe = jnp.where(valid[..., None], xf[tok_idx], 0.0)
            h = jax.nn.gelu(jnp.einsum('ech,ehf->ecf', xe, w1), approximate=True)
            ye = jnp.einsum('ecf,efh->ech', h, w2)
            tok_safe = jnp.where(valid, tok_idx, tokens)
            out = jnp.zeros((tokens + 1, hs), xf.dtype).at[tok_safe.reshape(-1)].add(ye.reshape(-1, hs))
            return out[:tokens]
        key = jax.random.key(seed)
        k1, k2, k3, k4 = jax.random.split(key, 4)
        hs, ffn = (128, 512)
        x = jax.random.normal(k1, (256, 2, hs), dtype=jnp.float32)
        router_w = jax.random.normal(k2, (hs, NUM_EXPERTS), dtype=jnp.float32) * hs ** (-0.5)
        w1 = jax.random.normal(k3, (NUM_EXPERTS, hs, ffn), dtype=jnp.float32) * 0.02
        w2 = jax.random.normal(k4, (NUM_EXPERTS, ffn, hs), dtype=jnp.float32) * 0.02
        bias = jnp.zeros((1, 1, hs), dtype=jnp.float32)
        return {'x': x, 'router_w': router_w, 'w1': w1, 'w2': w2, 'bias': bias}
    _L1_ffn_in = _L1_ffn_setup()
    _L1_c = _w((lambda *s: np.random.randn(*s).astype(np.float32) * 0.05)(4, 128))
    _L1_wmod = _w((lambda *s: np.random.randn(*s).astype(np.float32) * 0.05)(128, 6 * 128) * 128 ** (-0.5))
    _d = {'L0_attn_hidden_states': _L0_attn_in['hidden_states'], 'L0_attn_Wq': _L0_attn_in['Wq'], 'L0_attn_Wk': _L0_attn_in['Wk'], 'L0_attn_Wv': _L0_attn_in['Wv'], 'L0_attn_Wo': _L0_attn_in['Wo'], 'L0_ffn_gate_w': _L0_ffn_in['gate_w'], 'L0_ffn_w1': _L0_ffn_in['w1'], 'L0_ffn_w2': _L0_ffn_in['w2'], 'L0_c': _L0_c, 'L0_wmod': _L0_wmod, 'L1_attn_W_in': _L1_attn_in['W_in'], 'L1_attn_conv_w': _L1_attn_in['conv_w'], 'L1_attn_conv_b': _L1_attn_in['conv_b'], 'L1_attn_W_xproj': _L1_attn_in['W_xproj'], 'L1_attn_log_A': _L1_attn_in['log_A'], 'L1_attn_D_param': _L1_attn_in['D_param'], 'L1_attn_W_out': _L1_attn_in['W_out'], 'L1_ffn_router_w': _L1_ffn_in['router_w'], 'L1_ffn_w1': _L1_ffn_in['w1'], 'L1_ffn_w2': _L1_ffn_in['w2'], 'L1_ffn_bias': _L1_ffn_in['bias'], 'L1_c': _L1_c, 'L1_wmod': _L1_wmod}
    _x0 = _d['L0_attn_hidden_states']
    _d['L0_attn_hidden_states'] = jax.random.normal(jax.random.fold_in(jax.random.key(seed), 1), (4, 1024, 128), dtype=_x0.dtype)
    del _x0
    return _d

def reference(L0_attn_hidden_states, L0_attn_Wq, L0_attn_Wk, L0_attn_Wv, L0_attn_Wo, L0_ffn_gate_w, L0_ffn_w1, L0_ffn_w2, L0_c, L0_wmod, L1_attn_W_in, L1_attn_conv_w, L1_attn_conv_b, L1_attn_W_xproj, L1_attn_log_A, L1_attn_D_param, L1_attn_W_out, L1_ffn_router_w, L1_ffn_w1, L1_ffn_w2, L1_ffn_bias, L1_c, L1_wmod):

    def _L0_attn_ref(hidden_states, Wq, Wk, Wv, Wo):
        import jax, jax.numpy as jnp
        import numpy as np
        B, S, HID = (1, 256, 128)
        H, HKV, D = (16, 4, 64)
        THETA = 10000.0

        def _rope_tables(seq_len, head_dim):
            inv_freq = 1.0 / THETA ** (jnp.arange(0, head_dim, 2, dtype=jnp.float32) / head_dim)
            freqs = jnp.arange(seq_len, dtype=jnp.float32)[:, None] * inv_freq[None, :]
            emb = jnp.concatenate([freqs, freqs], axis=-1)
            return (jnp.cos(emb)[:, 0::2], jnp.sin(emb)[:, 0::2])

        def _apply_rope(x, cos, sin):
            xe, xo = (x[..., 0::2], x[..., 1::2])
            re = xe * cos - xo * sin
            ro = xe * sin + xo * cos
            return jnp.stack([re, ro], axis=-1).reshape(x.shape)
        b, s, _ = hidden_states.shape
        q = (hidden_states @ Wq).reshape(b, s, H, D).transpose(0, 2, 1, 3)
        k = (hidden_states @ Wk).reshape(b, s, HKV, D).transpose(0, 2, 1, 3)
        v = (hidden_states @ Wv).reshape(b, s, HKV, D).transpose(0, 2, 1, 3)
        cos, sin = _rope_tables(s, D)
        q = _apply_rope(q, cos, sin)
        k = _apply_rope(k, cos, sin)
        G = H // HKV
        qg = q.reshape(b, HKV, G, s, D)
        scale = jnp.float32(D) ** (-0.5)
        scores = jnp.einsum('bkgqd,bkpd->bkgqp', qg, k) * scale
        causal = jnp.tril(jnp.ones((s, s), dtype=bool))
        scores = jnp.where(causal, scores, jnp.float32(-1e+30))
        probs = jax.nn.softmax(scores, axis=-1)
        out = jnp.einsum('bkgqp,bkpd->bkgqd', probs, v).reshape(b, H, s, D)
        out = out.transpose(0, 2, 1, 3).reshape(b, s, H * D)
        return out @ Wo

    def _L0_ffn_ref(hidden_states, gate_w, w1, w2):
        import jax, jax.numpy as jnp
        import numpy as np
        TOP_K = 2
        ROUTED_SCALING = 1.0
        x = jnp.transpose(hidden_states, (1, 0, 2))
        B, S, H = x.shape
        E = gate_w.shape[0]
        xt = x.reshape(-1, H)
        T = xt.shape[0]
        scores = jax.nn.softmax(xt @ gate_w.T, axis=-1)
        topk_w, topk_idx = jax.lax.top_k(scores, TOP_K)
        topk_w = topk_w / (jnp.sum(topk_w, axis=-1, keepdims=True) + 1e-20)
        topk_w = topk_w * ROUTED_SCALING
        combine = jnp.zeros((T, E), dtype=xt.dtype)
        combine = combine.at[jnp.arange(T)[:, None], topk_idx].set(topk_w)
        out = jnp.zeros_like(xt)
        for e in range(E):
            h = xt @ w1[e]
            g, u = jnp.split(h, 2, axis=-1)
            y = jax.nn.silu(g) * u @ w2[e]
            out = out + combine[:, e:e + 1] * y
        out = out.reshape(B, S, H)
        return jnp.transpose(out, (1, 0, 2))

    def _L1_attn_ref(x, W_in, conv_w, conv_b, W_xproj, log_A, D_param, W_out):
        import jax, jax.numpy as jnp
        import numpy as np
        D_MODEL, D_STATE, D_CONV = (128, 16, 4)
        BATCH, SEQ_LEN = (2, 256)

        def _selective_scan(u, A, B_sel, C_sel, delta):
            deltaA = jnp.exp(delta[..., None, None] * A[None, None])
            deltaB_u = delta[..., None, None] * B_sel[:, :, None, :] * u[..., None]

            def step(h, inp):
                a_t, bu_t, c_t = inp
                h = a_t * h + bu_t
                y_t = jnp.einsum('bdn,bn->bd', h, c_t)
                return (h, y_t)
            h0 = jnp.zeros((u.shape[0], u.shape[2], A.shape[1]), dtype=u.dtype)
            xs = (jnp.swapaxes(deltaA, 0, 1), jnp.swapaxes(deltaB_u, 0, 1), jnp.swapaxes(C_sel, 0, 1))
            _, ys = jax.lax.scan(step, h0, xs)
            return jnp.swapaxes(ys, 0, 1)
        batch, seq_len, d_model = x.shape
        xz = x @ W_in
        x_main, z = jnp.split(xz, 2, axis=-1)
        x_ncl = jnp.swapaxes(x_main, 1, 2)
        x_conv = jax.lax.conv_general_dilated(x_ncl, conv_w, window_strides=(1,), padding=[(D_CONV - 1, 0)], dimension_numbers=('NCH', 'OIH', 'NCH'), feature_group_count=d_model)
        x_conv = x_conv + conv_b[None, :, None]
        x_conv = jax.nn.silu(jnp.swapaxes(x_conv, 1, 2))
        proj = x_conv @ W_xproj
        B_sel = proj[..., :D_STATE]
        C_sel = proj[..., D_STATE:2 * D_STATE]
        delta = jax.nn.softplus(proj[..., -1])
        A = -jnp.exp(log_A)
        y = _selective_scan(x_conv, A, B_sel, C_sel, delta)
        y = y + x_conv * D_param[None, None, :]
        y = y * jax.nn.silu(z)
        return y @ W_out

    def _L1_ffn_ref(x, router_w, w1, w2, bias):
        import jax, jax.numpy as jnp
        import numpy as np
        NUM_EXPERTS = 8
        TOP_K = 2
        CAPACITY_FACTOR = 1.0

        def _dispatch_compute(xf, top_expert, w1, w2, capacity):
            tokens, hs = xf.shape
            tpe = jnp.bincount(top_expert, length=NUM_EXPERTS)
            indices = jnp.argsort(top_expert)
            offsets = jnp.concatenate([jnp.zeros((1,), tpe.dtype), jnp.cumsum(tpe)[:-1]])
            slot = jnp.arange(capacity)
            pos = offsets[:, None] + slot[None, :]
            valid = slot[None, :] < tpe[:, None]
            tok_idx = indices[jnp.minimum(pos, tokens - 1)]
            xe = jnp.where(valid[..., None], xf[tok_idx], 0.0)
            h = jax.nn.gelu(jnp.einsum('ech,ehf->ecf', xe, w1), approximate=True)
            ye = jnp.einsum('ecf,efh->ech', h, w2)
            tok_safe = jnp.where(valid, tok_idx, tokens)
            out = jnp.zeros((tokens + 1, hs), xf.dtype).at[tok_safe.reshape(-1)].add(ye.reshape(-1, hs))
            return out[:tokens]
        sl, bs, hs = x.shape
        tokens = sl * bs
        capacity = int(CAPACITY_FACTOR * tokens / NUM_EXPERTS)
        xf = x.reshape(tokens, hs)
        scores = jax.nn.softmax(xf @ router_w, axis=-1)
        expert_weights, top_experts = jax.lax.top_k(scores, TOP_K)
        out = jnp.zeros_like(xf)
        for k in range(TOP_K):
            y = _dispatch_compute(xf, top_experts[:, k].astype(jnp.int32), w1, w2, capacity)
            out = out + y * expert_weights[:, k][:, None]
        return out.reshape(sl, bs, hs) + bias
    x = L0_attn_hidden_states
    mod = (_silu(L0_c) @ L0_wmod).reshape(L0_c.shape[0], 6, 1, -1)
    sa, ca, ga, sb, cb, gb = (mod[:, 0], mod[:, 1], mod[:, 2], mod[:, 3], mod[:, 4], mod[:, 5])
    ga = (2 * (ga >= 0) - 1) * jnp.maximum(jnp.abs(ga), 0.25)
    gb = (2 * (gb >= 0) - 1) * jnp.maximum(jnp.abs(gb), 0.25)
    h = _layernorm(x, axis=-1) * (1 + ca) + sa
    x = x + ga * _L0_attn_ref(h, L0_attn_Wq, L0_attn_Wk, L0_attn_Wv, L0_attn_Wo)
    h = _layernorm(x, axis=-1) * (1 + cb) + sb
    x = x + gb * _L0_ffn_ref(h, L0_ffn_gate_w, L0_ffn_w1, L0_ffn_w2)
    mod = (_silu(L1_c) @ L1_wmod).reshape(L1_c.shape[0], 6, 1, -1)
    sa, ca, ga, sb, cb, gb = (mod[:, 0], mod[:, 1], mod[:, 2], mod[:, 3], mod[:, 4], mod[:, 5])
    ga = (2 * (ga >= 0) - 1) * jnp.maximum(jnp.abs(ga), 0.25)
    gb = (2 * (gb >= 0) - 1) * jnp.maximum(jnp.abs(gb), 0.25)
    h = _layernorm(x, axis=-1) * (1 + ca) + sa
    x = x + ga * _L1_attn_ref(h, L1_attn_W_in, L1_attn_conv_w, L1_attn_conv_b, L1_attn_W_xproj, L1_attn_log_A, L1_attn_D_param, L1_attn_W_out)
    h = _layernorm(x, axis=-1) * (1 + cb) + sb
    x = x + gb * _L1_ffn_ref(h, L1_ffn_router_w, L1_ffn_w1, L1_ffn_w2, L1_ffn_bias)
    return x

_drawn_inputs = setup_inputs


def setup_inputs(seed=0):
    import zlib

    import numpy as np

    out = dict(_drawn_inputs(seed))
    spreads = {'L1_attn_D_param': (1.0, 0.6), 'L1_ffn_bias': (0.0, 2.0)}
    factors = {'L0_attn_Wq': 8.0,
     'L0_attn_Wk': 8.0,
     'L0_attn_Wv': 8.0,
     'L0_attn_Wo': 8.0,
     'L0_ffn_gate_w': 8.0,
     'L0_ffn_w1': 8.0,
     'L0_ffn_w2': 8.0,
     'L0_c': 8.0,
     'L0_wmod': 8.0,
     'L1_attn_W_in': 8.0,
     'L1_attn_conv_w': 8.0,
     'L1_attn_conv_b': 8.0,
     'L1_attn_W_xproj': 8.0,
     'L1_attn_log_A': 8.0,
     'L1_attn_W_out': 8.0,
     'L1_ffn_router_w': 26.887,
     'L1_ffn_w1': 29.725,
     'L1_ffn_w2': 25.873}
    for name, (base, spread) in spreads.items():
        noise = np.random.default_rng([zlib.crc32(name.encode()), seed]).standard_normal(out[name].shape)
        drawn = base * np.exp(spread * noise) if base else spread * noise
        out[name] = jnp.asarray(drawn.astype(out[name].dtype))
    for name, factor in factors.items():
        out[name] = (out[name] * factor).astype(out[name].dtype)
    return out
```

```python
from contextlib import ExitStack

import numpy as np

import concourse.bass as bass
from concourse import mybir

F32 = mybir.dt.float32
F32R = mybir.dt.float32r
BF16 = mybir.dt.bfloat16
ALU = mybir.AluOpType
ACT = mybir.ActivationFunctionType
AX = mybir.AxisListType.X

P = 128
BATCH, SEQ, HID = 4, 1024, 128
TOK = BATCH * SEQ
TILES = TOK // P
TPB = SEQ // P
BANK = 512
H, HKV, D = 16, 4, 64
E0, F0 = 8, 176
E1, F1 = 8, 512
NST = 16
TAPS = 4
CAPACITY = TOK // E1
THETA = 10000.0
EPS = 1e-5
NEG = -1e30


class Count:

    def __init__(self, sem):
        self.sem, self.value = sem, 0


class Queues:

    ENGINES = ("tensor", "vector", "scalar", "gpsimd", "sync")

    def __init__(self, nc, ctx):
        self.nc, self.ctx = nc, ctx
        self.todo = {e: [] for e in self.ENGINES}
        self.counts = {}
        self.met = {}

    def count(self, name):
        if name not in self.counts:
            self.counts[name] = Count(self.ctx.enter_context(self.nc.semaphore(name)))
        return self.counts[name]

    def put(self, engine, issue, wait=(), signal=None, step=1):
        todo = self.todo[engine]
        for name, value in wait:
            if self.met.get((engine, name), 0) < value:
                self.met[engine, name] = value
                todo.append((None, self.counts[name].sem, value))
        if signal is None:
            todo.append((issue, None, 0))
            return None
        count = self.count(signal)
        count.value += step
        todo.append((issue, count.sem, step))
        return signal, count.value

    def pe(self, issue, wait=(), signal=None):
        return self.put("tensor", issue, wait, signal)

    def dve(self, issue, wait=(), signal=None):
        return self.put("vector", issue, wait, signal)

    def act(self, issue, wait=(), signal=None):
        return self.put("scalar", issue, wait, signal)

    def pool(self, issue, wait=(), signal=None):
        return self.put("gpsimd", issue, wait, signal)

    def dma(self, out, in_, signal, wait=(), engine="sync"):
        if in_.dtype == F32R:
            out, in_ = out.bitcast(F32), in_.bitcast(F32)
        return self.put(engine, lambda e: e.dma_start(out, in_), wait, signal, 16)

    def run(self):
        todo, self.todo = self.todo, {e: [] for e in self.ENGINES}

        def emit(e, items):
            for issue, sem, n in items:
                if issue is None:
                    e.wait_ge(sem, n)
                elif sem is None:
                    issue(e)
                else:
                    issue(e).then_inc(sem, n)

        with self.nc.Block() as block:
            for name in self.ENGINES:
                if todo[name]:
                    def body(e, items=todo[name]):
                        emit(e, items)
                    {"tensor": block.tensor, "vector": block.vector, "scalar": block.scalar,
                     "gpsimd": block.gpsimd, "sync": block.sync}[name](body)


def modulation(q, nc, layer, c_t, wmod, mod_t, gate_bc):
    with ExitStack() as ctx:
        ct = ctx.enter_context(nc.sbuf_tensor(f"ct{layer}", [P, BATCH], F32))
        sct = ctx.enter_context(nc.sbuf_tensor(f"sct{layer}", [P, BATCH], F32))
        wm = ctx.enter_context(nc.sbuf_tensor(f"wm{layer}", [P, 6 * HID], F32))
        sign = ctx.enter_context(nc.sbuf_tensor(f"sign{layer}", [P, BATCH, HID], F32))
        size = ctx.enter_context(nc.sbuf_tensor(f"size{layer}", [P, BATCH, HID], F32))
        ps_col = ctx.enter_context(nc.psum_tensor(f"ps_col{layer}", [P, 6, BATCH], F32))
        ps_row = [ctx.enter_context(nc.psum_tensor(f"ps_row{layer}{w}", [P, BATCH, HID], F32)) for w in range(2)]
        in_c = q.dma(ct[:, :], c_t, "mod_in")
        in_w = q.dma(wm[:, :], wmod, "mod_in")
        got_c = q.act(lambda e: e.activation(sct[:, :], ct[:, :], ACT.Silu), [in_w], "mod_silu")
        for j in range(6):
            cols = q.pe(lambda e, j=j: e.matmul(ps_col[:, j, :], wm[:, j * HID:(j + 1) * HID], sct[:, :],
                                                start=True, stop=True), [got_c, in_w], "mod_pe")
        t = q.dve(lambda e: e.tensor_copy(mod_t[:, :, :], ps_col[:, :, :]), [cols], "mod_dve")
        for j in (1, 4):
            q.dve(lambda e, j=j: e.tensor_scalar(mod_t[:, j, :], ps_col[:, j, :], 1.0, None, ALU.add), [t], "mod_dve")
        for w, j in enumerate((2, 5)):
            for b in range(BATCH):
                rows = q.pe(lambda e, w=w, j=j, b=b: e.matmul(
                    ps_row[w][:, b, :], sct[:, b:b + 1].to_broadcast([P, P]), wm[:, j * HID:(j + 1) * HID],
                    start=True, stop=True), (), "mod_pe")
            t = q.dve(lambda e, w=w: e.tensor_scalar(sign[:, :, :], ps_row[w][:, :, :], 0.0, 2.0, ALU.is_ge, ALU.mult),
                      [rows, t], "mod_dve")
            t = q.dve(lambda e: e.tensor_scalar(sign[:, :, :], sign[:, :, :], -1.0, None, ALU.add), [t], "mod_dve")
            t = q.dve(lambda e, w=w: e.tensor_tensor(size[:, :, :], ps_row[w][:, :, :], sign[:, :, :], ALU.mult),
                      [t], "mod_dve")
            t = q.dve(lambda e, w=w: e.scalar_tensor_tensor(gate_bc[w][:, :, :], size[:, :, :], 0.25, sign[:, :, :],
                                                            ALU.max, ALU.mult), [t], "mod_dve")
        q.run()


def layernorm_t(q, nc, name, x, mod_t, shift, scale, h_t, ident, eps):
    with ExitStack() as ctx:
        stats = ctx.enter_context(nc.sbuf_tensor(f"stats{name}", [P, TILES, 6], F32))
        mv = ctx.enter_context(nc.sbuf_tensor(f"mv{name}", [P, TILES, 2], F32))
        std = ctx.enter_context(nc.sbuf_tensor(f"std{name}", [P, TILES], F32))
        rstd = ctx.enter_context(nc.sbuf_tensor(f"rstd{name}", [P, TILES], F32))
        nmr = ctx.enter_context(nc.sbuf_tensor(f"nmr{name}", [P, TILES], F32))
        xn = ctx.enter_context(nc.sbuf_tensor(f"xn{name}", [P, TILES, HID], F32))
        ps = [ctx.enter_context(nc.psum_tensor(f"ps_ln{name}{i}", [P, BANK], F32)) for i in range(4)]
        for i in range(TILES):
            t = q.dve(lambda e, i=i: e.bn_stats(stats[:, i, :], x[:, i, :]), (), "ln_stats")
        for i in range(TILES):
            t = q.dve(lambda e, i=i: e.bn_aggr(mv[:, i, :], stats[:, i, :]), [t], "ln_stats")
        t_std = q.act(lambda e: e.activation(std[:, :], mv[:, :, 1], ACT.Sqrt, bias=eps[:, 0:1]), [t], "ln_std")
        t = q.dve(lambda e: e.reciprocal(rstd[:, :], std[:, :]), [t_std], "ln_stats")
        t = q.dve(lambda e: e.scalar_tensor_tensor(nmr[:, :], mv[:, :, 0], -1.0, rstd[:, :], ALU.mult, ALU.mult),
                  [t], "ln_stats")
        free = [None] * 4
        for i in range(TILES):
            put = q.dve if i % 2 else q.pool
            t_n = put(lambda e, i=i: e.tensor_scalar(xn[:, i, :], x[:, i, :], rstd[:, i:i + 1], nmr[:, i:i + 1],
                                                     ALU.mult, ALU.add), [t], "ln_norm_dve" if i % 2 else "ln_norm_pool")
            n = i // 4
            w = [t_n] + ([free[n % 4]] if i % 4 == 0 and free[n % 4] else [])
            t_t = q.pe(lambda e, i=i, n=n: e.transpose(ps[n % 4][:, (i % 4) * P:(i % 4 + 1) * P], xn[:, i, :],
                                                       ident[:, :]), w, "ln_tr")
            if i % 4 == 3:
                b = i // TPB
                cols = slice(n * BANK, (n + 1) * BANK)
                if n % 2:
                    free[n % 4] = q.dve(lambda e, n=n, b=b, cols=cols: e.tensor_scalar(
                        h_t[:, cols], ps[n % 4][:, :], mod_t[:, scale, b:b + 1], mod_t[:, shift, b:b + 1],
                        ALU.mult, ALU.add), [t_t], "ln_out_dve")
                else:
                    free[n % 4] = q.act(lambda e, n=n, b=b, cols=cols: e.activation(
                        h_t[:, cols], ps[n % 4][:, :], ACT.Identity, bias=mod_t[:, shift, b:b + 1],
                        scale=mod_t[:, scale, b:b + 1]), [t_t], "ln_out_act")
        q.run()


def attention(q, nc, a, h_t, gate_bc, ident, ident_b):
    G = H // HKV
    NPAIR = G // 2
    NQB = SEQ // P
    NCH = SEQ // BANK
    x = h_t[:, :].rearrange("p (t n) -> p t n", n=HID)
    with ExitStack() as ctx:
        def sb(name, shape, dt=F32):
            return ctx.enter_context(nc.sbuf_tensor(name, shape, dt))

        def pb(name, shape):
            return ctx.enter_context(nc.psum_tensor(name, shape, F32))

        wq, wqs = sb("wq", [P, H * D]), sb("wqs", [P, H * D])
        wk, wks = sb("wk", [P, HKV, 2, D]), sb("wks", [P, HKV, 2, D])
        wv = sb("wv", [P, HKV * D])
        wo = sb("wo", [P, H // 2, HID])
        cos, sin = sb("cos", [P, SEQ]), sb("sin", [P, SEQ])
        mask_b = sb("mask_b", [P, 2, P], BF16)
        x1 = [sb(f"x1_{i}", [P, G, SEQ], F32R) for i in range(2)]
        x2 = [sb(f"x2_{i}", [P, G, SEQ], F32R) for i in range(2)]
        k1 = [sb(f"k1_{i}", [P, SEQ], F32R) for i in range(2)]
        kl_dup = sb("kl_dup", [P, SEQ], F32R)
        k2 = [[sb(f"k2_{i}{j}", [P, SEQ], F32R) for j in range(2)] for i in range(2)]
        v = [sb(f"v_{i}", [P, NQB, HKV * D]) for i in range(2)]
        t1, t2, rot = sb("t1", [P, BANK]), sb("t2", [P, BANK]), sb("rot", [P, BANK])
        mask_f = t1[:, 0:2 * P].rearrange("p (i n) -> p i n", i=2)
        prob = [sb(f"prob{i}", [P, BANK]) for i in range(4)]
        attn_t = sb("attn_t", [P, H // 2, SEQ])
        neg_m = [sb(f"neg_m{i}", [P, G * NQB]) for i in range(2)]
        row_l = [sb(f"row_l{i}", [P, G * NQB]) for i in range(2)]
        ln_l = sb("ln_l", [P, G * NQB])
        neg_lse = sb("neg_lse", [P, G * NQB])
        lse_hi = [sb(f"lse_hi{i}", [G * NQB, P], F32R) for i in range(2)]
        lse_lo = [sb(f"lse_lo{i}", [G * NQB, P], F32R) for i in range(2)]
        scaled = sb("scaled", [P, 4, HID])

        ps_a = [pb(f"ps_a{i}", [P, 2 * BANK]) for i in range(2)]
        ps_s = [pb(f"ps_s{i}", [P, BANK]) for i in range(2)]
        ps_o = pb("ps_o", [P, BANK])
        ps_m = pb("ps_m", [P, BANK])

        loads = [(w[:, :, i, :], a[n].rearrange("k (g d) -> k g d", g=HKV))
                 for w, n in ((wk, "wk"), (wks, "wks")) for i in range(2)]
        loads += [(wq[:, :], a["wq"]), (wqs[:, :], a["wqs"]), (cos[:, :], a["cos"]), (sin[:, :], a["sin"]),
                 (wv[:, :], a["wv"]), (mask_f, a["masks"]),
                 (wo[:, :, :], a["wo"].rearrange("(c p) n -> p c n", p=P))]
        for out, in_ in loads:
            loaded = q.dma(out, in_, "attn_in")
        t_mask = q.dve(lambda e: e.tensor_copy(mask_b[:, :, :], mask_f), [loaded], "attn_const_dve")
        for i in range(2):
            for h in range(G):
                lo = 0 if h % 2 else D
                q.pool(lambda e, i=i, h=h, lo=lo: e.memset(x2[i][lo:lo + D, h, :].bitcast(F32), 0.0), (), "attn_const")
            for odd in range(2):
                lo = 0 if odd else D
                t = q.pool(lambda e, i=i, odd=odd, lo=lo: e.memset(k2[i][odd][lo:lo + D, :].bitcast(F32), 0.0),
                           (), "attn_const")
                consts = q.pool(lambda e, i=i, odd=odd, lo=lo: e.memset(k2[i][odd][lo:lo + 2, :].bitcast(F32), 1.0),
                                [t], "attn_const")

        a_free = [[], []]
        state = {"unit": 0, "m_free": [], "v_done": {}, "rot_done": [t_mask], "o_free": [], "lse_free": {}}

        def take_a():
            i = state["unit"] % 2
            state["unit"] += 1
            return i, ps_a[i], a_free[i]

        def project_v(b):
            for n in range(NQB // 2):
                for j in range(2):
                    t0 = b * SEQ + (2 * n + j) * P
                    t = q.pe(lambda e, j=j, t0=t0: e.matmul(ps_m[:, j * HKV * D:(j + 1) * HKV * D], h_t[:, t0:t0 + P],
                                                            wv[:, :], start=True, stop=True),
                             [loaded] + state["m_free"] if j == 0 else (), "v_pe")
                t = q.act(lambda e, n=n, b=b: e.activation(
                    v[b % 2][:, 2 * n:2 * n + 2, :], ps_m[:, :].rearrange("p (j n) -> p j n", j=2), ACT.Copy),
                    [t] + pv_done.get(b - 2, []), "v_copy")
                state["m_free"] = [t]
            state["v_done"][b] = t

        pv_done = {}
        x_free, k_free = {}, {}
        a_done = {}
        ready_k, ready_x = {}, {}

        def project(g):
            b, kv = g // HKV, g % HKV
            buf = g % 2
            steps = []

            def rotated(lhs, lhs_swapped, c):
                _, ps, free = take_a()
                i = (state["unit"] - 1) % 2
                cols = slice(b * SEQ + c * BANK, b * SEQ + (c + 1) * BANK)
                q.pe(lambda e: e.matmul(ps[:, 0:BANK], lhs, h_t[:, cols], start=True, stop=True), [loaded] + free)
                t = q.pe(lambda e: e.matmul(ps[:, BANK:2 * BANK], lhs_swapped, h_t[:, cols], start=True, stop=True),
                         (), "proj_pe")
                cc = slice(c * BANK, (c + 1) * BANK)
                q.dve(lambda e: e.tensor_tensor(t1[:, :], ps[:, 0:BANK], cos[:, cc], ALU.mult),
                      [t] + state["rot_done"], "rot_dve")
                t = q.dve(lambda e: e.tensor_tensor(t2[:, :], ps[:, BANK:2 * BANK], sin[:, cc], ALU.mult), (), "rot_dve")
                a_free[i] = [t]
                t = q.pool(lambda e: e.tensor_tensor(rot[:, :], t1[:, :], t2[:, :], ALU.add), [t] + state["rot_done"], "rot_pool")
                return t

            def k_step(c):
                def run():
                    cc = slice(c * BANK, (c + 1) * BANK)
                    t = rotated(wk[:, kv, :, :], wks[:, kv, :, :], c)
                    scale = float(D) ** -0.5
                    t = q.dve(lambda e: e.tensor_scalar(k1[buf][:, cc], rot[:, :], scale, None, ALU.mult),
                              [t, consts] + k_free.get(g - 2, []), "k_split")
                    t = q.dve(lambda e: e.scalar_tensor_tensor(kl_dup[:, cc], rot[:, :], scale,
                                                               k1[buf][:, cc].bitcast(F32), ALU.mult, ALU.subtract),
                              [t] + a_done.get(g - 1, []), "k_split")
                    state["rot_done"] = [t]
                    for odd in range(2):
                        lo = D if odd else 0
                        t = q.dve(lambda e, odd=odd, lo=lo: e.tensor_copy(
                            k2[buf][odd][lo:lo + D, cc], kl_dup[lo:lo + D, cc].bitcast(F32)), [t], "k_split")
                    ready_k[g] = [t]
                return run

            def q_step(pair, c):
                def run():
                    cc = slice(c * BANK, (c + 1) * BANK)
                    w0 = (kv * NPAIR + pair) * P
                    t = rotated(wq[:, w0:w0 + P], wqs[:, w0:w0 + P], c)
                    for odd in range(2):
                        lo, other = (D, 0) if odd else (0, D)
                        h = 2 * pair + odd
                        t_hi = q.dve(lambda e, lo=lo, h=h: e.tensor_copy(x1[buf][lo:lo + D, h, cc], rot[lo:lo + D, :]),
                                     [t] + x_free.get(g - 2, []), "q_split")
                        t_lo = q.dve(lambda e, lo=lo, other=other, h=h: e.tensor_tensor(
                            x1[buf][other:other + D, h, cc], rot[lo:lo + D, :], x1[buf][lo:lo + D, h, cc].bitcast(F32),
                            ALU.subtract), [t_hi], "q_split")
                        ready_x[g, h] = [t_lo]
                        ready_x[g, h, c] = q.dma(x2[buf][lo:lo + D, h, cc], x1[buf][lo:lo + D, h, cc],
                                                 f"x2_q{buf}", [t_hi, consts] + x_free.get(g - 2, []))
                        state["rot_done"] = [t_lo]
                return run

            for c in range(NCH):
                steps.append(k_step(c))
            for pair in range(NPAIR):
                for c in range(NCH):
                    steps.append(q_step(pair, c))
            return steps

        def first_pass(g):
            buf = g % 2
            units = []

            def unit(h, qb):
                def run():
                    i, ps, free = take_a()
                    n = (qb + 1) * P
                    col = h * NQB + qb
                    qs = slice(qb * P, (qb + 1) * P)
                    first = True
                    for c0 in range(0, n, BANK):
                        c1 = min(c0 + BANK, n)
                        diag = c1 == n
                        q.pe(lambda e, c0=c0, c1=c1: e.matmul(ps[:, c0:c1], x1[buf][:, h, qs], k1[buf][:, c0:c1],
                                                              start=True, stop=False),
                             (ready_k[g] + ready_x[g, h] + free) if first else ())
                        t = q.pe(lambda e, c0=c0, c1=c1, diag=diag: e.matmul(
                            ps[:, c0:c1], x1[buf][:, h, qs], kl_dup[:, c0:c1], start=False, stop=not diag),
                            (), None if diag else "s1_half")
                        first = False
                    t = q.pe(lambda e: e.matmul(ps[:, n - P:n], ident_b[:, :], mask_b[:, 0, :], start=False, stop=True),
                             [t_mask], "s1_pe")
                    t_m = q.dve(lambda e: e.tensor_reduce(neg_m[buf][:, col:col + 1], ps[:, 0:n], AX, ALU.max, negate=True),
                                [t] + state["lse_free"].get(g - 2, []), "s1_max")
                    t_e = q.act(lambda e: e.activation(ps[:, 0:n], ps[:, 0:n], ACT.Exp,
                                                       bias=neg_m[buf][:, col:col + 1],
                                                       accum_out=row_l[buf][:, col:col + 1]),
                                [t_m], "s1_exp")
                    a_free[i] = [t_e]
                    a_done[g] = [t]
                    state["last_exp"] = t_e
                return run

            for h in range(G):
                for qb in range(NQB):
                    units.append(unit(h, qb))
            return units

        def finish_rows(g):
            buf = g % 2
            t = q.act(lambda e: e.activation(ln_l[:, :], row_l[buf][:, :], ACT.Ln), [state["last_exp"]] + state.get("lse_t", []),
                      "lse_ln")
            t = q.dve(lambda e: e.tensor_tensor(neg_lse[:, :], neg_m[buf][:, :], ln_l[:, :], ALU.subtract),
                      [t] + state.get("lse_pe", []), "lse_dve")
            state["lse_t"] = [t]
            state["lse_free"][g] = [t]
            t = q.pe(lambda e: e.transpose(ps_m[0:G * NQB, 0:P], neg_lse[:, :], ident[:, :]), [t] + state["m_free"], "lse_pe")
            state["lse_pe"] = [t]
            old = state.get(("rows", buf), [])
            t_hi = q.dve(lambda e: e.tensor_copy(lse_hi[buf][:, :], ps_m[0:G * NQB, 0:P]), [t] + old, "lse_dve")
            t_lo = q.dve(lambda e: e.tensor_tensor(lse_lo[buf][:, :], ps_m[0:G * NQB, 0:P], lse_hi[buf][:, :].bitcast(F32),
                                                   ALU.subtract), [t_hi], "lse_dve")
            state["m_free"] = [t_lo]
            for h in range(G):
                lo = 0 if h % 2 else D
                for k, part in enumerate((lse_hi, lse_lo)):
                    t = q.dma(x2[buf][lo + k:lo + k + 1, h, :], part[buf][h * NQB:(h + 1) * NQB, :], f"x2_rows{buf}",
                              [t_lo, consts] + x_free.get(g - 2, []))
            state["rows", buf] = [t]

        def second_pass(g):
            b, kv = g // HKV, g % HKV
            buf = g % 2
            steps = []
            work = []
            for pair in range(NPAIR):
                for c in range(NCH):
                    nk = (c + 1) * BANK // P
                    for kb in range(nk):
                        off = max(kb * P - c * BANK, 0)
                        work.append((pair, c, kb, off, kb * P >= c * BANK, kb == nk - 1))
            pending = []

            def product():
                (pair, c, kb, off, _, last), t_p, n = pending.pop(0)
                w = BANK - off
                for odd in range(2):
                    wait = [t_p[odd]] + ([state["v_done"][b]] + state["o_free"] if kb == 0 else [])
                    t = q.pe(lambda e, odd=odd: e.matmul(
                        ps_o[odd * D:(odd + 1) * D, off:BANK], v[b % 2][:, kb, kv * D:(kv + 1) * D],
                        prob[2 * (n % 2) + odd][:, 0:w], start=kb == 0, stop=last), wait, "pv_pe")
                state["prob", n % 2] = [t]
                pv_done[b] = [t]
                if last:
                    t = q.dve(lambda e: e.tensor_copy(attn_t[:, kv * NPAIR + pair, c * BANK:(c + 1) * BANK], ps_o[:, :]),
                              [t] + state.get("wo_pe", []), "o_copy")
                    state["o_free"] = [t]
                    state["o_last"] = t

            def step(item):
                def run():
                    pair, c, kb, off, diag, last = item
                    w = BANK - off
                    q0 = c * BANK + off
                    n = state.setdefault("steps", 0)
                    state["steps"] += 1
                    tokens = []
                    for odd in range(2):
                        h = 2 * pair + odd
                        ks = slice(kb * P, (kb + 1) * P)
                        wait = state.get(("s_free", odd), []) + state["rows", buf] + [ready_x[g, G - 1, NCH - 1]]
                        q.pe(lambda e, odd=odd, h=h, ks=ks: e.matmul(
                            ps_s[odd][:, 0:w], k1[buf][:, ks], x1[buf][:, h, q0:q0 + w], start=True, stop=False), wait)
                        t = q.pe(lambda e, odd=odd, h=h, ks=ks: e.matmul(
                            ps_s[odd][:, 0:w], k2[buf][odd][:, ks], x2[buf][:, h, q0:q0 + w], start=False, stop=not diag),
                            (), None if diag else "s2_pe")
                        if diag:
                            t = q.pe(lambda e, odd=odd: e.matmul(ps_s[odd][:, 0:P], ident_b[:, :], mask_b[:, 1, :],
                                                                 start=False, stop=True), (), "s2_pe")
                        t = q.act(lambda e, odd=odd: e.activation(prob[2 * (n % 2) + odd][:, 0:w], ps_s[odd][:, 0:w],
                                                                  ACT.Exp), [t] + state.get(("prob", n % 2), []), "s2_exp")
                        state["s_free", odd] = [t]
                        tokens.append(t)
                    x_free[g] = k_free[g] = [t_last for t_last in [("s2_pe", q.counts["s2_pe"].value)]]
                    if pending:
                        product()
                    pending.append((item, tokens, n))
                return run

            steps = [step(item) for item in work]
            steps.append(lambda: product())
            return steps

        def output(b):
            x_in = q.dma(x[:, b * TPB:(b + 1) * TPB, :], a["x"][b].rearrange("(t p) n -> p t n", p=P), f"x_again{b % 2}",
                         [h_done[b]])
            for n in range(TPB // 4):
                for j in range(4):
                    blk = slice((n * 4 + j) * P, (n * 4 + j + 1) * P)
                    for c in range(H // 2):
                        t = q.pe(lambda e, j=j, c=c, blk=blk: e.matmul(
                            ps_m[:, j * HID:(j + 1) * HID], attn_t[:, c, blk], wo[:, c, :],
                            start=c == 0, stop=c == H // 2 - 1),
                            [state["o_last"]] + state["m_free"] if j == 0 and c == 0 else (),
                            "wo_pe" if c == H // 2 - 1 and j == 3 else None)
                tile = b * TPB + n * 4
                t_s = q.dve(lambda e, b=b: e.tensor_tensor(
                    scaled[:, :, :], ps_m[:, :].rearrange("p (j n) -> p j n", j=4),
                    gate_bc[:, b:b + 1, :].to_broadcast([P, 4, HID]), ALU.mult), [t] + state.get("res", []), "wo_scale")
                state["m_free"] = [t_s]
                state["res"] = [q.pool(lambda e, tile=tile: e.tensor_tensor(
                    x[:, tile:tile + 4, :], x[:, tile:tile + 4, :], scaled[:, :, :], ALU.add), [t_s, x_in], "wo_add")]
            state["wo_pe"] = [t]

        h_done = {}
        groups = BATCH * HKV
        for g in range(groups + 1):
            if g < groups:
                if g % HKV == 0:
                    project_v(g // HKV)
                for s in project(g):
                    s()
                h_done[g // HKV] = ("proj_pe", q.counts["proj_pe"].value)
            first = first_pass(g) if g < groups else []
            second = second_pass(g - 1) if g else []
            na, nb = len(first), len(second)
            ia = ib = 0
            while ia < na or ib < nb:
                if ib >= nb or (ia < na and ia * max(nb, 1) <= ib * na):
                    first[ia]()
                    ia += 1
                else:
                    second[ib]()
                    ib += 1
            if g < groups:
                finish_rows(g)
            if g and (g - 1) % HKV == HKV - 1:
                output((g - 1) // HKV)
        q.run()


def route(q, nc, name, ctx, h_t, gate, loaded, iota, tri, capacity):
    NE = 8
    shape = [P, TILES, NE]
    combine = ctx.enter_context(nc.sbuf_tensor(f"combine{name}", shape, F32))
    with ExitStack() as own:
        def sb(n, s=shape):
            return own.enter_context(nc.sbuf_tensor(f"{n}{name}", s, F32))
        ps = own.enter_context(nc.psum_tensor(f"ps_route{name}", shape, F32))
        prob, tmp, cand = sb("r_prob"), sb("r_tmp"), sb("r_cand")
        mask = [sb("r_mask0"), sb("r_mask1")]
        top = [sb("r_top0", [P, TILES]), sb("r_top1", [P, TILES])]
        red = sb("r_red", [P, TILES])
        for i in range(TILES):
            t = q.pe(lambda e, i=i: e.matmul(ps[:, i, :], h_t[:, i * P:(i + 1) * P], gate[:, :], start=True, stop=True),
                     [loaded], "route_pe")
        chain = [t]

        def dve(f):
            chain[0] = q.dve(f, [chain[0]], "route_dve")

        def over(v):
            return v[:, :].rearrange("p (t o) -> p t o", o=1).to_broadcast(shape)

        io = iota[:, :].rearrange("p (o n) -> p o n", o=1).to_broadcast(shape)
        dve(lambda e: e.tensor_reduce(red[:, :], ps[:, :, :], AX, ALU.max))
        dve(lambda e: e.tensor_tensor(tmp[:, :, :], ps[:, :, :], over(red), ALU.subtract))
        chain[0] = q.act(lambda e: e.activation(tmp[:, :, :], tmp[:, :, :], ACT.Exp), [chain[0]], "route_exp")
        dve(lambda e: e.tensor_reduce(red[:, :], tmp[:, :, :], AX, ALU.add))
        dve(lambda e: e.reciprocal(red[:, :], red[:, :]))
        dve(lambda e: e.tensor_tensor(prob[:, :, :], tmp[:, :, :], over(red), ALU.mult))
        dve(lambda e: e.tensor_copy(tmp[:, :, :], prob[:, :, :]))
        for k in range(2):
            m, tp = mask[k], top[k]
            dve(lambda e, tp=tp: e.tensor_reduce(tp[:, :], tmp[:, :, :], AX, ALU.max))
            dve(lambda e, tp=tp: e.tensor_tensor(cand[:, :, :], tmp[:, :, :], over(tp), ALU.is_equal))
            dve(lambda e: e.tensor_scalar(cand[:, :, :], cand[:, :, :], -float(NE), float(NE), ALU.mult, ALU.add))
            dve(lambda e: e.tensor_tensor(cand[:, :, :], cand[:, :, :], io, ALU.add))
            dve(lambda e: e.tensor_reduce(red[:, :], cand[:, :, :], AX, ALU.min))
            dve(lambda e, m=m: e.tensor_tensor(m[:, :, :], io, over(red), ALU.is_equal))
            if k == 0:
                dve(lambda e, m=m: e.scalar_tensor_tensor(tmp[:, :, :], m[:, :, :], -2.0, tmp[:, :, :], ALU.mult, ALU.add))
        if capacity is None:
            dve(lambda e: e.tensor_tensor(red[:, :], top[0][:, :], top[1][:, :], ALU.add))
            dve(lambda e: e.tensor_scalar(red[:, :], red[:, :], 1e-20, None, ALU.add))
            dve(lambda e: e.reciprocal(red[:, :], red[:, :]))
            for k in range(2):
                dve(lambda e, k=k: e.tensor_tensor(top[k][:, :], top[k][:, :], red[:, :], ALU.mult))
        else:
            ones = sb("r_ones", [P, P])
            t_one = q.pool(lambda e: e.memset(ones[:, :], 1.0), (), "route_pool")
            ps_rank = own.enter_context(nc.psum_tensor(f"ps_rank{name}", shape, F32))
            ps_tot = own.enter_context(nc.psum_tensor(f"ps_tot{name}", shape, F32))
            run_a, run_b = sb("r_run_a"), sb("r_run_b")
            for k in range(2):
                t = q.pe(lambda e, k=k: e.matmul(ps_rank[:, :, :], tri[:, :], mask[k][:, :, :], start=True, stop=True),
                         [chain[0], t_one], "rank_pe")
                chain[0] = q.pe(lambda e, k=k: e.matmul(ps_tot[:, :, :], ones[:, :], mask[k][:, :, :], start=True, stop=True),
                                (), "rank_pe")
                dve(lambda e: e.memset(run_a[:, 0:1, :], 0.0))
                dve(lambda e: e.tensor_copy(run_a[:, 1:TILES, :], ps_tot[:, 0:TILES - 1, :]))
                src, dst = run_a, run_b
                s = 1
                while s < TILES:
                    dve(lambda e, s=s, src=src, dst=dst: e.tensor_copy(dst[:, 0:s, :], src[:, 0:s, :]))
                    dve(lambda e, s=s, src=src, dst=dst: e.tensor_tensor(
                        dst[:, s:TILES, :], src[:, s:TILES, :], src[:, 0:TILES - s, :], ALU.add))
                    src, dst = dst, src
                    s *= 2
                dve(lambda e, src=src: e.tensor_tensor(src[:, :, :], src[:, :, :], ps_rank[:, :, :], ALU.add))
                dve(lambda e, src=src, k=k: e.scalar_tensor_tensor(mask[k][:, :, :], src[:, :, :], float(capacity),
                                                                   mask[k][:, :, :], ALU.is_lt, ALU.mult))
        dve(lambda e: e.tensor_tensor(tmp[:, :, :], mask[0][:, :, :], over(top[0]), ALU.mult))
        dve(lambda e: e.tensor_tensor(cand[:, :, :], mask[1][:, :, :], over(top[1]), ALU.mult))
        dve(lambda e: e.tensor_tensor(combine[:, :, :], tmp[:, :, :], cand[:, :, :], ALU.add))
        q.run()
    return combine


def experts(q, nc, name, x, h_t, combine, gate_bc, up, down, fp, gated, bias_bc):
    NE = 8
    NCHUNK = TOK // BANK
    NF = 2 if gated else 4
    with ExitStack() as ctx:
        def sb(n, s):
            return ctx.enter_context(nc.sbuf_tensor(f"{n}{name}", s, F32))
        hid = [sb(f"hid{i}", [fp, NF, BANK]) for i in range(2)]
        silu = [sb(f"silu{i}", [fp, BANK]) for i in range(2)]
        acc = [sb(f"acc{i}", [P, 4, HID]) for i in range(2)]
        part = [sb(f"part{i}", [P, 4, HID]) for i in range(2)]
        ps_up = [ctx.enter_context(nc.psum_tensor(f"ps_up{name}{i}", [P, 2, BANK], F32)) for i in range(3)]
        ps_dn = [ctx.enter_context(nc.psum_tensor(f"ps_dn{name}{i}", [P, 4, HID], F32)) for i in range(2)]
        up_free, dn_free = [[], [], []], [[], []]
        hid_free, part_free, silu_free = [[], []], [[], []], [[], []]
        acc_done = {}
        units = [(n, e) for n in range(NCHUNK) for e in range(NE)]
        made = {}

        def up_stage(k):
            n, e = units[k]
            cols = slice(n * BANK, (n + 1) * BANK)
            for j in range(2):
                r = (2 * k + j) % 3
                ps = ps_up[r]
                for m in range(2):
                    t = q.pe(lambda en, ps=ps, m=m, j=j, e=e: en.matmul(ps[0:fp, m, :], up(e, 2 * j + m), h_t[:, cols],
                                                                        start=True, stop=True),
                             up_free[r] if m == 0 else (), "up_pe")
                dst = hid[k % 2]
                if gated:
                    t_s = q.act(lambda en, ps=ps, j=j: en.activation(silu[j][:, :], ps[0:fp, 0, :], ACT.Silu),
                                [t] + silu_free[j], "up_act")
                    t = q.dve(lambda en, ps=ps, j=j, dst=dst: en.tensor_tensor(dst[:, j, :], ps[0:fp, 1, :], silu[j][:, :],
                                                                               ALU.mult), [t_s] + hid_free[k % 2], "up_dve")
                    silu_free[j] = [t]
                else:
                    t = q.act(lambda en, ps=ps, j=j, dst=dst: en.activation(dst[:, 2 * j:2 * j + 2, :], ps[0:fp, :, :],
                                                                            ACT.Gelu_apprx_tanh),
                              [t] + hid_free[k % 2], "up_act")
                up_free[r] = [t]
            made[k] = t

        def down_stage(k):
            n, e = units[k]
            ps = ps_dn[k % 2]
            for i in range(4):
                for f in range(NF):
                    t = q.pe(lambda en, i=i, f=f: en.matmul(ps[:, i, :], hid[k % 2][:, f, i * P:(i + 1) * P], down(e, f),
                                                            start=f == 0, stop=f == NF - 1),
                             [made[k]] + dn_free[k % 2] if i == 0 and f == 0 else (), "dn_pe" if i == 3 and f == NF - 1 else None)
            hid_free[k % 2] = [t]
            w = combine[:, 4 * n:4 * n + 4, e:e + 1].to_broadcast([P, 4, HID])
            a = acc[n % 2]
            if e == 0:
                t = q.dve(lambda en: en.tensor_tensor(a[:, :, :], ps[:, :, :], w, ALU.mult),
                          [t] + acc_done.get(n - 2, []), "dn_dve")
                dn_free[k % 2] = [t]
                acc_done[n] = [t]
                return
            pt = part[k % 2]
            t = q.dve(lambda en: en.tensor_tensor(pt[:, :, :], ps[:, :, :], w, ALU.mult), [t] + part_free[k % 2], "dn_dve")
            dn_free[k % 2] = [t]
            t = q.pool(lambda en: en.tensor_tensor(a[:, :, :], a[:, :, :], pt[:, :, :], ALU.add),
                       [t] + acc_done[n], "dn_add")
            part_free[k % 2] = [t]
            acc_done[n] = [t]
            if e == NE - 1:
                b = n * 4 // TPB
                if bias_bc is not None:
                    t = q.pool(lambda en: en.tensor_tensor(a[:, :, :], a[:, :, :],
                                                           bias_bc[:, :, :].to_broadcast([P, 4, HID]), ALU.add),
                               [t], "dn_add")
                t = q.pool(lambda en: en.tensor_tensor(a[:, :, :], a[:, :, :], gate_bc[:, b:b + 1, :].to_broadcast([P, 4, HID]),
                                                       ALU.mult), [t], "dn_add")
                t = q.pool(lambda en: en.tensor_tensor(x[:, 4 * n:4 * n + 4, :], x[:, 4 * n:4 * n + 4, :], a[:, :, :], ALU.add),
                           [t], "dn_add")
                acc_done[n] = [t]

        for k in range(len(units)):
            up_stage(k)
            if k:
                down_stage(k - 1)
        down_stage(len(units) - 1)
        q.run()


def selective_scan(q, nc, a, x, h_t, gate_bc):
    FG = P // NST
    NG = HID // FG
    with ExitStack() as ctx:
        def sb(n, s=(P, SEQ)):
            return ctx.enter_context(nc.sbuf_tensor(f"m_{n}", list(s), F32))

        def pb(n, s):
            return ctx.enter_context(nc.psum_tensor(f"m_{n}", s, F32))
        w_in, w_x, w_out = sb("w_in", (P, 2 * HID)), sb("w_x", (P, 2 * NST + 1)), sb("w_out", (P, HID))
        w_b, w_c, w_d = sb("w_b", (P, FG, NST)), sb("w_c", (P, FG, NST)), sb("w_d", (P, P))
        cw, cb, dp = sb("cw", (P, TAPS)), sb("cb", (P, 1)), sb("dp", (P, 1))
        a_neg, log_a = sb("a_neg", (P, NG)), sb("log_a", (P, NG))
        sel = sb("sel", (P, NG * P))
        fold = sb("fold", (P, 2 * P - FG))
        xm = [sb(f"xm{i}", (P, SEQ + TAPS - 1)) for i in range(2)]
        z = [sb(f"z{i}") for i in range(2)]
        u, conv = [sb(f"u{i}") for i in range(2)], sb("conv")
        raw, soft, delta, du = sb("raw"), sb("soft"), [sb(f"delta{i}") for i in range(2)], [sb(f"du{i}") for i in range(2)]
        brep, crep = [sb(f"brep{i}") for i in range(2)], [sb(f"crep{i}") for i in range(2)]
        da, bu, st, hc = ([sb(f"{n}{i}") for i in range(2)] for n in ("da", "bu", "st", "hc"))
        y = sb("y")
        scaled = sb("scaled", (P, 4, HID))
        ps_y = [pb(f"ps_y{i}", [P, BANK]) for i in range(2)]
        ps_x = [pb(f"ps_x{i}", [P, 2 * BANK]) for i in range(2)]
        ps_w = [pb(f"ps_w{i}", [P, BANK]) for i in range(2)]

        for out, in_ in [(w_in[:, :], a["w_in"]), (w_x[:, :], a["w_xproj"]), (w_out[:, :], a["w_out"]),
                         (cw[:, :], a["conv_w"]), (cb[:, :], a["conv_b"]), (dp[:, :], a["d_param"]),
                         (log_a[:, :], a["log_a"]), (sel[:, :], a["sel"]), (fold[:, :], a["fold"])]:
            loaded = q.dma(out, in_, "mamba_in")
        q.dve(lambda e: e.tensor_copy(w_b[:, :, :], w_x[:, 0:NST].rearrange("p (o n) -> p o n", o=1).to_broadcast([P, FG, NST])),
              [loaded], "m_const")
        q.dve(lambda e: e.tensor_copy(w_c[:, :, :], w_x[:, NST:2 * NST].rearrange("p (o n) -> p o n", o=1).to_broadcast([P, FG, NST])),
              (), "m_const")
        reps = q.dve(lambda e: e.tensor_copy(w_d[:, :], w_x[:, 2 * NST:2 * NST + 1].to_broadcast([P, P])), (), "m_const")
        t = q.act(lambda e: e.activation(a_neg[:, :], log_a[:, :], ACT.Exp), [loaded], "m_a")
        t_a = q.dve(lambda e: e.tensor_scalar(a_neg[:, :], a_neg[:, :], -1.0, None, ALU.mult), [t], "m_const")
        for i in range(2):
            t_pad = q.pool(lambda e, i=i: e.memset(xm[i][:, 0:TAPS - 1], 0.0), (), "m_pad")

        w_free = [[], []]
        nw = [0]

        def product(lhs, cols, wait):
            i = nw[0] % 2
            nw[0] += 1
            return i, q.pe(lambda e, i=i: e.matmul(ps_w[i][:, :], lhs, cols, start=True, stop=True),
                           wait + w_free[i], "mw_pe")

        old = {}

        def prepare(b):
            k = b % 2
            for c in range(SEQ // BANK):
                cols = h_t[:, b * SEQ + c * BANK:b * SEQ + (c + 1) * BANK]
                i, t = product(w_in[:, 0:HID], cols, [loaded])
                t_x = q.act(lambda e, i=i, c=c: e.activation(xm[k][:, TAPS - 1 + c * BANK:TAPS - 1 + (c + 1) * BANK], ps_w[i][:, :],
                                                             ACT.Copy), [t, t_pad] + old.get(("conv", b - 2), []), "m_act")
                w_free[i] = [t_x]
                i, t = product(w_in[:, HID:2 * HID], cols, [])
                t = q.act(lambda e, i=i, c=c: e.activation(z[k][:, c * BANK:(c + 1) * BANK], ps_w[i][:, :], ACT.Silu),
                          [t] + old.get(("y", b - 2), []), "m_act")
                w_free[i] = [t]
            t = q.dve(lambda e: e.tensor_scalar(conv[:, :], xm[k][:, 0:SEQ], cw[:, 0:1], cb[:, 0:1], ALU.mult, ALU.add),
                      [t_x] + old.get(("u", b - 1), []), "m_conv")
            for j in range(1, TAPS):
                t = q.dve(lambda e, j=j: e.scalar_tensor_tensor(conv[:, :], xm[k][:, j:j + SEQ], cw[:, j:j + 1], conv[:, :],
                                                                ALU.mult, ALU.add), [t], "m_conv")
            old["conv", b] = [t]
            t_u = q.act(lambda e: e.activation(u[k][:, :], conv[:, :], ACT.Silu), [t] + old.get(("y", b - 2), []), "m_act")
            old["u", b] = [t_u]
            for dst, w, what in ((brep, w_b, "b"), (crep, w_c, "c")):
                for c in range(SEQ // BANK):
                    i, t = product(w[:, :, :], u[k][:, c * BANK:(c + 1) * BANK], [t_u, reps])
                    t = q.act(lambda e, i=i, c=c, dst=dst: e.activation(dst[k][:, c * BANK:(c + 1) * BANK], ps_w[i][:, :], ACT.Copy),
                              [t] + old.get(("scan", b - 2), []), "m_act")
                    w_free[i] = [t]
            old["bc", b] = [t]
            for c in range(SEQ // BANK):
                i, t = product(w_d[:, :], u[k][:, c * BANK:(c + 1) * BANK], [])
                t = q.act(lambda e, i=i, c=c: e.activation(raw[:, c * BANK:(c + 1) * BANK], ps_w[i][:, :], ACT.Copy),
                          [t] + old.get(("du", b - 1), []), "m_act")
                w_free[i] = [t]
            t = q.act(lambda e: e.activation(soft[:, :], raw[:, :], ACT.Abs), [t], "m_act")
            t = q.act(lambda e: e.activation(soft[:, :], soft[:, :], ACT.Exp, scale=-1.0), [t], "m_act")
            t = q.act(lambda e: e.activation(soft[:, :], soft[:, :], ACT.Ln, bias=1.0), [t], "m_act")
            t_d = q.dve(lambda e: e.scalar_tensor_tensor(delta[k][:, :], raw[:, :], 0.0, soft[:, :], ALU.max, ALU.add),
                        [t] + old.get(("scan", b - 2), []), "m_delta")
            t = q.dve(lambda e: e.tensor_tensor(du[k][:, :], delta[k][:, :], u[k][:, :], ALU.mult), [t_d, t_u], "m_delta")
            old["du", b] = [t]

        def groups(b):
            k = b % 2
            pend = []

            def gather(g, t_hc):
                for c in range(SEQ // BANK):
                    w0 = P - FG - FG * g
                    t = q.pe(lambda e, c=c, w0=w0, g=g: e.matmul(ps_y[c][:, :], fold[:, w0:w0 + P],
                                                                 hc[g % 2][:, c * BANK:(c + 1) * BANK],
                                                                 start=g == 0, stop=g == NG - 1),
                             [t_hc] + (old.get(("ysum", b - 1), []) if g == 0 else []), "my_pe")
                old["hc", g % 2] = [t]
                return t

            for g in range(NG):
                i = g % 2
                for c in range(SEQ // BANK):
                    t = q.pe(lambda e, c=c, i=i, g=g: e.matmul(ps_x[i][:, c * BANK:(c + 1) * BANK], sel[:, g * P:(g + 1) * P],
                                                               du[k][:, c * BANK:(c + 1) * BANK], start=True, stop=True),
                             old["du", b] + old.get(("px", i), []), "mx_pe")
                t_da = q.act(lambda e, i=i, g=g: e.activation(da[i][:, :], delta[k][:, :], ACT.Exp, scale=a_neg[:, g:g + 1]),
                             [t_a] + old["du", b] + old.get(("st", i), []), "m_da")
                t_bu = q.dve(lambda e, i=i: e.tensor_tensor(bu[i][:, :], ps_x[i][:, :], brep[k][:, :], ALU.mult),
                             [t] + old["bc", b], "m_bu")
                old["px", i] = [t_bu]
                t = q.dve(lambda e, i=i: e.tensor_tensor_scan(st[i][:, :], da[i][:, :], bu[i][:, :], 0.0, ALU.mult, ALU.add),
                          [t_bu, t_da] + old.get(("hp", i), []), "m_scan")
                old["st", i] = [t]
                t = q.pool(lambda e, i=i: e.tensor_tensor(hc[i][:, :], st[i][:, :], crep[k][:, :], ALU.mult),
                           [t] + old.get(("hc", i), []) + old["bc", b], "m_hc")
                old["hp", i] = [t]
                if pend:
                    gather(*pend.pop())
                pend.append((g, t))
            t = gather(*pend.pop())
            old["scan", b] = [t]
            for c in range(SEQ // BANK):
                cc = slice(c * BANK, (c + 1) * BANK)
                t1 = q.dve(lambda e, c=c, cc=cc: e.scalar_tensor_tensor(y[:, cc], u[k][:, cc], dp[:, 0:1], ps_y[c][:, :],
                                                                        ALU.mult, ALU.add), [t] + old.get("out", []), "m_y")
            old["ysum", b] = [t1]
            t = q.dve(lambda e: e.tensor_tensor(y[:, :], y[:, :], z[k][:, :], ALU.mult), [t1], "m_y")
            old["y", b] = [t]
            for n in range(TPB // 4):
                i = nw[0] % 2
                nw[0] += 1
                for j in range(4):
                    blk = slice((n * 4 + j) * P, (n * 4 + j + 1) * P)
                    t_o = q.pe(lambda e, i=i, j=j, blk=blk: e.matmul(ps_w[i][:, j * HID:(j + 1) * HID], y[:, blk], w_out[:, :],
                                                                     start=True, stop=True), [t] + w_free[i], "mo_pe")
                old["out"] = [t_o]
                t_s = q.dve(lambda e, i=i: e.tensor_tensor(
                    scaled[:, :, :], ps_w[i][:, :].rearrange("p (j n) -> p j n", j=4),
                    gate_bc[:, b:b + 1, :].to_broadcast([P, 4, HID]), ALU.mult), [t_o] + old.get("res", []), "mo_dve")
                w_free[i] = [t_s]
                tile = b * TPB + n * 4
                old["res"] = [q.pool(lambda e, tile=tile: e.tensor_tensor(
                    x[:, tile:tile + 4, :], x[:, tile:tile + 4, :], scaled[:, :, :], ALU.add), [t_s], "mo_add")]

        prepare(0)
        for b in range(BATCH):
            if b + 1 < BATCH:
                prepare(b + 1)
            groups(b)
        q.run()


def program(nc, a, out):
    with ExitStack() as ctx:
        q = Queues(nc, ctx)

        def sb(name, shape, dt=F32):
            return ctx.enter_context(nc.sbuf_tensor(name, shape, dt))
        ident, ident_b = sb("ident", [P, P]), sb("ident_b", [P, P], BF16)
        eps = sb("eps", [P, 1])
        first_h = sb("first_h", [P, TOK])
        mod_t = [sb(f"mod_t{i}", [P, 6, BATCH]) for i in range(2)]
        gates = [[sb(f"gate0{w}", [P, BATCH, HID]) for w in range(2)]]

        q.dma(ident[:, :], a["ident"], "in0")
        with nc.sbuf_tensor("x_in", [P, TILES, HID], F32) as x_in:
          t = q.dma(x_in[:, :, :], a["x"].rearrange("b (t p) n -> p (b t) n", p=P), "in0")
          q.dve(lambda e: e.tensor_copy(ident_b[:, :], ident[:, :]), [t], "c0")
          q.dve(lambda e: e.memset(eps[:, :], EPS), (), "c0")
          modulation(q, nc, 0, a["c_t0"], a["wmod0"], mod_t[0], gates[0])
          layernorm_t(q, nc, "0", x_in, mod_t[0], 0, 1, first_h, ident, eps)
        attention(q, nc, a, first_h, gates[0][0], ident, ident_b)
        x = first_h[:, :].rearrange("p (t n) -> p t n", n=HID)
        h_t = sb("h_t", [P, TOK])
        gates.append([sb(f"gate1{w}", [P, BATCH, HID]) for w in range(2)])
        modulation(q, nc, 1, a["c_t1"], a["wmod1"], mod_t[1], gates[1])
        layernorm_t(q, nc, "1", x, mod_t[0], 3, 4, h_t, ident, eps)
        with ExitStack() as own:
            w1 = own.enter_context(nc.sbuf_tensor("w1_0", [P, E0, 4, F0 // 2], F32))
            w2 = own.enter_context(nc.sbuf_tensor("w2_0", [F0 // 2, E0, 2, HID], F32))
            gate = own.enter_context(nc.sbuf_tensor("gate_0", [P, E0], F32))
            iota = own.enter_context(nc.sbuf_tensor("iota_0", [P, E0], F32))
            q.dma(gate[:, :], a["gate_w"], "in1")
            t = q.dma(iota[:, :], a["iota"], "in1")
            src = a["w1_0"].rearrange("e h (s c f) -> h e c s f", s=2, c=2)
            for e_ in range(E0):
                for c in range(2):
                    t = q.dma(w1[:, e_, 2 * c:2 * c + 2, :], src[:, e_, c, :, :], "in1")
            t = q.dma(w2[:, :, :, :], a["w2_0"].rearrange("e (c f) n -> f e c n", c=2), "in1")
            combine = route(q, nc, "0", own, h_t, gate, t, iota, None, None)
            experts(q, nc, "0", x, h_t, combine, gates[0][1], lambda e, j: w1[:, e, j, :], lambda e, f: w2[:, e, f, :],
                    F0 // 2, True, None)

        layernorm_t(q, nc, "2", x, mod_t[1], 0, 1, h_t, ident, eps)
        selective_scan(q, nc, a, x, h_t, gates[1][0])
        layernorm_t(q, nc, "3", x, mod_t[1], 3, 4, h_t, ident, eps)
        with ExitStack() as own:
            w1 = own.enter_context(nc.sbuf_tensor("w1_1", [P, E1, F1], F32))
            w2 = own.enter_context(nc.sbuf_tensor("w2_1", [P, E1, F1 // P, HID], F32))
            gate = own.enter_context(nc.sbuf_tensor("gate_1", [P, E1], F32))
            iota = own.enter_context(nc.sbuf_tensor("iota_1", [P, E1], F32))
            tri = own.enter_context(nc.sbuf_tensor("tri", [P, P], F32))
            bias = own.enter_context(nc.sbuf_tensor("bias", [P, 1, HID], F32))
            q.dma(gate[:, :], a["router_w"], "in2")
            q.dma(iota[:, :], a["iota"], "in2")
            q.dma(tri[:, :], a["tri"], "in2")
            q.dma(bias[:, :, :], a["bias"].to_broadcast([P, 1, HID]), "in2")
            q.dma(w1[:, :, :], a["w1_1"].rearrange("e h f -> h e f"), "in2")
            t = q.dma(w2[:, :, :, :], a["w2_1"].rearrange("e (c f) n -> f e c n", f=P), "in2")
            combine = route(q, nc, "1", own, h_t, gate, t, iota, tri, CAPACITY)
            experts(q, nc, "1", x, h_t, combine, gates[1][1], lambda e, j: w1[:, e, j * P:(j + 1) * P],
                    lambda e, f: w2[:, e, f, :], P, False, bias)

        t = q.dma(out.rearrange("b (t p) n -> p (b t) n", p=P), x[:, :, :], "out")
        q.put("sync", lambda e: e.nop(), [t])
        q.run()


def constants():
    inv = (1.0 / THETA ** (np.arange(0, D, 2, dtype=np.float32) / np.float32(D))).astype(np.float32)
    freqs = np.arange(SEQ, dtype=np.float32)[:, None] * inv[None, :]
    emb = np.concatenate([freqs, freqs], axis=-1)[:, 0::2].astype(np.float32)
    cos, sin = np.cos(emb).T, np.sin(emb).T
    cos = np.repeat(cos, 2, axis=0)
    sin = np.repeat(sin, 2, axis=0) * np.tile(np.array([-1.0, 1.0], np.float32), D // 2)[:, None]
    i = np.arange(P)
    later = (i[None, :] > i[:, None]).astype(np.float32)
    fg = P // NST
    j = np.arange(HID // fg * P)
    w = np.arange(2 * P - fg)
    return {
        "cos": np.tile(cos, (2, 1)).astype(np.float32),
        "sin": np.tile(sin, (2, 1)).astype(np.float32),
        "masks": np.stack([later * np.float32(NEG), later.T * np.float32(NEG)], axis=1).astype(np.float32),
        "ident": np.eye(P, dtype=np.float32),
        "tri": later,
        "iota": np.tile(np.arange(E0, dtype=np.float32), (P, 1)),
        "sel": (i[:, None] == j[None, :] // NST).astype(np.float32),
        "fold": (w[None, :] == P - fg + i[:, None] // NST).astype(np.float32),
    }


def kernel(**inputs):
    import concourse.bacc as bacc
    from concourse.bass_utils import run_bass_kernel_spmd

    arr = {k: np.asarray(v) for k, v in inputs.items()}

    def swapped(w):
        return w.reshape(w.shape[0], -1, 2)[:, :, ::-1].reshape(w.shape)

    fields = {
        "x": arr["L0_attn_hidden_states"],
        "wq": arr["L0_attn_Wq"], "wqs": swapped(arr["L0_attn_Wq"]),
        "wk": arr["L0_attn_Wk"], "wks": swapped(arr["L0_attn_Wk"]),
        "wv": arr["L0_attn_Wv"], "wo": arr["L0_attn_Wo"],
        "gate_w": arr["L0_ffn_gate_w"].T, "w1_0": arr["L0_ffn_w1"], "w2_0": arr["L0_ffn_w2"],
        "c_t0": arr["L0_c"].T, "wmod0": arr["L0_wmod"],
        "w_in": arr["L1_attn_W_in"], "conv_w": arr["L1_attn_conv_w"].reshape(HID, TAPS),
        "conv_b": arr["L1_attn_conv_b"].reshape(HID, 1), "w_xproj": arr["L1_attn_W_xproj"],
        "log_a": arr["L1_attn_log_A"].reshape(HID * NST // P, P).T,
        "d_param": arr["L1_attn_D_param"].reshape(HID, 1), "w_out": arr["L1_attn_W_out"],
        "router_w": arr["L1_ffn_router_w"], "w1_1": arr["L1_ffn_w1"], "w2_1": arr["L1_ffn_w2"],
        "bias": arr["L1_ffn_bias"].reshape(1, 1, HID),
        "c_t1": arr["L1_c"].T, "wmod1": arr["L1_wmod"],
        **constants(),
    }
    nc = bacc.Bacc("TRN2", target_bir_lowering=False, num_devices=1)
    arrays, aps = {}, {}
    for name, value in fields.items():
        value = np.ascontiguousarray(value)
        arrays[f"in_{name}"] = value
        aps[name] = nc.dram_tensor(f"in_{name}", value.shape, mybir.dt.from_np(value.dtype), kind="ExternalInput").ap()
    out = nc.dram_tensor("out_x", (BATCH, SEQ, HID), F32, kind="ExternalOutput").ap()
    program(nc, aps, out)
    result = run_bass_kernel_spmd(nc, [arrays], core_ids=[0])
    return result.results[0]["out_x"]
```

```python
from contextlib import ExitStack

import numpy as np

import concourse.bass as bass
from concourse import mybir

F32 = mybir.dt.float32
F32R = mybir.dt.float32r
I32 = mybir.dt.int32
BF16 = mybir.dt.bfloat16
ALU = mybir.AluOpType
ACT = mybir.ActivationFunctionType
AX = mybir.AxisListType.X

P = 128
BATCH, SEQ, HID = 4, 1024, 128
TOK = BATCH * SEQ
TILES = TOK // P
TPB = SEQ // P
BANK = 512
H, HKV, D = 16, 4, 64
E0, F0 = 8, 176
E1, F1 = 8, 512
NST = 16
TAPS = 4
CAPACITY = TOK // E1
THETA = 10000.0
EPS = 1e-5
NEG = -1e30


class Count:

    def __init__(self, sem):
        self.sem, self.value = sem, 0


class Queues:

    ENGINES = ("tensor", "vector", "scalar", "gpsimd", "sync")

    def __init__(self, nc, ctx):
        self.nc, self.ctx = nc, ctx
        self.todo = {e: [] for e in self.ENGINES}
        self.counts = {}
        self.met = {}

    def count(self, name):
        if name not in self.counts:
            self.counts[name] = Count(self.ctx.enter_context(self.nc.semaphore(name)))
        return self.counts[name]

    def put(self, engine, issue, wait=(), signal=None, step=1):
        todo = self.todo[engine]
        for name, value in wait:
            if self.met.get((engine, name), 0) < value:
                self.met[engine, name] = value
                todo.append((None, self.counts[name].sem, value))
        if signal is None:
            todo.append((issue, None, 0))
            return None
        count = self.count(signal)
        count.value += step
        todo.append((issue, count.sem, step))
        return signal, count.value

    def pe(self, issue, wait=(), signal=None):
        return self.put("tensor", issue, wait, signal)

    def dve(self, issue, wait=(), signal=None):
        return self.put("vector", issue, wait, signal)

    def act(self, issue, wait=(), signal=None):
        return self.put("scalar", issue, wait, signal)

    def pool(self, issue, wait=(), signal=None):
        return self.put("gpsimd", issue, wait, signal)

    def dma(self, out, in_, signal, wait=(), engine="sync"):
        if in_.dtype == F32R:
            out, in_ = out.bitcast(F32), in_.bitcast(F32)
        return self.put(engine, lambda e: e.dma_start(out, in_), wait, signal, 16)

    def run(self):
        todo, self.todo = self.todo, {e: [] for e in self.ENGINES}

        def emit(e, items):
            for issue, sem, n in items:
                if issue is None:
                    e.wait_ge(sem, n)
                elif sem is None:
                    issue(e)
                else:
                    issue(e).then_inc(sem, n)

        with self.nc.Block() as block:
            for name in self.ENGINES:
                if todo[name]:
                    def body(e, items=todo[name]):
                        emit(e, items)
                    {"tensor": block.tensor, "vector": block.vector, "scalar": block.scalar,
                     "gpsimd": block.gpsimd, "sync": block.sync}[name](body)


def modulation(q, nc, layer, c_t, wmod, mod_t, gate_bc, rows_bc=None):
    with ExitStack() as ctx:
        ct = ctx.enter_context(nc.sbuf_tensor(f"ct{layer}", [P, BATCH], F32))
        sct = ctx.enter_context(nc.sbuf_tensor(f"sct{layer}", [P, BATCH], F32))
        wm = ctx.enter_context(nc.sbuf_tensor(f"wm{layer}", [P, 6 * HID], F32))
        sign = ctx.enter_context(nc.sbuf_tensor(f"sign{layer}", [P, BATCH, HID], F32))
        size = ctx.enter_context(nc.sbuf_tensor(f"size{layer}", [P, BATCH, HID], F32))
        ps_col = ctx.enter_context(nc.psum_tensor(f"ps_col{layer}", [P, 6, BATCH], F32))
        ps_row = [ctx.enter_context(nc.psum_tensor(f"ps_row{layer}{w}", [P, BATCH, HID], F32)) for w in range(2)]
        in_c = q.dma(ct[:, :], c_t, "mod_in")
        in_w = q.dma(wm[:, :], wmod, "mod_in")
        got_c = q.act(lambda e: e.activation(sct[:, :], ct[:, :], ACT.Silu), [in_w], "mod_silu")
        for j in range(6):
            cols = q.pe(lambda e, j=j: e.matmul(ps_col[:, j, :], wm[:, j * HID:(j + 1) * HID], sct[:, :],
                                                start=True, stop=True), [got_c, in_w], "mod_pe")
        t = q.dve(lambda e: e.tensor_copy(mod_t[:, :, :], ps_col[:, :, :]), [cols], "mod_dve")
        for j in (1, 4):
            q.dve(lambda e, j=j: e.tensor_scalar(mod_t[:, j, :], ps_col[:, j, :], 1.0, None, ALU.add), [t], "mod_dve")
        for w, j in enumerate((2, 5)):
            for b in range(BATCH):
                rows = q.pe(lambda e, w=w, j=j, b=b: e.matmul(
                    ps_row[w][:, b, :], sct[:, b:b + 1].to_broadcast([P, P]), wm[:, j * HID:(j + 1) * HID],
                    start=True, stop=True), (), "mod_pe")
            t = q.dve(lambda e, w=w: e.tensor_scalar(sign[:, :, :], ps_row[w][:, :, :], 0.0, 2.0, ALU.is_ge, ALU.mult),
                      [rows, t], "mod_dve")
            t = q.dve(lambda e: e.tensor_scalar(sign[:, :, :], sign[:, :, :], -1.0, None, ALU.add), [t], "mod_dve")
            t = q.dve(lambda e, w=w: e.tensor_tensor(size[:, :, :], ps_row[w][:, :, :], sign[:, :, :], ALU.mult),
                      [t], "mod_dve")
            t = q.dve(lambda e, w=w: e.scalar_tensor_tensor(gate_bc[w][:, :, :], size[:, :, :], 0.25, sign[:, :, :],
                                                            ALU.max, ALU.mult), [t], "mod_dve")
        if rows_bc is not None:
            for w, j in enumerate((3, 4)):
                for b in range(BATCH):
                    rows = q.pe(lambda e, w=w, j=j, b=b: e.matmul(
                        ps_row[w][:, b, :], sct[:, b:b + 1].to_broadcast([P, P]), wm[:, j * HID:(j + 1) * HID],
                        start=True, stop=True), [t], "mod_pe")
                q.dve(lambda e, w=w: e.tensor_scalar(rows_bc[w][:, :, :], ps_row[w][:, :, :], float(w), None, ALU.add),
                      [rows], "mod_dve")
        q.run()


def layernorm_t(q, nc, name, x, mod_t, shift, scale, h_t, ident, eps, rows_bc=None, h=None):
    with ExitStack() as ctx:
        stats = ctx.enter_context(nc.sbuf_tensor(f"stats{name}", [P, TILES, 6], F32))
        mv = ctx.enter_context(nc.sbuf_tensor(f"mv{name}", [P, TILES, 2], F32))
        std = ctx.enter_context(nc.sbuf_tensor(f"std{name}", [P, TILES], F32))
        rstd = ctx.enter_context(nc.sbuf_tensor(f"rstd{name}", [P, TILES], F32))
        nmr = ctx.enter_context(nc.sbuf_tensor(f"nmr{name}", [P, TILES], F32))
        xn = h if h is not None else ctx.enter_context(nc.sbuf_tensor(f"xn{name}", [P, TILES, HID], F32))
        ps = [ctx.enter_context(nc.psum_tensor(f"ps_ln{name}{i}", [P, BANK], F32)) for i in range(4)]
        for i in range(TILES):
            t = q.dve(lambda e, i=i: e.bn_stats(stats[:, i, :], x[:, i, :]), (), "ln_stats")
        for i in range(TILES):
            t = q.dve(lambda e, i=i: e.bn_aggr(mv[:, i, :], stats[:, i, :]), [t], "ln_stats")
        t_std = q.act(lambda e: e.activation(std[:, :], mv[:, :, 1], ACT.Sqrt, bias=eps[:, 0:1]), [t], "ln_std")
        t = q.dve(lambda e: e.reciprocal(rstd[:, :], std[:, :]), [t_std], "ln_stats")
        t = q.dve(lambda e: e.scalar_tensor_tensor(nmr[:, :], mv[:, :, 0], -1.0, rstd[:, :], ALU.mult, ALU.mult),
                  [t], "ln_stats")
        free = [None] * 4
        for i in range(TILES):
            put = q.dve if i % 2 else q.pool
            t_n = put(lambda e, i=i: e.tensor_scalar(xn[:, i, :], x[:, i, :], rstd[:, i:i + 1], nmr[:, i:i + 1],
                                                     ALU.mult, ALU.add), [t], "ln_norm_dve" if i % 2 else "ln_norm_pool")
            n = i // 4
            if rows_bc is not None:
                for op, r in ((ALU.mult, 1), (ALU.add, 0)):
                    t_n = put(lambda e, i=i, op=op, r=r: e.tensor_tensor(xn[:, i, :], xn[:, i, :], rows_bc[r][:, i // TPB, :], op),
                              [t_n], "ln_norm_dve" if i % 2 else "ln_norm_pool")
            w = [t_n] + ([free[n % 4]] if i % 4 == 0 and free[n % 4] else [])
            t_t = q.pe(lambda e, i=i, n=n: e.transpose(ps[n % 4][:, (i % 4) * P:(i % 4 + 1) * P], xn[:, i, :],
                                                       ident[:, :]), w, "ln_tr")
            if i % 4 == 3:
                b = i // TPB
                cols = slice(n * BANK, (n + 1) * BANK)
                if rows_bc is not None:
                    free[n % 4] = q.act(lambda e, n=n, cols=cols: e.activation(h_t[:, cols], ps[n % 4][:, :], ACT.Copy),
                                        [t_t], "ln_out_act")
                elif n % 2:
                    free[n % 4] = q.dve(lambda e, n=n, b=b, cols=cols: e.tensor_scalar(
                        h_t[:, cols], ps[n % 4][:, :], mod_t[:, scale, b:b + 1], mod_t[:, shift, b:b + 1],
                        ALU.mult, ALU.add), [t_t], "ln_out_dve")
                else:
                    free[n % 4] = q.act(lambda e, n=n, b=b, cols=cols: e.activation(
                        h_t[:, cols], ps[n % 4][:, :], ACT.Identity, bias=mod_t[:, shift, b:b + 1],
                        scale=mod_t[:, scale, b:b + 1]), [t_t], "ln_out_act")
        q.run()


def attention(q, nc, a, h_t, gate_bc, ident, ident_b):
    G = H // HKV
    NPAIR = G // 2
    NQB = SEQ // P
    NCH = SEQ // BANK
    x = h_t[:, :].rearrange("p (t n) -> p t n", n=HID)
    with ExitStack() as ctx:
        def sb(name, shape, dt=F32):
            return ctx.enter_context(nc.sbuf_tensor(name, shape, dt))

        def pb(name, shape):
            return ctx.enter_context(nc.psum_tensor(name, shape, F32))

        wq = sb("wq", [P, H * D])
        wk = sb("wk", [P, HKV, 2, D])
        wv = sb("wv", [P, HKV * D])
        wo = sb("wo", [P, H // 2, HID])
        cos, sin = sb("cos", [P, SEQ]), sb("sin", [P, SEQ])
        mask_b = sb("mask_b", [P, 2, P], BF16)
        x1 = [sb(f"x1_{i}", [P, G, SEQ], F32R) for i in range(2)]
        x2 = [sb(f"x2_{i}", [P, G, SEQ], F32R) for i in range(2)]
        k1 = [sb(f"k1_{i}", [P, SEQ], F32R) for i in range(3)]
        kl_dup = sb("kl_dup", [P, SEQ], F32R)
        k2 = [[sb(f"k2_{i}{j}", [P, SEQ], F32R) for j in range(2)] for i in range(3)]
        v = [sb(f"v_{i}", [P, NQB, D]) for i in range(2)]
        rot = [sb(f"rot{i}", [P, BANK]) for i in range(2)]
        other = [sb(f"other{i}", [P, BANK]) for i in range(2)]
        mask_f = sb("mask_f", [P, 2, P])
        prob = [sb(f"prob{i}", [P, BANK]) for i in range(4)]
        attn_t = sb("attn_t", [P, H // 2, SEQ])
        neg_m = [sb(f"neg_m{i}", [P, G * NQB]) for i in range(2)]
        row_l = [sb(f"row_l{i}", [P, G * NQB]) for i in range(2)]
        ln_l = sb("ln_l", [P, G * NQB])
        neg_lse = sb("neg_lse", [P, G * NQB])
        lse_hi = [sb(f"lse_hi{i}", [G * NQB, P], F32R) for i in range(2)]
        lse_lo = [sb(f"lse_lo{i}", [G * NQB, P], F32R) for i in range(2)]
        scaled = sb("scaled", [P, 4, HID])

        ring = pb("ring", [P, 4 * BANK])
        ps_s = [pb(f"ps_s{i}", [P, BANK]) for i in range(2)]
        ps_o = pb("ps_o", [P, BANK])
        ps_m = pb("ps_m", [P, BANK])

        loads = [(w[:, :, i, :], a[n].rearrange("k (g d) -> k g d", g=HKV))
                 for w, n in ((wk, "wk"),) for i in range(2)]
        loads += [(wq[:, :], a["wq"]), (cos[:, :], a["cos"]), (sin[:, :], a["sin"]),
                 (wv[:, :], a["wv"]), (mask_f[:, :, :], a["masks"]),
                 (wo[:, :, :], a["wo"].rearrange("(c p) n -> p c n", p=P))]
        for out, in_ in loads:
            loaded = q.dma(out, in_, "attn_in")
        t_mask = q.dve(lambda e: e.tensor_copy(mask_b[:, :, :], mask_f[:, :, :]), [loaded], "attn_const_dve")
        for i in range(2):
            for h in range(G):
                lo = 0 if h % 2 else D
                q.pool(lambda e, i=i, h=h, lo=lo: e.memset(x2[i][lo:lo + D, h, :].bitcast(F32), 0.0), (), "attn_const")
        for i in range(3):
            for odd in range(2):
                lo = 0 if odd else D
                t = q.pool(lambda e, i=i, odd=odd, lo=lo: e.memset(k2[i][odd][lo:lo + D, :].bitcast(F32), 0.0),
                           (), "attn_const")
                consts = q.pool(lambda e, i=i, odd=odd, lo=lo: e.memset(k2[i][odd][lo:lo + 2, :].bitcast(F32), 1.0),
                                [t], "attn_const")

        q.act(lambda e: e.preload_act_table_set("natural_log_exp_and_others"))
        ring_free = [[], [], [], []]
        state = {"at": 0, "m_free": [], "o_free": [], "v_done": {}}

        def take(n):
            if state["at"] + n > 4:
                state["at"] = 0
            i = state["at"]
            state["at"] = (i + n) % 4
            return range(i, i + n), ring[:, i * BANK:(i + n) * BANK], sum((ring_free[j] for j in range(i, i + n)), [])

        def release(banks, tokens):
            for j in banks:
                ring_free[j] = tokens

        pv_done = {}
        x_free = {}
        a_done = {}
        ready_k, ready_x = {}, {}

        def project(g):
            b, kv = g // HKV, g % HKV
            buf = g % 2
            begun = []

            def begin_v():
                banks, ps, free = take(1)
                for n in range(NQB):
                    t0 = b * SEQ + n * P
                    t = q.pe(lambda e, n=n, t0=t0: e.matmul(ps[:, n * D:(n + 1) * D], h_t[:, t0:t0 + P],
                                                            wv[:, kv * D:(kv + 1) * D], start=True, stop=True),
                             [loaded] + free if n == 0 else (), "v_pe" if n == NQB - 1 else None)
                t = q.act(lambda e: e.activation(v[buf][:, :, :], ps.rearrange("p (n d) -> p n d", n=NQB), ACT.Copy),
                          [t] + pv_done.get(g - 2, []), "v_copy")
                release(banks, [t])
                state["v_done"][g] = t

            def begin(weights, c):
                n = state["rotations"] = state.get("rotations", -1) + 1
                i = n % 2
                banks, ps, free = take(1)
                cols = slice(b * SEQ + c * BANK, b * SEQ + (c + 1) * BANK)
                cc = slice(c * BANK, (c + 1) * BANK)
                t = q.pe(lambda e: e.matmul(ps, weights, h_t[:, cols], start=True, stop=True), [loaded] + free, "proj_pe")
                old = state.get(("split", i), [])
                q.dve(lambda e: e.tensor_tensor(rot[i][:, :], ps, cos[:, cc], ALU.mult), [t] + old, "rot_dve")
                t = q.dve(lambda e: e.stream_shuffle(other[i][:, :], ps, [k ^ 1 for k in range(32)]), (), "rot_dve")
                release(banks, [t])
                t = q.pool(lambda e: e.tensor_tensor(other[i][:, :], other[i][:, :], sin[:, cc], ALU.mult), [t], "rot_pool")
                t = q.pool(lambda e: e.tensor_tensor(rot[i][:, :], rot[i][:, :], other[i][:, :], ALU.add), [t], "rot_pool")
                return i, t

            def begin_k(c):
                begun.append((split_k, c, *begin(wk[:, kv, :, :], c)))

            def begin_q(pair, c):
                w0 = (kv * NPAIR + pair) * P
                begun.append((split_q(pair), c, *begin(wq[:, w0:w0 + P], c)))

            def split_k(c, i, t):
                cc = slice(c * BANK, (c + 1) * BANK)
                scale = float(D) ** -0.5
                t = q.dve(lambda e: e.tensor_scalar(k1[g % 3][:, cc], rot[i][:, :], scale, None, ALU.mult),
                          [t, consts] + x_free.get((g - 3, NPAIR - 1), []), "k_split")
                t = q.dve(lambda e: e.scalar_tensor_tensor(kl_dup[:, cc], rot[i][:, :], scale,
                                                           k1[g % 3][:, cc].bitcast(F32), ALU.mult, ALU.subtract),
                          [t] + a_done.get(g - 1, []), "k_split")
                for odd in range(2):
                    lo = D if odd else 0
                    t = q.dve(lambda e, odd=odd, lo=lo: e.tensor_copy(
                        k2[g % 3][odd][lo:lo + D, cc], kl_dup[lo:lo + D, cc].bitcast(F32)), [t], "k_split")
                ready_k[g] = [t]
                state["split", i] = [t]

            def split_q(pair):
                def run(c, i, t):
                    cc = slice(c * BANK, (c + 1) * BANK)
                    hi = []
                    for odd in range(2):
                        lo = D if odd else 0
                        h = 2 * pair + odd
                        t_hi = q.dve(lambda e, lo=lo, h=h: e.tensor_copy(x1[buf][lo:lo + D, h, cc], rot[i][lo:lo + D, :]),
                                     [t] + x_free.get((g - 2, pair), []), "q_split")
                        hi.append(t_hi)
                        ready_x[g, h, c] = q.dma(x2[buf][lo:lo + D, h, cc], x1[buf][lo:lo + D, h, cc],
                                                 f"x2_q{buf}", [t_hi, consts] + x_free.get((g - 2, pair), []))
                    for odd in range(2):
                        lo, far = (D, 0) if odd else (0, D)
                        h = 2 * pair + odd
                        t = q.dve(lambda e, lo=lo, far=far, h=h: e.tensor_tensor(
                            x1[buf][far:far + D, h, cc], rot[i][lo:lo + D, :], x1[buf][lo:lo + D, h, cc].bitcast(F32),
                            ALU.subtract), [hi[odd]], "q_split")
                        ready_x[g, h] = [t]
                    state["split", i] = [t]
                return run

            def split():
                f, c, i, t = begun.pop(0)
                f(c, i, t)

            def both(f, *args):
                def run():
                    f(*args)
                    if len(begun) > 1:
                        split()
                return run

            steps = [(2.5, both(begin_k, c)) for c in range(NCH)]
            steps += [(2.5, both(begin_q, pair, c)) for pair in range(NPAIR) for c in range(NCH)]
            steps += [(0.1, split), (1.0, begin_v)]
            return steps

        def first_pass(g):
            buf = g % 2
            units = []

            waiting = []

            def exp_of(i):
                banks, ps, n, col, t_m = waiting.pop(0)
                t_e = q.act(lambda e: e.activation(ps[:, 0:n], ps[:, 0:n], ACT.Exp, bias=neg_m[buf][:, col:col + 1],
                                                   accum_out=row_l[buf][:, col:col + 1]), [t_m], "s1_exp")
                release(banks, [t_e])
                state["last_exp"] = t_e

            def unit(h, qb):
                def run():
                    n = (qb + 1) * P
                    banks, ps, free = take(-(-n // BANK))
                    col = h * NQB + qb
                    qs = slice(qb * P, (qb + 1) * P)
                    first = True
                    for c0 in range(0, n, BANK):
                        c1 = min(c0 + BANK, n)
                        diag = c1 == n
                        q.pe(lambda e, c0=c0, c1=c1: e.matmul(ps[:, c0:c1], x1[buf][:, h, qs], k1[g % 3][:, c0:c1],
                                                              start=True, stop=False),
                             (ready_k[g] + ready_x[g, h] + free) if first else ())
                        q.pe(lambda e, c0=c0, c1=c1, diag=diag: e.matmul(
                            ps[:, c0:c1], x1[buf][:, h, qs], kl_dup[:, c0:c1], start=False, stop=not diag))
                        first = False
                    t = q.pe(lambda e: e.matmul(ps[:, n - P:n], ident_b[:, :], mask_b[:, 0, :], start=False, stop=True),
                             [t_mask], "s1_pe")
                    t_m = q.dve(lambda e: e.tensor_reduce(neg_m[buf][:, col:col + 1], ps[:, 0:n], AX, ALU.max, negate=True),
                                [t] + state.get(("lse_free", g - 2), []), "s1_max")
                    a_done[g] = [t]
                    waiting.append((banks, ps, n, col, t_m))
                    if len(waiting) > 1:
                        exp_of(0)
                return run

            for h in range(G):
                for qb in range(NQB):
                    units.append(((qb + 1) * 0.14 + 0.2, unit(h, qb)))
            units.append((0.1, lambda: exp_of(0)))
            units.append((0.1, lambda: finish_rows(g)))
            return units

        def finish_rows(g):
            buf = g % 2
            t = q.act(lambda e: e.activation(ln_l[:, :], row_l[buf][:, :], ACT.Ln), [state["last_exp"]] + state.get("lse_t", []),
                      "lse_ln")
            t = q.dve(lambda e: e.tensor_tensor(neg_lse[:, :], neg_m[buf][:, :], ln_l[:, :], ALU.subtract),
                      [t] + state.get("lse_pe", []), "lse_dve")
            state["lse_t"] = [t]
            state["lse_free", g] = [t]
            t = q.pe(lambda e: e.transpose(ps_m[0:G * NQB, 0:P], neg_lse[:, :], ident[:, :]), [t] + state["m_free"], "lse_pe")
            state["lse_pe"] = [t]
            old = state.get(("rows", buf), [])
            t_hi = q.dve(lambda e: e.tensor_copy(lse_hi[buf][:, :], ps_m[0:G * NQB, 0:P]), [t] + old, "lse_dve")
            t_lo = q.dve(lambda e: e.tensor_tensor(lse_lo[buf][:, :], ps_m[0:G * NQB, 0:P], lse_hi[buf][:, :].bitcast(F32),
                                                   ALU.subtract), [t_hi], "lse_dve")
            state["m_free"] = [t_lo]
            for h in range(G):
                lo = 0 if h % 2 else D
                for k, part in enumerate((lse_hi, lse_lo)):
                    t = q.dma(x2[buf][lo + k:lo + k + 1, h, :], part[buf][h * NQB:(h + 1) * NQB, :], f"x2_rows{buf}",
                              [t_lo, consts] + x_free.get((g - 2, NPAIR - 1), []))
            state["rows", buf] = [t]

        def second_pass(g):
            b, kv = g // HKV, g % HKV
            buf = g % 2
            steps = []
            work = []
            for pair in range(NPAIR):
                for c in range(NCH):
                    nk = (c + 1) * BANK // P
                    for kb in range(nk):
                        off = max(kb * P - c * BANK, 0)
                        work.append((pair, c, kb, off, kb * P >= c * BANK, kb == nk - 1))
            pending = []

            def product():
                (pair, c, kb, off, _, last), t_p, n = pending.pop(0)
                w = BANK - off
                for odd in range(2):
                    wait = [t_p[odd]] + ([state["v_done"][g]] + state["o_free"] if kb == 0 else [])
                    t = q.pe(lambda e, odd=odd: e.matmul(
                        ps_o[odd * D:(odd + 1) * D, off:BANK], v[buf][:, kb, :],
                        prob[2 * (n % 2) + odd][:, 0:w], start=kb == 0, stop=last), wait, "pv_pe")
                state["prob", n % 2] = [t]
                pv_done[g] = [t]
                if last:
                    t = q.dve(lambda e: e.tensor_copy(attn_t[:, kv * NPAIR + pair, c * BANK:(c + 1) * BANK], ps_o[:, :]),
                              [t] + state.get("wo_pe", []), "o_copy")
                    state["o_free"] = [t]
                    state["o_last"] = t

            def step(item):
                def run():
                    pair, c, kb, off, diag, last = item
                    w = BANK - off
                    q0 = c * BANK + off
                    n = state.setdefault("steps", 0)
                    state["steps"] += 1
                    tokens = []
                    for odd in range(2):
                        h = 2 * pair + odd
                        ks = slice(kb * P, (kb + 1) * P)
                        wait = state.get(("s_free", odd), []) + state["rows", buf] + [ready_x[g, G - 1, NCH - 1]]
                        q.pe(lambda e, odd=odd, h=h, ks=ks: e.matmul(
                            ps_s[odd][:, 0:w], k1[g % 3][:, ks], x1[buf][:, h, q0:q0 + w], start=True, stop=False), wait)
                        t = q.pe(lambda e, odd=odd, h=h, ks=ks: e.matmul(
                            ps_s[odd][:, 0:w], k2[g % 3][odd][:, ks], x2[buf][:, h, q0:q0 + w], start=False, stop=not diag),
                            (), None if diag else "s2_pe")
                        if diag:
                            t = q.pe(lambda e, odd=odd: e.matmul(ps_s[odd][:, 0:P], ident_b[:, :], mask_b[:, 1, :],
                                                                 start=False, stop=True), (), "s2_pe")
                        t = q.act(lambda e, odd=odd: e.activation(prob[2 * (n % 2) + odd][:, 0:w], ps_s[odd][:, 0:w],
                                                                  ACT.Exp), [t] + state.get(("prob", n % 2), []), "s2_exp")
                        state["s_free", odd] = [t]
                        tokens.append(t)
                    x_free[g, pair] = [("s2_pe", q.counts["s2_pe"].value)]
                    if pending:
                        product()
                    pending.append((item, tokens, n))
                return run

            steps = [((BANK - item[3]) / BANK * 1.8 + 0.1, step(item)) for item in work]
            steps.append((0.9, lambda: product()))
            if kv == HKV - 1:
                steps.append((1.0, lambda: output(b)))
            return steps

        def output(b):
            x_in = q.dma(x[:, b * TPB:(b + 1) * TPB, :], a["x"][b].rearrange("(t p) n -> p t n", p=P), f"x_again{b % 2}",
                         [h_done[b]])
            for n in range(TPB // 4):
                for j in range(4):
                    blk = slice((n * 4 + j) * P, (n * 4 + j + 1) * P)
                    for c in range(H // 2):
                        t = q.pe(lambda e, j=j, c=c, blk=blk: e.matmul(
                            ps_m[:, j * HID:(j + 1) * HID], attn_t[:, c, blk], wo[:, c, :],
                            start=c == 0, stop=c == H // 2 - 1),
                            [state["o_last"]] + state["m_free"] if j == 0 and c == 0 else (),
                            "wo_pe" if c == H // 2 - 1 and j == 3 else None)
                tile = b * TPB + n * 4
                t_s = q.dve(lambda e, b=b: e.tensor_tensor(
                    scaled[:, :, :], ps_m[:, :].rearrange("p (j n) -> p j n", j=4),
                    gate_bc[:, b:b + 1, :].to_broadcast([P, 4, HID]), ALU.mult), [t] + state.get("res", []), "wo_scale")
                state["m_free"] = [t_s]
                state["res"] = [q.pool(lambda e, tile=tile: e.tensor_tensor(
                    x[:, tile:tile + 4, :], x[:, tile:tile + 4, :], scaled[:, :, :], ALU.add), [t_s, x_in], "wo_add")]
            state["wo_pe"] = [t]

        h_done = {}
        groups = BATCH * HKV
        order = []

        def spread(steps, start):
            total = sum(cost for cost, _ in steps)
            used = 0.0
            for cost, step in steps:
                order.append((start + used / total, step))
                used += cost
            return total

        for g in range(groups):
            def projected(g=g):
                h_done[g // HKV] = ("proj_pe", q.counts["proj_pe"].value)
            turn = project(g)
            before_pair_1 = sum(cost for cost, _ in turn[:2 * NCH])
            total = spread(turn + [(0.0, projected)] + first_pass(g), g)
            lag = before_pair_1 / total
            spread(second_pass(g), g + 1 + lag - 1e-6)
        for _, step in sorted(order, key=lambda item: item[0]):
            step()
        q.run()


def route(q, nc, name, ctx, h_t, gate, loaded, iota, tri, capacity):
    NE = 8
    shape = [P, TILES, NE]
    if capacity is None:
        combine = ctx.enter_context(nc.sbuf_tensor(f"combine{name}", shape, F32))
    else:
        slot = ctx.enter_context(nc.sbuf_tensor("slot", [P, 2, TILES], I32))
        weight = ctx.enter_context(nc.sbuf_tensor("weight", [P, 2, TILES], F32))
    with ExitStack() as own:
        def sb(n, s=shape):
            return own.enter_context(nc.sbuf_tensor(f"{n}{name}", s, F32))
        ps = own.enter_context(nc.psum_tensor(f"ps_route{name}", shape, F32))
        prob, tmp, cand = sb("r_prob"), sb("r_tmp"), sb("r_cand")
        mask = [sb("r_mask0"), sb("r_mask1")]
        top = [sb("r_top0", [P, TILES]), sb("r_top1", [P, TILES])]
        red = sb("r_red", [P, TILES])
        for i in range(TILES):
            t = q.pe(lambda e, i=i: e.matmul(ps[:, i, :], h_t[:, i * P:(i + 1) * P], gate[:, :], start=True, stop=True),
                     [loaded], "route_pe")
        chain = [t]

        def dve(f):
            chain[0] = q.dve(f, [chain[0]], "route_dve")

        def over(v):
            return v[:, :].rearrange("p (t o) -> p t o", o=1).to_broadcast(shape)

        io = iota[:, :].rearrange("p (o n) -> p o n", o=1).to_broadcast(shape)
        dve(lambda e: e.tensor_reduce(red[:, :], ps[:, :, :], AX, ALU.max))
        dve(lambda e: e.tensor_tensor(tmp[:, :, :], ps[:, :, :], over(red), ALU.subtract))
        chain[0] = q.act(lambda e: e.activation(tmp[:, :, :], tmp[:, :, :], ACT.Exp), [chain[0]], "route_exp")
        dve(lambda e: e.tensor_reduce(red[:, :], tmp[:, :, :], AX, ALU.add))
        dve(lambda e: e.reciprocal(red[:, :], red[:, :]))
        dve(lambda e: e.tensor_tensor(prob[:, :, :], tmp[:, :, :], over(red), ALU.mult))
        dve(lambda e: e.tensor_copy(tmp[:, :, :], prob[:, :, :]))
        for k in range(2):
            m, tp = mask[k], top[k]
            dve(lambda e, tp=tp: e.tensor_reduce(tp[:, :], tmp[:, :, :], AX, ALU.max))
            dve(lambda e, tp=tp: e.tensor_tensor(cand[:, :, :], tmp[:, :, :], over(tp), ALU.is_equal))
            dve(lambda e: e.tensor_scalar(cand[:, :, :], cand[:, :, :], -float(NE), float(NE), ALU.mult, ALU.add))
            dve(lambda e: e.tensor_tensor(cand[:, :, :], cand[:, :, :], io, ALU.add))
            dve(lambda e: e.tensor_reduce(red[:, :], cand[:, :, :], AX, ALU.min))
            dve(lambda e, m=m: e.tensor_tensor(m[:, :, :], io, over(red), ALU.is_equal))
            if k == 0:
                dve(lambda e, m=m: e.scalar_tensor_tensor(tmp[:, :, :], m[:, :, :], -2.0, tmp[:, :, :], ALU.mult, ALU.add))
        if capacity is None:
            dve(lambda e: e.tensor_tensor(red[:, :], top[0][:, :], top[1][:, :], ALU.add))
            dve(lambda e: e.tensor_scalar(red[:, :], red[:, :], 1e-20, None, ALU.add))
            dve(lambda e: e.reciprocal(red[:, :], red[:, :]))
            for k in range(2):
                dve(lambda e, k=k: e.tensor_tensor(top[k][:, :], top[k][:, :], red[:, :], ALU.mult))
        else:
            ones = sb("r_ones", [P, P])
            t_one = q.pool(lambda e: e.memset(ones[:, :], 1.0), (), "route_pool")
            ps_rank = own.enter_context(nc.psum_tensor(f"ps_rank{name}", shape, F32))
            ps_tot = own.enter_context(nc.psum_tensor(f"ps_tot{name}", shape, F32))
            run_a, run_b = sb("r_run_a"), sb("r_run_b")
            for k in range(2):
                t = q.pe(lambda e, k=k: e.matmul(ps_rank[:, :, :], tri[:, :], mask[k][:, :, :], start=True, stop=True),
                         [chain[0], t_one], "rank_pe")
                chain[0] = q.pe(lambda e, k=k: e.matmul(ps_tot[:, :, :], ones[:, :], mask[k][:, :, :], start=True, stop=True),
                                (), "rank_pe")
                dve(lambda e: e.memset(run_a[:, 0:1, :], 0.0))
                dve(lambda e: e.tensor_copy(run_a[:, 1:TILES, :], ps_tot[:, 0:TILES - 1, :]))
                src, dst = run_a, run_b
                s = 1
                while s < TILES:
                    dve(lambda e, s=s, src=src, dst=dst: e.tensor_copy(dst[:, 0:s, :], src[:, 0:s, :]))
                    dve(lambda e, s=s, src=src, dst=dst: e.tensor_tensor(
                        dst[:, s:TILES, :], src[:, s:TILES, :], src[:, 0:TILES - s, :], ALU.add))
                    src, dst = dst, src
                    s *= 2
                dve(lambda e, src=src: e.tensor_tensor(src[:, :, :], src[:, :, :], ps_rank[:, :, :], ALU.add))
                late = 2.0 * NE * capacity
                dve(lambda e, src=src: e.tensor_scalar(tmp[:, :, :], src[:, :, :], float(capacity), late, ALU.is_ge, ALU.mult))
                dve(lambda e, src=src: e.tensor_tensor(tmp[:, :, :], tmp[:, :, :], src[:, :, :], ALU.add))
                dve(lambda e: e.scalar_tensor_tensor(tmp[:, :, :], io, float(capacity), tmp[:, :, :], ALU.mult, ALU.add))
                dve(lambda e, k=k: e.tensor_tensor(tmp[:, :, :], tmp[:, :, :], mask[k][:, :, :], ALU.mult))
                dve(lambda e: e.tensor_reduce(red[:, :], tmp[:, :, :], AX, ALU.add))
                dve(lambda e, k=k: e.tensor_copy(slot[:, k, :], red[:, :]))
                dve(lambda e, k=k: e.tensor_copy(weight[:, k, :], top[k][:, :]))
            q.run()
            return slot, weight
        dve(lambda e: e.tensor_tensor(tmp[:, :, :], mask[0][:, :, :], over(top[0]), ALU.mult))
        dve(lambda e: e.tensor_tensor(cand[:, :, :], mask[1][:, :, :], over(top[1]), ALU.mult))
        dve(lambda e: e.tensor_tensor(combine[:, :, :], tmp[:, :, :], cand[:, :, :], ALU.add))
        q.run()
    return combine


def experts(q, nc, name, x, h_t, combine, gate_bc, up, down, fp, gated, bias_bc):
    NE = 8
    NCHUNK = TOK // BANK
    NF = 2 if gated else 4
    with ExitStack() as ctx:
        def sb(n, s):
            return ctx.enter_context(nc.sbuf_tensor(f"{n}{name}", s, F32))
        hid = [sb(f"hid{i}", [fp, NF, BANK]) for i in range(2)]
        silu = [sb(f"silu{i}", [fp, BANK]) for i in range(2)]
        acc = [sb(f"acc{i}", [P, 4, HID]) for i in range(2)]
        part = [sb(f"part{i}", [P, 4, HID]) for i in range(2)]
        ps_up = [ctx.enter_context(nc.psum_tensor(f"ps_up{name}{i}", [P, 2, BANK], F32)) for i in range(3)]
        ps_dn = [ctx.enter_context(nc.psum_tensor(f"ps_dn{name}{i}", [P, 4, HID], F32)) for i in range(2)]
        up_free, dn_free = [[], [], []], [[], []]
        hid_free, part_free, silu_free = [[], []], [[], []], [[], []]
        acc_done = {}
        units = [(n, e) for n in range(NCHUNK) for e in range(NE)]
        made = {}

        def up_stage(k):
            n, e = units[k]
            cols = slice(n * BANK, (n + 1) * BANK)
            for j in range(2):
                r = (2 * k + j) % 3
                ps = ps_up[r]
                for m in range(2):
                    t = q.pe(lambda en, ps=ps, m=m, j=j, e=e: en.matmul(ps[0:fp, m, :], up(e, 2 * j + m), h_t[:, cols],
                                                                        start=True, stop=True),
                             up_free[r] if m == 0 else (), "up_pe")
                dst = hid[k % 2]
                if gated:
                    t_s = q.act(lambda en, ps=ps, j=j: en.activation(silu[j][:, :], ps[0:fp, 0, :], ACT.Silu),
                                [t] + silu_free[j], "up_act")
                    t = q.dve(lambda en, ps=ps, j=j, dst=dst: en.tensor_tensor(dst[:, j, :], ps[0:fp, 1, :], silu[j][:, :],
                                                                               ALU.mult), [t_s] + hid_free[k % 2], "up_dve")
                    silu_free[j] = [t]
                else:
                    t = q.act(lambda en, ps=ps, j=j, dst=dst: en.activation(dst[:, 2 * j:2 * j + 2, :], ps[0:fp, :, :],
                                                                            ACT.Gelu_apprx_tanh),
                              [t] + hid_free[k % 2], "up_act")
                up_free[r] = [t]
            made[k] = t

        def down_stage(k):
            n, e = units[k]
            ps = ps_dn[k % 2]
            for i in range(4):
                for f in range(NF):
                    t = q.pe(lambda en, i=i, f=f: en.matmul(ps[:, i, :], hid[k % 2][:, f, i * P:(i + 1) * P], down(e, f),
                                                            start=f == 0, stop=f == NF - 1),
                             [made[k]] + dn_free[k % 2] if i == 0 and f == 0 else (), "dn_pe" if i == 3 and f == NF - 1 else None)
            hid_free[k % 2] = [t]
            w = combine[:, 4 * n:4 * n + 4, e:e + 1].to_broadcast([P, 4, HID])
            a = acc[n % 2]
            if e == 0:
                t = q.dve(lambda en: en.tensor_tensor(a[:, :, :], ps[:, :, :], w, ALU.mult),
                          [t] + acc_done.get(n - 2, []), "dn_dve")
                dn_free[k % 2] = [t]
                acc_done[n] = [t]
                return
            pt = part[k % 2]
            t = q.dve(lambda en: en.tensor_tensor(pt[:, :, :], ps[:, :, :], w, ALU.mult), [t] + part_free[k % 2], "dn_dve")
            dn_free[k % 2] = [t]
            t = q.pool(lambda en: en.tensor_tensor(a[:, :, :], a[:, :, :], pt[:, :, :], ALU.add),
                       [t] + acc_done[n], "dn_add")
            part_free[k % 2] = [t]
            acc_done[n] = [t]
            if e == NE - 1:
                b = n * 4 // TPB
                if bias_bc is not None:
                    t = q.pool(lambda en: en.tensor_tensor(a[:, :, :], a[:, :, :],
                                                           bias_bc[:, :, :].to_broadcast([P, 4, HID]), ALU.add),
                               [t], "dn_add")
                t = q.pool(lambda en: en.tensor_tensor(a[:, :, :], a[:, :, :], gate_bc[:, b:b + 1, :].to_broadcast([P, 4, HID]),
                                                       ALU.mult), [t], "dn_add")
                t = q.pool(lambda en: en.tensor_tensor(x[:, 4 * n:4 * n + 4, :], x[:, 4 * n:4 * n + 4, :], a[:, :, :], ALU.add),
                           [t], "dn_add")
                acc_done[n] = [t]

        for k in range(len(units)):
            up_stage(k)
            if k:
                down_stage(k - 1)
        down_stage(len(units) - 1)
        q.run()


def capacity_experts(q, nc, x, h, slot, weight, w1_in, w2, bias_bc, gate_bc, ident, slots_in, slots_out, out):
    NE, NF = E1, F1 // P
    NSLOT = NE * CAPACITY
    SB = CAPACITY // P
    with ExitStack() as ctx:
        def sb(n, s, dt=F32):
            return ctx.enter_context(nc.sbuf_tensor(f"c_{n}", s, dt))
        got = sb("got", [P, 2, TILES, HID])
        w_stage = [sb(f"w_stage{i}", [P, F1]) for i in range(2)]
        w_hi, w_lo = ([sb(f"{n}{i}", [P, F1], F32R) for i in range(2)] for n in ("w_hi", "w_lo"))
        rows = [sb(f"rows{i}", [P, SB, HID]) for i in range(2)]
        xt_hi, xt_lo = ([sb(f"{n}{i}", [P, CAPACITY], F32R) for i in range(2)] for n in ("xt_hi", "xt_lo"))
        hid = [sb(f"hid{i}", [P, NF, CAPACITY]) for i in range(2)]
        res = [sb(f"res{i}", [P, SB, HID]) for i in range(2)]
        acc = [sb(f"acc{i}", [P, 4, HID]) for i in range(2)]
        ps_up = [ctx.enter_context(nc.psum_tensor(f"c_up{i}", [P, 2, BANK], F32)) for i in range(2)]
        ps_tr = [ctx.enter_context(nc.psum_tensor(f"c_tr{i}", [P, BANK], F32)) for i in range(2)]
        ps_dn = [ctx.enter_context(nc.psum_tensor(f"c_dn{i}", [P, SB, HID], F32)) for i in range(2)]

        def scatter(k):
            for i in range(TILES):
                t = q.put("gpsimd", lambda e, i=i, k=k: e.indirect_dma_start(
                    slots_in[k][:, :], bass.IndirectOffsetOnAxis(ap=slot[:, k, i:i + 1], axis=0), h[:, i, :], None,
                    bounds_check=NSLOT - 1, oob_is_err=False), (), f"scatter{k}", 16)
            return t

        def gather(k, written):
            for i in range(TILES):
                q.put("gpsimd", lambda e, i=i, k=k: e.indirect_dma_start(
                    got[:, k, i, :], None, slots_out[k][:, :], bass.IndirectOffsetOnAxis(ap=slot[:, k, i:i + 1], axis=0),
                    bounds_check=NSLOT - 1, oob_is_err=False), written + [zeroed], f"gather{k}_{i // 4}", 16)

        zeroed = q.dve(lambda e: e.memset(got[:, :, :, :], 0.0), (), "got_zero")
        scattered = [scatter(0), scatter(1)]
        free = {}
        made = {}

        def begin(n):
            k, e_, i = n // NE, n % NE, n % 2
            t_w = q.dma(w_stage[i][:, :], w1_in[e_], f"c_w{i}", free.get(("stage", i), []))
            t_h = q.dve(lambda e: e.tensor_copy(w_hi[i][:, :], w_stage[i][:, :]), [t_w] + free.get(("up", i), []), "c_wsplit")
            t_w = q.dve(lambda e: e.tensor_tensor(w_lo[i][:, :], w_stage[i][:, :], w_hi[i][:, :].bitcast(F32), ALU.subtract),
                        [t_h], "c_wsplit")
            free["stage", i] = [t_w]
            t = q.dma(rows[i][:, :, :], slots_in[k][e_ * CAPACITY:(e_ + 1) * CAPACITY, :].rearrange("(s p) n -> p s n", p=P),
                      f"c_rows{i}", [scattered[k]] + free.get(("rows", i), []))
            for j in range(SB):
                t_t = q.pe(lambda e, j=j: e.transpose(ps_tr[i][:, j * P:(j + 1) * P], rows[i][:, j, :], ident[:, :]),
                           [t] + free.get(("tr", i), []) if j == 0 else (), "c_tr" if j == SB - 1 else None)
            free["rows", i] = [t_t]
            t = q.dve(lambda e: e.tensor_copy(xt_hi[i][:, :], ps_tr[i][:, :]), [t_t] + free.get(("up", i), []), "c_xsplit")
            t = q.dve(lambda e: e.tensor_tensor(xt_lo[i][:, :], ps_tr[i][:, :], xt_hi[i][:, :].bitcast(F32), ALU.subtract),
                      [t], "c_xsplit")
            free["tr", i] = [t]
            for j in range(NF // 2):
                for m in range(2):
                    f = slice((2 * j + m) * P, (2 * j + m + 1) * P)
                    parts = ((w_hi, xt_hi), (w_hi, xt_lo), (w_lo, xt_hi))
                    for p, (w, xx) in enumerate(parts):
                        t_u = q.pe(lambda e, j=j, m=m, f=f, w=w, xx=xx, p=p: e.matmul(
                            ps_up[j][:, m, :], w[i][:, f], xx[i][:, :], start=p == 0, stop=p == 2),
                            [t, t_w] + free.get(("ps", j), []) if m == 0 and p == 0 else (),
                            "c_up" if m == 1 and p == 2 else None)
                t_g = q.act(lambda e, j=j: e.activation(hid[i][:, 2 * j:2 * j + 2, :], ps_up[j][:, :, :], ACT.Gelu_apprx_tanh),
                            [t_u] + free.get(("hid", i), []), "c_gelu")
                free["ps", j] = [t_g]
            free["up", i] = [t_u]
            made[n] = t_g

        def end(n):
            e_, i = n % NE, n % 2
            for j in range(SB):
                for f in range(NF):
                    t = q.pe(lambda e, j=j, f=f: e.matmul(ps_dn[i][:, j, :], hid[i][:, f, j * P:(j + 1) * P], w2[:, e_, f, :],
                                                          start=f == 0, stop=f == NF - 1),
                             [made[n]] + free.get(("dn", i), []) if j == 0 and f == 0 else (),
                             "c_dn" if j == SB - 1 and f == NF - 1 else None)
            free["hid", i] = [t]
            t = q.act(lambda e: e.activation(res[i][:, :, :], ps_dn[i][:, :, :], ACT.Copy), [t] + free.get(("res", i), []), "c_res")
            free["dn", i] = [t]
            t = q.dma(slots_out[n // NE][e_ * CAPACITY:(e_ + 1) * CAPACITY, :].rearrange("(s p) n -> p s n", p=P), res[i][:, :, :],
                      f"c_out{i}", [t])
            free["res", i] = [t]

        def results(k):
            return free["res", 0] + free["res", 1]

        for n in range(2 * NE):
            begin(n)
            if n:
                end(n - 1)
            if n == NE:
                gather(0, results(0))
        end(2 * NE - 1)
        state = {}
        gather(1, results(1))

        def wide(v):
            return v.rearrange("p (t o) -> p t o", o=1).to_broadcast([P, 4, HID])

        def mix(m):
            ts = slice(4 * m, 4 * m + 4)
            a, b = acc[m % 2], m * 4 // TPB
            t = q.dve(lambda e: e.tensor_tensor(a[:, :, :], got[:, 0, ts, :], wide(weight[:, 0, ts]), ALU.mult),
                      [(f"gather0_{m}", 4 * 16)] + state.get(m % 2, []), "c_mix")
            t_1 = q.dve(lambda e: e.tensor_tensor(got[:, 1, ts, :], got[:, 1, ts, :], wide(weight[:, 1, ts]), ALU.mult),
                        [(f"gather1_{m}", 4 * 16)], "c_mix")
            t = q.dve(lambda e: e.tensor_tensor(a[:, :, :], a[:, :, :], bias_bc[:, :, :].to_broadcast([P, 4, HID]), ALU.add),
                      [t], "c_mix")
            t = q.dve(lambda e: e.tensor_tensor(a[:, :, :], a[:, :, :], got[:, 1, ts, :], ALU.add), [t, t_1], "c_mix")
            t = q.dve(lambda e: e.tensor_tensor(a[:, :, :], a[:, :, :], gate_bc[:, b:b + 1, :].to_broadcast([P, 4, HID]), ALU.mult),
                      [t], "c_mix")
            t = q.dve(lambda e: e.tensor_tensor(x[:, ts, :], x[:, ts, :], a[:, :, :], ALU.add), [t], "c_mix")
            state[m % 2] = [t]
            q.dma(out[b, (m * 4 % TPB) * P:(m * 4 % TPB + 4) * P, :].rearrange("(t p) n -> p t n", p=P), x[:, ts, :], "out", [t])

        for m in range(TILES // 4):
            mix(m)
        q.put("sync", lambda e: e.nop(), [("out", q.counts["out"].value)])
        q.run()


def selective_scan(q, nc, a, x, h_t, gate_bc):
    FG = P // NST
    NG = HID // FG
    with ExitStack() as ctx:
        def sb(n, s=(P, SEQ), dt=F32):
            return ctx.enter_context(nc.sbuf_tensor(f"m_{n}", list(s), dt))

        def pb(n, s):
            return ctx.enter_context(nc.psum_tensor(f"m_{n}", s, F32))
        w_in, w_x, w_out = sb("w_in", (P, 2 * HID)), sb("w_x", (P, 2 * NST + 1)), sb("w_out", (P, HID))
        w_b, w_c, w_d = sb("w_b", (P, FG, NST)), sb("w_c", (P, FG, NST)), sb("w_d", (P, P))
        cw, cb, dp = sb("cw", (P, TAPS)), sb("cb", (P, 1)), sb("dp", (P, 1))
        a_neg, log_a = sb("a_neg", (P, NG)), sb("log_a", (P, NG))
        sel_in, sel = sb("sel_in", (P, NG * P // 2)), sb("sel", (P, NG * P), F32R)
        fold = sb("fold", (P, 2 * P - FG))
        xm = [sb(f"xm{i}", (P, SEQ + TAPS - 1)) for i in range(2)]
        z = [sb(f"z{i}") for i in range(2)]
        u, conv = [sb(f"u{i}") for i in range(2)], sb("conv")
        raw, soft, delta, du = sb("raw"), sb("soft"), [sb(f"delta{i}") for i in range(2)], sb("du")
        du_hi, du_lo = ([sb(f"{n}{i}", (P, SEQ), F32R) for i in range(2)] for n in ("du_hi", "du_lo"))
        brep, crep = [sb(f"brep{i}") for i in range(2)], [sb(f"crep{i}") for i in range(2)]
        da, bu, st, hc = ([sb(f"{n}{i}") for i in range(3)] for n in ("da", "bu", "st", "hc"))
        y = sb("y")
        scaled = sb("scaled", (P, 4, HID))
        ps_y = [pb(f"ps_y{i}", [P, BANK]) for i in range(2)]
        ps_x = [pb(f"ps_x{i}", [P, 2 * BANK]) for i in range(2)]
        ps_w = [pb(f"ps_w{i}", [P, BANK]) for i in range(2)]

        for out, in_ in [(w_in[:, :], a["w_in"]), (w_x[:, :], a["w_xproj"]), (w_out[:, :], a["w_out"]),
                         (cw[:, :], a["conv_w"]), (cb[:, :], a["conv_b"]), (dp[:, :], a["d_param"]),
                         (log_a[:, :], a["log_a"]), (fold[:, :], a["fold"])]:
            loaded = q.dma(out, in_, "mamba_in")
        half = NG * P // 2
        for i in range(2):
            t = q.dma(sel_in[:, :], a["sel"][:, i * half:(i + 1) * half], f"sel_in{i}", [("m_sel", i)] if i else ())
            t_sel = q.dve(lambda e, i=i: e.tensor_copy(sel[:, i * half:(i + 1) * half], sel_in[:, :]), [t], "m_sel")
        q.dve(lambda e: e.tensor_copy(w_b[:, :, :], w_x[:, 0:NST].rearrange("p (o n) -> p o n", o=1).to_broadcast([P, FG, NST])),
              [loaded], "m_const")
        q.dve(lambda e: e.tensor_copy(w_c[:, :, :], w_x[:, NST:2 * NST].rearrange("p (o n) -> p o n", o=1).to_broadcast([P, FG, NST])),
              (), "m_const")
        reps = q.dve(lambda e: e.tensor_copy(w_d[:, :], w_x[:, 2 * NST:2 * NST + 1].to_broadcast([P, P])), (), "m_const")
        t = q.act(lambda e: e.activation(a_neg[:, :], log_a[:, :], ACT.Exp), [loaded], "m_a")
        t_a = q.dve(lambda e: e.tensor_scalar(a_neg[:, :], a_neg[:, :], -1.0, None, ALU.mult), [t], "m_const")
        for i in range(2):
            t_pad = q.pool(lambda e, i=i: e.memset(xm[i][:, 0:TAPS - 1], 0.0), (), "m_pad")

        w_free = [[], []]
        nw = [0]

        def product(lhs, cols, wait):
            i = nw[0] % 2
            nw[0] += 1
            return i, q.pe(lambda e, i=i: e.matmul(ps_w[i][:, :], lhs, cols, start=True, stop=True),
                           wait + w_free[i], "mw_pe")

        old = {}

        def prepare(b):
            k = b % 2
            for c in range(SEQ // BANK):
                cols = h_t[:, b * SEQ + c * BANK:b * SEQ + (c + 1) * BANK]
                i, t = product(w_in[:, 0:HID], cols, [loaded])
                t_x = q.act(lambda e, i=i, c=c: e.activation(xm[k][:, TAPS - 1 + c * BANK:TAPS - 1 + (c + 1) * BANK], ps_w[i][:, :],
                                                             ACT.Copy), [t, t_pad] + old.get(("conv", b - 2), []), "m_act")
                w_free[i] = [t_x]
                yield
                i, t = product(w_in[:, HID:2 * HID], cols, [])
                t = q.act(lambda e, i=i, c=c: e.activation(z[k][:, c * BANK:(c + 1) * BANK], ps_w[i][:, :], ACT.Silu),
                          [t] + old.get(("y", b - 2), []), "m_act")
                w_free[i] = [t]
                yield
            t = q.dve(lambda e: e.tensor_scalar(conv[:, :], xm[k][:, 0:SEQ], cw[:, 0:1], cb[:, 0:1], ALU.mult, ALU.add),
                      [t_x] + old.get(("u", b - 1), []), "m_conv")
            for j in range(1, TAPS):
                t = q.dve(lambda e, j=j: e.scalar_tensor_tensor(conv[:, :], xm[k][:, j:j + SEQ], cw[:, j:j + 1], conv[:, :],
                                                                ALU.mult, ALU.add), [t], "m_conv")
                yield
            old["conv", b] = [t]
            t_u = q.act(lambda e: e.activation(u[k][:, :], conv[:, :], ACT.Silu), [t] + old.get(("y", b - 2), []), "m_act")
            old["u", b] = [t_u]
            yield
            for dst, w, what in ((brep, w_b, "b"), (crep, w_c, "c")):
                for c in range(SEQ // BANK):
                    i, t = product(w[:, :, :], u[k][:, c * BANK:(c + 1) * BANK], [t_u, reps])
                    t = q.act(lambda e, i=i, c=c, dst=dst: e.activation(dst[k][:, c * BANK:(c + 1) * BANK], ps_w[i][:, :], ACT.Copy),
                              [t] + old.get(("scan", b - 2), []), "m_act")
                    w_free[i] = [t]
                    yield
            old["bc", b] = [t]
            for c in range(SEQ // BANK):
                i, t = product(w_d[:, :], u[k][:, c * BANK:(c + 1) * BANK], [])
                t = q.act(lambda e, i=i, c=c: e.activation(raw[:, c * BANK:(c + 1) * BANK], ps_w[i][:, :], ACT.Copy),
                          [t] + old.get(("du", b - 1), []), "m_act")
                w_free[i] = [t]
            yield
            t = q.act(lambda e: e.activation(soft[:, :], raw[:, :], ACT.Abs), [t], "m_act")
            t = q.act(lambda e: e.activation(soft[:, :], soft[:, :], ACT.Exp, scale=-1.0), [t], "m_act")
            t = q.act(lambda e: e.activation(soft[:, :], soft[:, :], ACT.Ln, bias=1.0), [t], "m_act")
            t_d = q.dve(lambda e: e.scalar_tensor_tensor(delta[k][:, :], raw[:, :], 0.0, soft[:, :], ALU.max, ALU.add),
                        [t] + old.get(("scan", b - 2), []), "m_delta")
            yield
            t = q.dve(lambda e: e.tensor_tensor(du[:, :], delta[k][:, :], u[k][:, :], ALU.mult),
                      [t_d, t_u] + old.get(("du", b - 1), []), "m_delta")
            t = q.dve(lambda e: e.tensor_copy(du_hi[k][:, :], du[:, :]), [t] + old.get(("scan", b - 2), []), "m_delta")
            t = q.dve(lambda e: e.tensor_tensor(du_lo[k][:, :], du[:, :], du_hi[k][:, :].bitcast(F32), ALU.subtract), [t], "m_delta")
            old["du", b] = [t]
            yield

        def groups(b):
            k = b % 2
            pend = []

            def gather(g, r, t_hc):
                for c in range(SEQ // BANK):
                    w0 = P - FG - FG * g
                    t = q.pe(lambda e, c=c: e.matmul(ps_y[c][:, :], fold[:, w0:w0 + P], hc[r][:, c * BANK:(c + 1) * BANK],
                                                     start=g == 0, stop=g == NG - 1),
                             [t_hc] + (old.get(("ysum", b - 1), []) if g == 0 else []), "my_pe")
                old["hc", r] = [t]
                return t

            for g in range(NG):
                n = b * NG + g
                i, r = n % 2, n % 3
                for c in range(SEQ // BANK):
                    for part in (du_hi, du_lo):
                        t = q.pe(lambda e, c=c, i=i, g=g, part=part: e.matmul(
                            ps_x[i][:, c * BANK:(c + 1) * BANK], sel[:, g * P:(g + 1) * P],
                            part[k][:, c * BANK:(c + 1) * BANK], start=part is du_hi, stop=part is du_lo),
                            [t_sel] + old["du", b] + old.get(("px", i), []), "mx_pe")
                t_da = q.act(lambda e, r=r, g=g: e.activation(da[r][:, :], delta[k][:, :], ACT.Exp, scale=a_neg[:, g:g + 1]),
                             [t_a] + old["du", b] + old.get(("st", r), []), "m_da")
                t_bu = q.dve(lambda e, i=i, r=r: e.tensor_tensor(bu[r][:, :], ps_x[i][:, :], brep[k][:, :], ALU.mult),
                             [t] + old["bc", b] + old.get(("st", r), []), "m_bu")
                old["px", i] = [t_bu]
                t = q.dve(lambda e, r=r: e.tensor_tensor_scan(st[r][:, :], da[r][:, :], bu[r][:, :], 0.0, ALU.mult, ALU.add),
                          [t_bu, t_da] + old.get(("hp", r), []), "m_scan")
                old["st", r] = [t]
                t = q.pool(lambda e, r=r: e.tensor_tensor(hc[r][:, :], st[r][:, :], crep[k][:, :], ALU.mult),
                           [t] + old.get(("hc", r), []) + old["bc", b], "m_hc")
                old["hp", r] = [t]
                if len(pend) == 2:
                    gather(*pend.pop(0))
                pend.append((g, r, t))
                yield
            for item in pend:
                t = gather(*item)
            old["scan", b] = [t]
            for c in range(SEQ // BANK):
                cc = slice(c * BANK, (c + 1) * BANK)
                t1 = q.dve(lambda e, c=c, cc=cc: e.scalar_tensor_tensor(y[:, cc], u[k][:, cc], dp[:, 0:1], ps_y[c][:, :],
                                                                        ALU.mult, ALU.add), [t] + old.get("out", []), "m_y")
            old["ysum", b] = [t1]
            t = q.dve(lambda e: e.tensor_tensor(y[:, :], y[:, :], z[k][:, :], ALU.mult), [t1], "m_y")
            old["y", b] = [t]
            for n in range(TPB // 4):
                i = nw[0] % 2
                nw[0] += 1
                for j in range(4):
                    blk = slice((n * 4 + j) * P, (n * 4 + j + 1) * P)
                    t_o = q.pe(lambda e, i=i, j=j, blk=blk: e.matmul(ps_w[i][:, j * HID:(j + 1) * HID], y[:, blk], w_out[:, :],
                                                                     start=True, stop=True), [t] + w_free[i], "mo_pe")
                old["out"] = [t_o]
                t_s = q.dve(lambda e, i=i: e.tensor_tensor(
                    scaled[:, :, :], ps_w[i][:, :].rearrange("p (j n) -> p j n", j=4),
                    gate_bc[:, b:b + 1, :].to_broadcast([P, 4, HID]), ALU.mult), [t_o] + old.get("res", []), "mo_dve")
                w_free[i] = [t_s]
                tile = b * TPB + n * 4
                old["res"] = [q.pool(lambda e, tile=tile: e.tensor_tensor(
                    x[:, tile:tile + 4, :], x[:, tile:tile + 4, :], scaled[:, :, :], ALU.add), [t_s], "mo_add")]

        for _ in prepare(0):
            pass
        for b in range(BATCH):
            ahead = prepare(b + 1) if b + 1 < BATCH else iter(())
            for _ in groups(b):
                next(ahead, None)
                next(ahead, None)
            for _ in ahead:
                pass
        q.run()


def program(nc, a, out):
    with ExitStack() as ctx:
        q = Queues(nc, ctx)

        def sb(name, shape, dt=F32):
            return ctx.enter_context(nc.sbuf_tensor(name, shape, dt))
        ident, ident_b = sb("ident", [P, P]), sb("ident_b", [P, P], BF16)
        eps = sb("eps", [P, 1])
        first_h = sb("first_h", [P, TOK])
        mod_t = [sb(f"mod_t{i}", [P, 6, BATCH]) for i in range(2)]
        gates = [[sb(f"gate0{w}", [P, BATCH, HID]) for w in range(2)]]

        slots_in, slots_out = ([nc.dram_tensor(f"{n}{k}", (E1 * CAPACITY, HID), F32, kind="Internal").ap()
                                for k in range(2)] for n in ("slots_in", "slots_out"))
        zeros = sb("zeros", [P, 1, HID])
        t_zero = q.pool(lambda e: e.memset(zeros[:, :, :], 0.0), (), "zeros")

        q.dma(ident[:, :], a["ident"], "in0")
        with nc.sbuf_tensor("x_in", [P, TILES, HID], F32) as x_in:
          t = q.dma(x_in[:, :, :], a["x"].rearrange("b (t p) n -> p (b t) n", p=P), "in0")
          q.dve(lambda e: e.tensor_copy(ident_b[:, :], ident[:, :]), [t], "c0")
          q.dve(lambda e: e.memset(eps[:, :], EPS), (), "c0")
          modulation(q, nc, 0, a["c_t0"], a["wmod0"], mod_t[0], gates[0])
          for k in range(2):
              t_zero = q.dma(slots_in[k].rearrange("(s p) n -> p s n", p=P), zeros[:, :, :].to_broadcast([P, E1 * CAPACITY // P, HID]),
                             "slots_zero", [t_zero])
          layernorm_t(q, nc, "0", x_in, mod_t[0], 0, 1, first_h, ident, eps)
        q.put("sync", lambda e: e.nop(), [t_zero])
        attention(q, nc, a, first_h, gates[0][0], ident, ident_b)
        x = first_h[:, :].rearrange("p (t n) -> p t n", n=HID)
        h_t = sb("h_t", [P, TOK])
        gates.append([sb(f"gate1{w}", [P, BATCH, HID]) for w in range(2)])
        rows_bc = [sb(f"rows_bc{w}", [P, BATCH, HID]) for w in range(2)]
        modulation(q, nc, 1, a["c_t1"], a["wmod1"], mod_t[1], gates[1], rows_bc)
        layernorm_t(q, nc, "1", x, mod_t[0], 3, 4, h_t, ident, eps)
        with ExitStack() as own:
            w1 = own.enter_context(nc.sbuf_tensor("w1_0", [P, E0, 4, F0 // 2], F32))
            w2 = own.enter_context(nc.sbuf_tensor("w2_0", [F0 // 2, E0, 2, HID], F32))
            gate = own.enter_context(nc.sbuf_tensor("gate_0", [P, E0], F32))
            iota = own.enter_context(nc.sbuf_tensor("iota_0", [P, E0], F32))
            q.dma(gate[:, :], a["gate_w"], "in1")
            t = q.dma(iota[:, :], a["iota"], "in1")
            src = a["w1_0"].rearrange("e h (s c f) -> h e c s f", s=2, c=2)
            for e_ in range(E0):
                for c in range(2):
                    t = q.dma(w1[:, e_, 2 * c:2 * c + 2, :], src[:, e_, c, :, :], "in1")
            t = q.dma(w2[:, :, :, :], a["w2_0"].rearrange("e (c f) n -> f e c n", c=2), "in1")
            combine = route(q, nc, "0", own, h_t, gate, t, iota, None, None)
            experts(q, nc, "0", x, h_t, combine, gates[0][1], lambda e, j: w1[:, e, j, :], lambda e, f: w2[:, e, f, :],
                    F0 // 2, True, None)

        layernorm_t(q, nc, "2", x, mod_t[1], 0, 1, h_t, ident, eps)
        selective_scan(q, nc, a, x, h_t, gates[1][0])
        with ExitStack() as own:
            h = own.enter_context(nc.sbuf_tensor("h_nat", [P, TILES, HID], F32))
            w2 = own.enter_context(nc.sbuf_tensor("w2_1", [P, E1, F1 // P, HID], F32))
            gate = own.enter_context(nc.sbuf_tensor("gate_1", [P, E1], F32))
            iota = own.enter_context(nc.sbuf_tensor("iota_1", [P, E1], F32))
            tri = own.enter_context(nc.sbuf_tensor("tri", [P, P], F32))
            bias = own.enter_context(nc.sbuf_tensor("bias", [P, 1, HID], F32))
            q.dma(gate[:, :], a["router_w"], "in2")
            q.dma(iota[:, :], a["iota"], "in2")
            q.dma(tri[:, :], a["tri"], "in2")
            q.dma(bias[:, :, :], a["bias"].to_broadcast([P, 1, HID]), "in2")
            t = q.dma(w2[:, :, :, :], a["w2_1"].rearrange("e (c f) n -> f e c n", f=P), "in2")
            layernorm_t(q, nc, "3", x, mod_t[1], 3, 4, h_t, ident, eps, rows_bc, h)
            slot, weight = route(q, nc, "1", own, h_t, gate, t, iota, tri, CAPACITY)
            capacity_experts(q, nc, x, h, slot, weight, a["w1_1"], w2, bias, gates[1][1], ident, slots_in, slots_out, out)


def constants():
    inv = (1.0 / THETA ** (np.arange(0, D, 2, dtype=np.float32) / np.float32(D))).astype(np.float32)
    freqs = np.arange(SEQ, dtype=np.float32)[:, None] * inv[None, :]
    emb = np.concatenate([freqs, freqs], axis=-1)[:, 0::2].astype(np.float32)
    cos, sin = np.cos(emb).T, np.sin(emb).T
    cos = np.repeat(cos, 2, axis=0)
    sin = np.repeat(sin, 2, axis=0) * np.tile(np.array([-1.0, 1.0], np.float32), D // 2)[:, None]
    i = np.arange(P)
    later = (i[None, :] > i[:, None]).astype(np.float32)
    fg = P // NST
    j = np.arange(HID // fg * P)
    w = np.arange(2 * P - fg)
    return {
        "cos": np.tile(cos, (2, 1)).astype(np.float32),
        "sin": np.tile(sin, (2, 1)).astype(np.float32),
        "masks": np.stack([later * np.float32(NEG), later.T * np.float32(NEG)], axis=1).astype(np.float32),
        "ident": np.eye(P, dtype=np.float32),
        "tri": later,
        "iota": np.tile(np.arange(E0, dtype=np.float32), (P, 1)),
        "sel": (i[:, None] == j[None, :] // NST).astype(np.float32),
        "fold": (w[None, :] == P - fg + i[:, None] // NST).astype(np.float32),
    }


def kernel(**inputs):
    import concourse.bacc as bacc
    from concourse.bass_utils import run_bass_kernel_spmd

    arr = {k: np.asarray(v) for k, v in inputs.items()}

    fields = {
        "x": arr["L0_attn_hidden_states"],
        "wq": arr["L0_attn_Wq"], "wk": arr["L0_attn_Wk"], "wv": arr["L0_attn_Wv"], "wo": arr["L0_attn_Wo"],
        "gate_w": arr["L0_ffn_gate_w"].T, "w1_0": arr["L0_ffn_w1"], "w2_0": arr["L0_ffn_w2"],
        "c_t0": arr["L0_c"].T, "wmod0": arr["L0_wmod"],
        "w_in": arr["L1_attn_W_in"], "conv_w": arr["L1_attn_conv_w"].reshape(HID, TAPS),
        "conv_b": arr["L1_attn_conv_b"].reshape(HID, 1), "w_xproj": arr["L1_attn_W_xproj"],
        "log_a": arr["L1_attn_log_A"].reshape(HID * NST // P, P).T,
        "d_param": arr["L1_attn_D_param"].reshape(HID, 1), "w_out": arr["L1_attn_W_out"],
        "router_w": arr["L1_ffn_router_w"], "w1_1": arr["L1_ffn_w1"], "w2_1": arr["L1_ffn_w2"],
        "bias": arr["L1_ffn_bias"].reshape(1, 1, HID),
        "c_t1": arr["L1_c"].T, "wmod1": arr["L1_wmod"],
        **constants(),
    }
    nc = bacc.Bacc("TRN2", target_bir_lowering=False, num_devices=1)
    arrays, aps = {}, {}
    for name, value in fields.items():
        value = np.ascontiguousarray(value)
        arrays[f"in_{name}"] = value
        aps[name] = nc.dram_tensor(f"in_{name}", value.shape, mybir.dt.from_np(value.dtype), kind="ExternalInput").ap()
    out = nc.dram_tensor("out_x", (BATCH, SEQ, HID), F32, kind="ExternalOutput").ap()
    program(nc, aps, out)
    result = run_bass_kernel_spmd(nc, [arrays], core_ids=[0])
    return result.results[0]["out_x"]
```

```python
from contextlib import ExitStack

import numpy as np

import concourse.bass as bass
from concourse import mybir

F32 = mybir.dt.float32
F32R = mybir.dt.float32r
I32 = mybir.dt.int32
BF16 = mybir.dt.bfloat16
ALU = mybir.AluOpType
ACT = mybir.ActivationFunctionType
AX = mybir.AxisListType.X

P = 128
BATCH, SEQ, HID = 4, 1024, 128
TOK = BATCH * SEQ
TILES = TOK // P
TPB = SEQ // P
BANK = 512
H, HKV, D = 16, 4, 64
E0, F0 = 8, 176
E1, F1 = 8, 512
NST = 16
TAPS = 4
CAPACITY = TOK // E1
THETA = 10000.0
EPS = 1e-5
NEG = -1e30


class Count:

    def __init__(self, sem):
        self.sem, self.value = sem, 0


class Queues:

    ENGINES = ("tensor", "vector", "scalar", "gpsimd", "sync")

    def __init__(self, nc, ctx):
        self.nc, self.ctx = nc, ctx
        self.todo = {e: [] for e in self.ENGINES}
        self.counts = {}
        self.met = {}

    def count(self, name):
        if name not in self.counts:
            self.counts[name] = Count(self.ctx.enter_context(self.nc.semaphore(name)))
        return self.counts[name]

    def put(self, engine, issue, wait=(), signal=None, step=1):
        todo = self.todo[engine]
        for name, value in wait:
            if self.met.get((engine, name), 0) < value:
                self.met[engine, name] = value
                todo.append((None, self.counts[name].sem, value))
        if signal is None:
            todo.append((issue, None, 0))
            return None
        count = self.count(signal)
        count.value += step
        todo.append((issue, count.sem, step))
        return signal, count.value

    def pe(self, issue, wait=(), signal=None):
        return self.put("tensor", issue, wait, signal)

    def dve(self, issue, wait=(), signal=None):
        return self.put("vector", issue, wait, signal)

    def act(self, issue, wait=(), signal=None):
        return self.put("scalar", issue, wait, signal)

    def pool(self, issue, wait=(), signal=None):
        return self.put("gpsimd", issue, wait, signal)

    def dma(self, out, in_, signal, wait=(), engine="sync"):
        if in_.dtype == F32R:
            out, in_ = out.bitcast(F32), in_.bitcast(F32)
        return self.put(engine, lambda e: e.dma_start(out, in_), wait, signal, 16)

    def run(self):
        todo, self.todo = self.todo, {e: [] for e in self.ENGINES}

        def emit(e, items):
            for issue, sem, n in items:
                if issue is None:
                    e.wait_ge(sem, n)
                elif sem is None:
                    issue(e)
                else:
                    issue(e).then_inc(sem, n)

        with self.nc.Block() as block:
            for name in self.ENGINES:
                if todo[name]:
                    def body(e, items=todo[name]):
                        emit(e, items)
                    {"tensor": block.tensor, "vector": block.vector, "scalar": block.scalar,
                     "gpsimd": block.gpsimd, "sync": block.sync}[name](body)


def modulation(q, nc, ctx, banks, layer, c_t, wmod, mod_t, gate_bc, rows_bc=None):
    ct = ctx.enter_context(nc.sbuf_tensor(f"ct{layer}", [P, BATCH], F32))
    sct = ctx.enter_context(nc.sbuf_tensor(f"sct{layer}", [P, BATCH], F32))
    wm = ctx.enter_context(nc.sbuf_tensor(f"wm{layer}", [P, 6 * HID], F32))
    sign = ctx.enter_context(nc.sbuf_tensor(f"sign{layer}", [P, BATCH, HID], F32))
    size = ctx.enter_context(nc.sbuf_tensor(f"size{layer}", [P, BATCH, HID], F32))
    ps_col = banks[0][:, 0:6 * BATCH].rearrange("p (j b) -> p j b", b=BATCH)
    ps_row = [bank.rearrange("p (b n) -> p b n", b=BATCH) for bank in banks[1:3]]
    in_c = q.dma(ct[:, :], c_t, "mod_in")
    in_w = q.dma(wm[:, :], wmod, "mod_in")
    got_c = q.act(lambda e: e.activation(sct[:, :], ct[:, :], ACT.Silu), [in_w], "mod_silu")
    for j in range(6):
        cols = q.pe(lambda e, j=j: e.matmul(ps_col[:, j, :], wm[:, j * HID:(j + 1) * HID], sct[:, :],
                                            start=True, stop=True), [got_c, in_w], "mod_pe")
    t = q.dve(lambda e: e.tensor_copy(mod_t[:, :, :], ps_col[:, :, :]), [cols], "mod_dve")
    for j in (1, 4):
        q.dve(lambda e, j=j: e.tensor_scalar(mod_t[:, j, :], ps_col[:, j, :], 1.0, None, ALU.add), [t], "mod_dve")
    for w, j in enumerate((2, 5)):
        for b in range(BATCH):
            rows = q.pe(lambda e, w=w, j=j, b=b: e.matmul(
                ps_row[w][:, b, :], sct[:, b:b + 1].to_broadcast([P, P]), wm[:, j * HID:(j + 1) * HID],
                start=True, stop=True), (), "mod_pe")
        t = q.dve(lambda e, w=w: e.tensor_scalar(sign[:, :, :], ps_row[w][:, :, :], 0.0, 2.0, ALU.is_ge, ALU.mult),
                  [rows, t], "mod_dve")
        t = q.dve(lambda e: e.tensor_scalar(sign[:, :, :], sign[:, :, :], -1.0, None, ALU.add), [t], "mod_dve")
        t = q.dve(lambda e, w=w: e.tensor_tensor(size[:, :, :], ps_row[w][:, :, :], sign[:, :, :], ALU.mult),
                  [t], "mod_dve")
        t = q.dve(lambda e, w=w: e.scalar_tensor_tensor(gate_bc[w][:, :, :], size[:, :, :], 0.25, sign[:, :, :],
                                                        ALU.max, ALU.mult), [t], "mod_dve")
    if rows_bc is not None:
        for w, j in enumerate((3, 4)):
            for b in range(BATCH):
                rows = q.pe(lambda e, w=w, j=j, b=b: e.matmul(
                    ps_row[w][:, b, :], sct[:, b:b + 1].to_broadcast([P, P]), wm[:, j * HID:(j + 1) * HID],
                    start=True, stop=True), [t], "mod_pe")
            q.dve(lambda e, w=w: e.tensor_scalar(rows_bc[w][:, :, :], ps_row[w][:, :, :], float(w), None, ALU.add),
                  [rows], "mod_dve")


def row_stats(q, x, stats, mv, tiles, wait):
    for i in tiles:
        t = q.dve(lambda e, i=i: e.bn_stats(stats[:, i, :], x[:, i, :]), wait, "ln_stats")
    for i in tiles:
        t = q.dve(lambda e, i=i: e.bn_aggr(mv[:, i, :], stats[:, i, :]), [t], "ln_stats")
    return t


def layernorm_t(q, nc, ctx, banks, name, x, mv, have, mod_t, shift, scale, h_t, ident, eps, rows_bc=None, h=None, use=None):
    std = ctx.enter_context(nc.sbuf_tensor(f"std{name}", [P, TILES], F32))
    rstd = ctx.enter_context(nc.sbuf_tensor(f"rstd{name}", [P, TILES], F32))
    nmr = ctx.enter_context(nc.sbuf_tensor(f"nmr{name}", [P, TILES], F32))
    xn = h if h is not None else ctx.enter_context(nc.sbuf_tensor(f"xn{name}", [P, TILES, HID], F32))
    ps, done = banks, []
    t_std = q.act(lambda e: e.activation(std[:, :], mv[:, :, 1], ACT.Sqrt, bias=eps[:, 0:1]), have, "ln_std")
    t = q.dve(lambda e: e.reciprocal(rstd[:, :], std[:, :]), [t_std], "ln_stats")
    t = q.dve(lambda e: e.scalar_tensor_tensor(nmr[:, :], mv[:, :, 0], -1.0, rstd[:, :], ALU.mult, ALU.mult),
              [t], "ln_stats")
    free = [None] * 4
    for i in range(TILES):
        on_pool = i % (2 if rows_bc is None else 4) == 0
        put, made = (q.pool, "ln_norm_pool") if on_pool else (q.dve, "ln_norm_dve")
        t_n = put(lambda e, i=i: e.tensor_scalar(xn[:, i, :], x[:, i, :], rstd[:, i:i + 1], nmr[:, i:i + 1],
                                                 ALU.mult, ALU.add), [t], made)
        n = i // 4
        if rows_bc is not None:
            for op, r in ((ALU.mult, 1), (ALU.add, 0)):
                t_n = put(lambda e, i=i, op=op, r=r: e.tensor_tensor(xn[:, i, :], xn[:, i, :], rows_bc[r][:, i // TPB, :], op),
                          [t_n], made)
        w = [t_n] + ([free[n % 4]] if i % 4 == 0 and free[n % 4] else [])
        t_t = q.pe(lambda e, i=i, n=n: e.transpose(ps[n % 4][:, (i % 4) * P:(i % 4 + 1) * P], xn[:, i, :],
                                                   ident[:, :]), w, "ln_tr")
        if i % 4 == 3:
            b = i // TPB
            cols = slice(n * BANK, (n + 1) * BANK)
            if rows_bc is not None:
                free[n % 4] = q.act(lambda e, n=n, cols=cols: e.activation(h_t[:, cols], ps[n % 4], ACT.Copy),
                                    [t_t], "ln_out_act")
            elif n % 2:
                free[n % 4] = q.dve(lambda e, n=n, b=b, cols=cols: e.tensor_scalar(
                    h_t[:, cols], ps[n % 4], mod_t[:, scale, b:b + 1], mod_t[:, shift, b:b + 1],
                    ALU.mult, ALU.add), [t_t], "ln_out_dve")
            else:
                free[n % 4] = q.act(lambda e, n=n, b=b, cols=cols: e.activation(
                    h_t[:, cols], ps[n % 4], ACT.Identity, bias=mod_t[:, shift, b:b + 1],
                    scale=mod_t[:, scale, b:b + 1]), [t_t], "ln_out_act")
            done.append(free[n % 4])
            if use is not None and n:
                use(n - 1, done[n - 1])
    if use is not None:
        use(TILES // 4 - 1, done[-1])
    return done


def attention_tensors(nc, ctx):
    def sb(name, shape):
        return ctx.enter_context(nc.sbuf_tensor(name, shape, F32))
    wq = sb("wq", [P, H * D])
    wk = sb("wk", [P, HKV, 2, D])
    wv = sb("wv", [P, HKV * D])
    wo = sb("wo", [P, H // 2, HID])
    cos, sin = sb("cos", [P, SEQ]), sb("sin", [P, SEQ])
    mask_f = sb("mask_f", [P, 2, P])
    return wq, wk, wv, wo, cos, sin, mask_f


def load_attention(q, a, tensors):
    wq, wk, wv, wo, cos, sin, mask_f = tensors
    loads = [(wk[:, :, i, :], a["wk"].rearrange("k (g d) -> k g d", g=HKV)) for i in range(2)]
    loads += [(wq[:, :], a["wq"]), (cos[:, :], a["cos"]), (sin[:, :], a["sin"]), (wv[:, :], a["wv"]),
              (mask_f[:, :, :], a["masks"]), (wo[:, :, :], a["wo"].rearrange("(c p) n -> p c n", p=P))]
    for out, in_ in loads:
        q.dma(out, in_, "attn_in")


def attention(q, nc, a, weights, h_t, gate_bc, ident, ident_b, stats, mv):
    G = H // HKV
    NPAIR = G // 2
    NQB = SEQ // P
    NCH = SEQ // BANK
    x = h_t[:, :].rearrange("p (t n) -> p t n", n=HID)
    with ExitStack() as ctx:
        def sb(name, shape, dt=F32):
            return ctx.enter_context(nc.sbuf_tensor(name, shape, dt))

        def pb(name, shape):
            return ctx.enter_context(nc.psum_tensor(name, shape, F32))

        wq, wk, wv, wo, cos, sin, mask_f = weights
        loaded = "attn_in", q.counts["attn_in"].value
        mask_b = sb("mask_b", [P, 2, P], BF16)
        x1 = [sb(f"x1_{i}", [P, G, SEQ], F32R) for i in range(2)]
        x2 = [sb(f"x2_{i}", [P, G, SEQ], F32R) for i in range(2)]
        k1 = [sb(f"k1_{i}", [P, SEQ], F32R) for i in range(3)]
        kl_dup = sb("kl_dup", [P, SEQ], F32R)
        k2 = [[sb(f"k2_{i}{j}", [P, SEQ], F32R) for j in range(2)] for i in range(3)]
        v = [sb(f"v_{i}", [P, NQB, D]) for i in range(2)]
        rot = [sb(f"rot{i}", [P, BANK]) for i in range(2)]
        other = [sb(f"other{i}", [P, BANK]) for i in range(2)]
        prob = [sb(f"prob{i}", [P, BANK]) for i in range(6)]
        attn_t = sb("attn_t", [P, H // 2, SEQ])
        neg_m = [sb(f"neg_m{i}", [P, G * NQB]) for i in range(2)]
        row_l = [sb(f"row_l{i}", [P, G * NQB]) for i in range(2)]
        ln_l = sb("ln_l", [P, G * NQB])
        neg_lse = sb("neg_lse", [P, G * NQB])
        lse_hi = [sb(f"lse_hi{i}", [G * NQB, P], F32R) for i in range(2)]
        lse_lo = [sb(f"lse_lo{i}", [G * NQB, P], F32R) for i in range(2)]
        scaled = sb("scaled", [P, 4, HID])

        RING = 7
        ring = pb("ring", [P, RING * BANK])
        ps_o = pb("ps_o", [P, BANK])

        t_mask = q.dve(lambda e: e.tensor_copy(mask_b[:, :, :], mask_f[:, :, :]), [loaded], "attn_const_dve")
        for i in range(2):
            for h in range(G):
                lo = 0 if h % 2 else D
                q.pool(lambda e, i=i, h=h, lo=lo: e.memset(x2[i][lo:lo + D, h, :].bitcast(F32), 0.0), (), "attn_const")
        for i in range(3):
            for odd in range(2):
                lo = 0 if odd else D
                t = q.pool(lambda e, i=i, odd=odd, lo=lo: e.memset(k2[i][odd][lo:lo + D, :].bitcast(F32), 0.0),
                           (), "attn_const")
                consts = q.pool(lambda e, i=i, odd=odd, lo=lo: e.memset(k2[i][odd][lo:lo + 2, :].bitcast(F32), 1.0),
                                [t], "attn_const")

        q.act(lambda e: e.preload_act_table_set("natural_log_exp_and_others"))
        ring_free = [[] for _ in range(RING)]
        state = {"at": 0, "o_free": [], "v_done": {}}

        def take(n):
            if state["at"] + n > RING:
                state["at"] = 0
            i = state["at"]
            state["at"] = (i + n) % RING
            assert None not in ring_free[i:i + n], "a bank is taken again before its release is known"
            free = sum(ring_free[i:i + n], [])
            ring_free[i:i + n] = [None] * n
            return range(i, i + n), ring[:, i * BANK:(i + n) * BANK], free

        def release(banks, tokens):
            for j in banks:
                ring_free[j] = tokens

        pv_done = {}
        x_free = {}
        a_done = {}
        ready_k, ready_x = {}, {}

        def project(g):
            b, kv = g // HKV, g % HKV
            buf = g % 2
            begun = []

            def begin_v():
                banks, ps, free = take(1)
                for n in range(NQB):
                    t0 = b * SEQ + n * P
                    t = q.pe(lambda e, n=n, t0=t0: e.matmul(ps[:, n * D:(n + 1) * D], h_t[:, t0:t0 + P],
                                                            wv[:, kv * D:(kv + 1) * D], start=True, stop=True),
                             [loaded] + free if n == 0 else (), "v_pe" if n == NQB - 1 else None)
                t = q.act(lambda e: e.activation(v[buf][:, :, :], ps.rearrange("p (n d) -> p n d", n=NQB), ACT.Copy),
                          [t] + pv_done.get(g - 2, []), "v_copy")
                release(banks, [t])
                state["v_done"][g] = t

            def begin(weights, c):
                n = state["rotations"] = state.get("rotations", -1) + 1
                i = n % 2
                banks, ps, free = take(1)
                cols = slice(b * SEQ + c * BANK, b * SEQ + (c + 1) * BANK)
                cc = slice(c * BANK, (c + 1) * BANK)
                t = q.pe(lambda e: e.matmul(ps, weights, h_t[:, cols], start=True, stop=True), [loaded] + free, "proj_pe")
                old = state.get(("split", i), [])
                q.dve(lambda e: e.tensor_tensor(rot[i][:, :], ps, cos[:, cc], ALU.mult), [t] + old, "rot_dve")
                t = q.dve(lambda e: e.stream_shuffle(other[i][:, :], ps, [k ^ 1 for k in range(32)]), (), "rot_dve")
                release(banks, [t])
                t = q.pool(lambda e: e.tensor_tensor(other[i][:, :], other[i][:, :], sin[:, cc], ALU.mult), [t], "rot_pool")
                t = q.pool(lambda e: e.tensor_tensor(rot[i][:, :], rot[i][:, :], other[i][:, :], ALU.add), [t], "rot_pool")
                return i, t

            def begin_k(c):
                begun.append((split_k, c, *begin(wk[:, kv, :, :], c)))

            def begin_q(pair, c):
                w0 = (kv * NPAIR + pair) * P
                begun.append((split_q(pair), c, *begin(wq[:, w0:w0 + P], c)))

            def split_k(c, i, t):
                cc = slice(c * BANK, (c + 1) * BANK)
                scale = float(D) ** -0.5
                t = q.dve(lambda e: e.tensor_scalar(k1[g % 3][:, cc], rot[i][:, :], scale, None, ALU.mult),
                          [t, consts] + x_free.get((g - 3, NPAIR - 1), []), "k_split")
                t = q.dve(lambda e: e.scalar_tensor_tensor(kl_dup[:, cc], rot[i][:, :], scale,
                                                           k1[g % 3][:, cc].bitcast(F32), ALU.mult, ALU.subtract),
                          [t] + a_done.get(g - 1, []), "k_split")
                for odd in range(2):
                    lo = D if odd else 0
                    t = q.dve(lambda e, odd=odd, lo=lo: e.tensor_copy(
                        k2[g % 3][odd][lo:lo + D, cc], kl_dup[lo:lo + D, cc].bitcast(F32)), [t], "k_split")
                ready_k[g] = [t]
                state["split", i] = [t]

            def split_q(pair):
                def run(c, i, t):
                    cc = slice(c * BANK, (c + 1) * BANK)
                    hi = []
                    for odd in range(2):
                        lo = D if odd else 0
                        h = 2 * pair + odd
                        t_hi = q.dve(lambda e, lo=lo, h=h: e.tensor_copy(x1[buf][lo:lo + D, h, cc], rot[i][lo:lo + D, :]),
                                     [t] + x_free.get((g - 2, pair), []), "q_split")
                        hi.append(t_hi)
                        ready_x[g, h, c] = q.dma(x2[buf][lo:lo + D, h, cc], x1[buf][lo:lo + D, h, cc],
                                                 f"x2_q{buf}", [t_hi, consts] + x_free.get((g - 2, pair), []))
                    for odd in range(2):
                        lo, far = (D, 0) if odd else (0, D)
                        h = 2 * pair + odd
                        t = q.dve(lambda e, lo=lo, far=far, h=h: e.tensor_tensor(
                            x1[buf][far:far + D, h, cc], rot[i][lo:lo + D, :], x1[buf][lo:lo + D, h, cc].bitcast(F32),
                            ALU.subtract), [hi[odd]], "q_split")
                        ready_x[g, h] = [t]
                    state["split", i] = [t]
                return run

            def split():
                f, c, i, t = begun.pop(0)
                f(c, i, t)

            def both(f, *args):
                def run():
                    f(*args)
                    if len(begun) > 1:
                        split()
                return run

            steps = [(3.7, both(begin_k, c)) for c in range(NCH)]
            steps += [(3.7, both(begin_q, pair, c)) for pair in range(NPAIR) for c in range(NCH)]
            steps += [(0.1, split), (1.0, begin_v)]
            return steps

        def first_pass(g):
            buf = g % 2
            units = []

            def unit(h, qb):
                def run():
                    n = (qb + 1) * P
                    banks, ps, free = take(-(-n // BANK))
                    col = h * NQB + qb
                    qs = slice(qb * P, (qb + 1) * P)
                    first = True
                    for c0 in range(0, n, BANK):
                        c1 = min(c0 + BANK, n)
                        diag = c1 == n
                        q.pe(lambda e, c0=c0, c1=c1: e.matmul(ps[:, c0:c1], x1[buf][:, h, qs], k1[g % 3][:, c0:c1],
                                                              start=True, stop=False),
                             (ready_k[g] + ready_x[g, h] + free) if first else ())
                        q.pe(lambda e, c0=c0, c1=c1, diag=diag: e.matmul(
                            ps[:, c0:c1], x1[buf][:, h, qs], kl_dup[:, c0:c1], start=False, stop=not diag))
                        first = False
                    t = q.pe(lambda e: e.matmul(ps[:, n - P:n], ident_b[:, :], mask_b[:, 0, :], start=False, stop=True),
                             [t_mask], "s1_pe")
                    t_m = q.dve(lambda e: e.tensor_reduce(neg_m[buf][:, col:col + 1], ps[:, 0:n], AX, ALU.max, negate=True),
                                [t] + state.get(("lse_free", g - 2), []), "s1_max")
                    a_done[g] = [t]
                    t_e = q.act(lambda e: e.activation(ps[:, 0:n], ps[:, 0:n], ACT.Exp, bias=neg_m[buf][:, col:col + 1],
                                                       accum_out=row_l[buf][:, col:col + 1]), [t_m], "s1_exp")
                    release(banks, [t_e])
                    state["last_exp"] = t_e
                return run

            for h in range(G):
                for qb in range(NQB):
                    units.append(((qb + 1) * 0.14 + 0.2, unit(h, qb)))
            units.append((0.1, lambda: finish_rows(g)))
            return units

        def finish_rows(g):
            buf = g % 2
            t = q.act(lambda e: e.activation(ln_l[:, :], row_l[buf][:, :], ACT.Ln), [state["last_exp"]] + state.get("lse_t", []),
                      "lse_ln")
            t = q.dve(lambda e: e.tensor_tensor(neg_lse[:, :], neg_m[buf][:, :], ln_l[:, :], ALU.subtract),
                      [t] + state.get("lse_pe", []), "lse_dve")
            state["lse_t"] = [t]
            state["lse_free", g] = [t]

        def place_rows(g):
            buf = g % 2
            banks, ps, free = take(1)
            t = q.pe(lambda e: e.transpose(ps[0:G * NQB, 0:P], neg_lse[:, :], ident[:, :]), state["lse_free", g] + free, "lse_pe")
            state["lse_pe"] = [t]
            old = state.get(("rows", buf), [])
            t_hi = q.dve(lambda e: e.tensor_copy(lse_hi[buf][:, :], ps[0:G * NQB, 0:P]), [t] + old, "lse_dve")
            t_lo = q.dve(lambda e: e.tensor_tensor(lse_lo[buf][:, :], ps[0:G * NQB, 0:P], lse_hi[buf][:, :].bitcast(F32),
                                                   ALU.subtract), [t_hi], "lse_dve")
            release(banks, [t_lo])
            for h in range(G):
                lo = 0 if h % 2 else D
                for k, part in enumerate((lse_hi, lse_lo)):
                    t = q.dma(x2[buf][lo + k:lo + k + 1, h, :], part[buf][h * NQB:(h + 1) * NQB, :], f"x2_rows{buf}",
                              [t_lo, consts] + x_free.get((g - 2, NPAIR - 1), []))
            state["rows", buf] = [t]

        def second_pass(g):
            b, kv = g // HKV, g % HKV
            buf = g % 2
            steps = []
            work = []
            for pair in range(NPAIR):
                for c in range(NCH):
                    nk = (c + 1) * BANK // P
                    for kb in range(nk):
                        off = max(kb * P - c * BANK, 0)
                        work.append((pair, c, kb, off, kb * P >= c * BANK, kb == nk - 1))
            pending = []

            def product():
                (pair, c, kb, off, _, last), t_p, n = pending.pop(0)
                w = BANK - off
                for odd in range(2):
                    wait = [t_p[odd]] + ([state["v_done"][g]] + state["o_free"] if kb == 0 else [])
                    t = q.pe(lambda e, odd=odd: e.matmul(
                        ps_o[odd * D:(odd + 1) * D, off:BANK], v[buf][:, kb, :],
                        prob[2 * (n % 3) + odd][:, 0:w], start=kb == 0, stop=last), wait, "pv_pe")
                state["prob", n % 3] = [t]
                pv_done[g] = [t]
                if last:
                    t = q.dve(lambda e: e.tensor_copy(attn_t[:, kv * NPAIR + pair, c * BANK:(c + 1) * BANK], ps_o[:, :]),
                              [t] + state.get(("wo_pe", c), []), "o_copy")
                    state["o_free"] = [t]
                    state["o_last"] = t

            def step(item):
                def run():
                    pair, c, kb, off, diag, last = item
                    w = BANK - off
                    q0 = c * BANK + off
                    n = state.setdefault("steps", 0)
                    state["steps"] += 1
                    tokens = []
                    for odd in range(2):
                        h = 2 * pair + odd
                        ks = slice(kb * P, (kb + 1) * P)
                        banks, ps, free = take(1)
                        wait = free + state["rows", buf] + [ready_x[g, G - 1, NCH - 1]]
                        q.pe(lambda e, odd=odd, h=h, ks=ks, ps=ps: e.matmul(
                            ps[:, 0:w], k1[g % 3][:, ks], x1[buf][:, h, q0:q0 + w], start=True, stop=False), wait)
                        t = q.pe(lambda e, odd=odd, h=h, ks=ks, ps=ps: e.matmul(
                            ps[:, 0:w], k2[g % 3][odd][:, ks], x2[buf][:, h, q0:q0 + w], start=False, stop=not diag),
                            (), None if diag else "s2_pe")
                        if diag:
                            t = q.pe(lambda e, ps=ps: e.matmul(ps[:, 0:P], ident_b[:, :], mask_b[:, 1, :],
                                                                 start=False, stop=True), (), "s2_pe")
                        t = q.act(lambda e, odd=odd, ps=ps: e.activation(prob[2 * (n % 3) + odd][:, 0:w], ps[:, 0:w],
                                                                  ACT.Exp), [t] + state.get(("prob", n % 3), []), "s2_exp")
                        release(banks, [t])
                        tokens.append(t)
                    x_free[g, pair] = [("s2_pe", q.counts["s2_pe"].value)]
                    if len(pending) == 2:
                        product()
                    pending.append((item, tokens, n))
                return run

            steps = [((BANK - item[3]) / BANK * 1.8 + 0.1, step(item)) for item in work]
            steps += [(0.3, lambda: product()), (0.3, lambda: product())]
            return steps

        def output(b, n):
            if n == 0:
                state["x_in"] = q.dma(x[:, b * TPB:(b + 1) * TPB, :], a["x"][b].rearrange("(t p) n -> p t n", p=P),
                                      f"x_again{b % 2}", [h_done[b]])
            x_in = state["x_in"]
            banks, ps, free = take(1)
            for c in range(H // 2):
                t = q.pe(lambda e, c=c: e.matmul(ps[:, 0:HID], attn_t[:, c, n * P:(n + 1) * P], wo[:, c, :],
                                                 start=c == 0, stop=c == H // 2 - 1),
                         [state["o_last"]] + free if c == 0 else (), "wo_pe" if c == H // 2 - 1 else None)
            state["wo_pe", n * P // BANK] = [t]
            i, tile = n % 4, b * TPB + n

            def add():
                t_s = q.dve(lambda e: e.tensor_tensor(scaled[:, i, :], ps[:, 0:HID], gate_bc[:, b, :], ALU.mult),
                            [t] + state.get(("res", i), []), "wo_scale")
                release(banks, [t_s])
                state["res", i] = [q.pool(lambda e: e.tensor_tensor(x[:, tile, :], x[:, tile, :], scaled[:, i, :], ALU.add),
                                          [t_s, x_in], "wo_add")]
                state["added"] = tile, state["res", i]
            state["add"] = add

        def output_stats():
            tile, wait = state.pop("added")
            row_stats(q, x, stats, mv, [tile], wait)

        h_done = {}
        groups = BATCH * HKV
        order = []

        def spread(steps, start):
            total = sum(cost for cost, _ in steps)
            used = 0.0
            for cost, step in steps:
                order.append((start + used / total, step))
                used += cost
            return total

        for g in range(groups):
            def projected(g=g):
                h_done[g // HKV] = ("proj_pe", q.counts["proj_pe"].value)
            turn = project(g)
            before_pair_1 = sum(cost for cost, _ in turn[:2 * NCH])
            total = spread(turn + [(0.0, projected)] + first_pass(g), g)
            lag = before_pair_1 / total
            spread(second_pass(g), g + 1 + lag - 1e-6)
            order.append((g + 1.04, lambda g=g: place_rows(g)))
            if g % HKV == HKV - 1:
                for n in range(TPB):
                    at = g + 2 + lag + (0.02 if n < TPB // 2 else 0.04) * n
                    order.append((at, lambda g=g, n=n: output(g // HKV, n)))
                    order.append((at + 0.016, lambda: state.pop("add")()))
                    order.append((at + 0.0199, output_stats))
        for _, step in sorted(order, key=lambda item: item[0]):
            step()
        q.run()


def scores(q, ps, h_t, gate, loaded):
    def chunk(n, done):
        for i in range(4 * n, 4 * n + 4):
            q.pe(lambda e, i=i: e.matmul(ps[:, i, :], h_t[:, i * P:(i + 1) * P], gate[:, :], start=True, stop=True),
                 [loaded, done], "route_pe")
    return chunk


def route(q, nc, name, ctx, ps, iota, loaded=None, tri=None, capacity=None, slotted=None):
    NE = 8
    shape = [P, TILES, NE]
    if capacity is None:
        combine = ctx.enter_context(nc.sbuf_tensor(f"combine{name}", shape, F32))
    else:
        slot = ctx.enter_context(nc.sbuf_tensor("slot", [P, 2, TILES], I32))
        weight = ctx.enter_context(nc.sbuf_tensor("weight", [P, 2, TILES], F32))
    def sb(n, s=shape):
        return ctx.enter_context(nc.sbuf_tensor(f"{n}{name}", s, F32))
    prob, tmp, cand = sb("r_prob"), sb("r_tmp"), sb("r_cand")
    mask = [sb("r_mask0"), sb("r_mask1")]
    top = [sb("r_top0", [P, TILES]), sb("r_top1", [P, TILES])]
    red = sb("r_red", [P, TILES])
    chain = [("route_pe", q.counts["route_pe"].value)]

    def dve(f):
        chain[0] = q.dve(f, [chain[0]], "route_dve")

    def over(v):
        return v[:, :].rearrange("p (t o) -> p t o", o=1).to_broadcast(shape)

    io = iota[:, :].rearrange("p (o n) -> p o n", o=1).to_broadcast(shape)
    dve(lambda e: e.tensor_reduce(red[:, :], ps[:, :, :], AX, ALU.max))
    dve(lambda e: e.tensor_tensor(tmp[:, :, :], ps[:, :, :], over(red), ALU.subtract))
    chain[0] = q.act(lambda e: e.activation(tmp[:, :, :], tmp[:, :, :], ACT.Exp), [chain[0]], "route_exp")
    dve(lambda e: e.tensor_reduce(red[:, :], tmp[:, :, :], AX, ALU.add))
    dve(lambda e: e.reciprocal(red[:, :], red[:, :]))
    dve(lambda e: e.tensor_tensor(prob[:, :, :], tmp[:, :, :], over(red), ALU.mult))
    dve(lambda e: e.tensor_copy(tmp[:, :, :], prob[:, :, :]))
    for k in range(2):
        m, tp = mask[k], top[k]
        dve(lambda e, tp=tp: e.tensor_reduce(tp[:, :], tmp[:, :, :], AX, ALU.max))
        dve(lambda e, tp=tp: e.tensor_tensor(cand[:, :, :], tmp[:, :, :], over(tp), ALU.is_equal))
        dve(lambda e: e.tensor_scalar(cand[:, :, :], cand[:, :, :], -float(NE), float(NE), ALU.mult, ALU.add))
        dve(lambda e: e.tensor_tensor(cand[:, :, :], cand[:, :, :], io, ALU.add))
        dve(lambda e: e.tensor_reduce(red[:, :], cand[:, :, :], AX, ALU.min))
        dve(lambda e, m=m: e.tensor_tensor(m[:, :, :], io, over(red), ALU.is_equal))
        if k == 0:
            dve(lambda e, m=m: e.scalar_tensor_tensor(tmp[:, :, :], m[:, :, :], -2.0, tmp[:, :, :], ALU.mult, ALU.add))
    if capacity is None:
        dve(lambda e: e.tensor_tensor(red[:, :], top[0][:, :], top[1][:, :], ALU.add))
        dve(lambda e: e.tensor_scalar(red[:, :], red[:, :], 1e-20, None, ALU.add))
        dve(lambda e: e.reciprocal(red[:, :], red[:, :]))
        for k in range(2):
            dve(lambda e, k=k: e.tensor_tensor(top[k][:, :], top[k][:, :], red[:, :], ALU.mult))
    else:
        ones = sb("r_ones", [P, P])
        t_one = q.pool(lambda e: e.memset(ones[:, :], 1.0), (), "route_pool")
        ps_both = ctx.enter_context(nc.psum_tensor(f"ps_rank{name}", [P, 2, TILES, NE], F32))
        ps_rank, ps_tot = ps_both[:, 0, :, :], ps_both[:, 1, :, :]
        run_a, run_b = sb("r_run_a"), sb("r_run_b")
        for k in range(2):
            t = q.pe(lambda e, k=k: e.matmul(ps_rank[:, :, :], tri[:, :], mask[k][:, :, :], start=True, stop=True),
                     [chain[0], t_one, loaded], "rank_pe")
            chain[0] = q.pe(lambda e, k=k: e.matmul(ps_tot[:, :, :], ones[:, :], mask[k][:, :, :], start=True, stop=True),
                            (), "rank_pe")
            dve(lambda e: e.memset(run_a[:, 0:1, :], 0.0))
            dve(lambda e: e.tensor_copy(run_a[:, 1:TILES, :], ps_tot[:, 0:TILES - 1, :]))
            src, dst = run_a, run_b
            s = 1
            while s < TILES:
                dve(lambda e, s=s, src=src, dst=dst: e.tensor_copy(dst[:, 0:s, :], src[:, 0:s, :]))
                dve(lambda e, s=s, src=src, dst=dst: e.tensor_tensor(
                    dst[:, s:TILES, :], src[:, s:TILES, :], src[:, 0:TILES - s, :], ALU.add))
                src, dst = dst, src
                s *= 2
            dve(lambda e, src=src: e.tensor_tensor(src[:, :, :], src[:, :, :], ps_rank[:, :, :], ALU.add))
            late = 2.0 * NE * capacity
            dve(lambda e, src=src: e.tensor_scalar(tmp[:, :, :], src[:, :, :], float(capacity), late, ALU.is_ge, ALU.mult))
            dve(lambda e, src=src: e.tensor_tensor(tmp[:, :, :], tmp[:, :, :], src[:, :, :], ALU.add))
            dve(lambda e: e.scalar_tensor_tensor(tmp[:, :, :], io, float(capacity), tmp[:, :, :], ALU.mult, ALU.add))
            dve(lambda e, k=k: e.tensor_tensor(tmp[:, :, :], tmp[:, :, :], mask[k][:, :, :], ALU.mult))
            dve(lambda e: e.tensor_reduce(red[:, :], tmp[:, :, :], AX, ALU.add))
            dve(lambda e, k=k: e.tensor_copy(slot[:, k, :], red[:, :]))
            slotted(slot, k, chain[0])
            dve(lambda e, k=k: e.tensor_copy(weight[:, k, :], top[k][:, :]))
        return slot, weight
    dve(lambda e: e.tensor_tensor(tmp[:, :, :], mask[0][:, :, :], over(top[0]), ALU.mult))
    dve(lambda e: e.tensor_tensor(cand[:, :, :], mask[1][:, :, :], over(top[1]), ALU.mult))
    dve(lambda e: e.tensor_tensor(combine[:, :, :], tmp[:, :, :], cand[:, :, :], ALU.add))
    return combine, chain[0]


def split_parts(q, name, src, hi, lo, width, wait=(), done=()):
    tokens = []
    for c in range(0, src.shape[1], width):
        cc = slice(c, c + width)
        t = q.act(lambda e, cc=cc: e.activation(hi[:, cc], src[:, cc], ACT.Copy),
                  list(wait) + list(done[c // width:c // width + 1]), f"{name}_hi")
        tokens.append(q.pool(lambda e, cc=cc: e.tensor_tensor(lo[:, cc], src[:, cc], hi[:, cc].bitcast(F32), ALU.subtract),
                             [t], f"{name}_lo"))
    return tokens


def experts(q, nc, banks, x, h, weights, combine, picked, rows, gate_bc, ident, stats, mv):
    (h_hi, h_lo, h_done), (w_hi, w_lo, w_done), w2 = h, weights[0], weights[1]
    NCHUNK = TOK // BANK
    NC = E0 * F0 // P
    with ExitStack() as ctx:
        def sb(n, s, dt=F32):
            return ctx.enter_context(nc.sbuf_tensor(f"e_{n}", s, dt))
        comb2 = sb("comb2", [P, TILES, 2, E0], F32R)
        comb_t = [sb(f"comb_t{i}", [P, BANK], F32R) for i in range(2)]
        silu = [sb(f"silu{i}", [P, BANK]) for i in range(2)]
        both = [sb(f"both{i}", [P, BANK]) for i in range(2)]
        hid = [sb(f"hid{i}", [P, BANK]) for i in range(4)]
        scaled = [sb(f"e_scaled{i}", [P, 4, HID]) for i in range(2)]
        ps_up = [banks[:, 2 * i:2 * i + 2, :] for i in range(2)]
        ps_c = [banks[:, 4 + i, :] for i in range(2)]
        ps_dn = banks[:, 6, :].rearrange("p (j n) -> p j n", n=HID)
        free = {}
        comb_done = {}
        turns = [0]

        for i in range(2):
            t_zero = q.pool(lambda e, i=i: e.memset(comb_t[i][:, :].bitcast(F32), 0.0), (), "e_zero")
        t = q.dve(lambda e: e.tensor_copy(comb2[:, :, 0, :], combine[:, :, :]), [picked], "e_comb")
        t_comb = q.dve(lambda e: e.tensor_tensor(comb2[:, :, 1, :], combine[:, :, :], comb2[:, :, 0, :].bitcast(F32),
                                                 ALU.subtract), [t], "e_comb")

        def spare():
            i = turns[0] % 2
            turns[0] += 1
            return i, free.get(("c", i), [])

        def transpose_combine(n):
            i, wait = spare()
            for j in range(4):
                t = q.pe(lambda e, j=j: e.transpose(ps_c[i][0:2 * E0, j * P:(j + 1) * P],
                                                    comb2[:, 4 * n + j, :, :].rearrange("p s e -> p (s e)").bitcast(F32),
                                                    ident[:, :]), [t_comb] + wait if j == 0 else (), "e_tr" if j == 3 else None)
            t = q.act(lambda e: e.activation(comb_t[n % 2][0:2 * E0, :], ps_c[i][0:2 * E0, :], ACT.Copy),
                      [t, t_zero] + free.get(("comb_t", n % 2), []), "e_comb_t")
            free["c", i] = [t]
            comb_done[n] = t

        def up_stage(k):
            n, c = divmod(k, NC)
            cols, ps = slice(n * BANK, (n + 1) * BANK), ps_up[k % 2]
            for m in range(2):
                f = slice(m * E0 * F0 + c * P, m * E0 * F0 + (c + 1) * P)
                for p, (w, xx) in enumerate(((w_hi, h_hi), (w_hi, h_lo), (w_lo, h_hi))):
                    t = q.pe(lambda e, m=m, f=f, w=w, xx=xx, p=p: e.matmul(ps[:, m, :], w[:, f], xx[:, cols],
                                                                           start=p == 0, stop=p == 2),
                             w_done + h_done[:n + 1] + free.get(("up", k % 2), []) if m == 0 and p == 0 else (),
                             f"e_up{m}" if p == 2 else None)
                if m == 0:
                    t_s = q.act(lambda e: e.activation(silu[k % 2][:, :], ps[:, 0, :], ACT.Silu),
                                [t] + free.get(("silu", k % 2), []), "e_silu")
            i, wait = spare()
            t_c = q.pe(lambda e: e.matmul(ps_c[i], rows[:, c * P:(c + 1) * P], comb_t[n % 2][:, :], start=True, stop=True),
                       [comb_done[n]] + wait, "e_rep")
            free["comb_t", n % 2] = [t_c]
            t = q.dve(lambda e: e.tensor_tensor(both[k % 2][:, :], silu[k % 2][:, :], ps[:, 1, :], ALU.mult), [t, t_s], "e_both")
            free["silu", k % 2] = free["up", k % 2] = [t]
            t = q.dve(lambda e: e.tensor_tensor(hid[k % 4][:, :], both[k % 2][:, :], ps_c[i], ALU.mult),
                      [t, t_c] + free.get(("hid", k % 4), []), "e_hid")
            free["c", i] = [t]
            return t

        def down_stage(k, made):
            n, c = divmod(k, NC)
            for i in range(4):
                t = q.pe(lambda e, i=i: e.matmul(ps_dn[:, i, :], hid[k % 4][:, i * P:(i + 1) * P], w2[:, c, :],
                                                 start=c == 0 and i == 0, stop=c == NC - 1 and i == 3),
                         [made] + (free.get("dn", []) if c == 0 else []) if i == 0 else (), "e_dn" if i == 3 else None)
            free["hid", k % 4] = [t]
            if c == NC - 1:
                b, sc = n * 4 // TPB, scaled[n % 2]
                t = q.dve(lambda e: e.tensor_tensor(sc[:, :, :], ps_dn[:, :, :], gate_bc[:, b:b + 1, :].to_broadcast([P, 4, HID]),
                                                    ALU.mult), [t] + free.get(("scaled", n % 2), []), "e_scale")
                free["dn"] = [t]
                free["scaled", n % 2] = [q.pool(lambda e: e.tensor_tensor(
                    x[:, 4 * n:4 * n + 4, :], x[:, 4 * n:4 * n + 4, :], sc[:, :, :], ALU.add), [t], "e_add")]

        transpose_combine(0)
        made = []
        LAG = 2
        for k in range(NCHUNK * NC):
            made.append(up_stage(k))
            if k >= LAG:
                down_stage(k - LAG, made[k - LAG])
            if k % NC == LAG + 1 and k > NC:
                n = k // NC - 1
                row_stats(q, x, stats, mv, range(4 * n, 4 * n + 4), free["scaled", n % 2])
            if k % NC == NC // 2 and k // NC + 1 < NCHUNK:
                transpose_combine(k // NC + 1)
        for k in range(NCHUNK * NC - LAG, NCHUNK * NC):
            down_stage(k, made[k])
        row_stats(q, x, stats, mv, range(TILES - 4, TILES), free["scaled", (NCHUNK - 1) % 2])
        q.run()


def scatter(q, h, slot, k, slots_in, picked):
    for i in range(TILES):
        t = q.put("gpsimd", lambda e, i=i: e.indirect_dma_start(
            slots_in[k][:, :], bass.IndirectOffsetOnAxis(ap=slot[:, k, i:i + 1], axis=0), h[:, i, :], None,
            bounds_check=E1 * CAPACITY - 1, oob_is_err=False), [picked], f"scatter{k}", 16)
    return t


def capacity_experts(q, nc, loaded, x, slot, weight, scattered, w1, w2, bias_bc, gate_bc, ident, slots_in, slots_out, out):
    NE, NF = E1, F1 // P
    NSLOT = NE * CAPACITY
    SB = CAPACITY // P
    NBUF = 3
    w_hi, w_lo, w_done = w1
    with ExitStack() as ctx:
        def sb(n, s, dt=F32):
            return ctx.enter_context(nc.sbuf_tensor(f"c_{n}", s, dt))
        got = sb("got", [P, 2, TILES, HID])
        rows = [sb(f"rows{i}", [P, SB, HID]) for i in range(NBUF)]
        xt_hi, xt_lo = ([sb(f"{n}{i}", [P, CAPACITY], F32R) for i in range(2)] for n in ("xt_hi", "xt_lo"))
        hid = [sb(f"hid{i}", [P, NF, CAPACITY]) for i in range(2)]
        res = [sb(f"res{i}", [P, SB, HID]) for i in range(2)]
        ps_up = [ctx.enter_context(nc.psum_tensor(f"c_up{i}", [P, 2, BANK], F32)) for i in range(2)]
        ps_tr = ctx.enter_context(nc.psum_tensor("c_tr", [P, BANK], F32))
        ps_dn = ctx.enter_context(nc.psum_tensor("c_dn", [P, SB, HID], F32))

        def gather(k, written):
            for i in range(TILES):
                q.put("gpsimd", lambda e, i=i, k=k: e.indirect_dma_start(
                    got[:, k, i, :], None, slots_out[k][:, :], bass.IndirectOffsetOnAxis(ap=slot[:, k, i:i + 1], axis=0),
                    bounds_check=NSLOT - 1, oob_is_err=False), written + zeroed, f"gather{k}_{i // 4}", 16)

        zeroed = [q.dve(lambda e: e.memset(got[:, :, :, :], 0.0), (), "got_zero")]
        free = {}
        split, made = {}, {}

        def fetch(n):
            k, e_, i = n // NE, n % NE, n % NBUF
            split[n] = q.dma(rows[i][:, :, :], slots_in[k][e_ * CAPACITY:(e_ + 1) * CAPACITY, :].rearrange("(s p) n -> p s n", p=P),
                             f"c_rows{i}", [scattered[k]] + free.get(("rows", i), []))

        def begin(n):
            r, i = n % NBUF, n % 2
            for j in range(SB):
                t_t = q.pe(lambda e, j=j: e.transpose(ps_tr[:, j * P:(j + 1) * P], rows[r][:, j, :], ident[:, :]),
                           [split[n]] + free.get("tr", []) if j == 0 else (), "c_tr" if j == SB - 1 else None)
            free["rows", r] = [t_t]
            t = q.dve(lambda e: e.tensor_copy(xt_hi[i][:, :], ps_tr[:, :]), [t_t] + free.get(("up", i), []), "c_xsplit")
            t = q.dve(lambda e: e.tensor_tensor(xt_lo[i][:, :], ps_tr[:, :], xt_hi[i][:, :].bitcast(F32), ALU.subtract),
                      [t], "c_xsplit")
            free["tr"] = [t]
            split[n] = t

        def up(n):
            e_, i = n % NE, n % 2
            for j in range(NF // 2):
                for m in range(2):
                    f = slice(e_ * F1 + (2 * j + m) * P, e_ * F1 + (2 * j + m + 1) * P)
                    for p, (w, xx) in enumerate(((w_hi, xt_hi), (w_hi, xt_lo), (w_lo, xt_hi))):
                        t_u = q.pe(lambda e, j=j, m=m, f=f, w=w, xx=xx, p=p: e.matmul(
                            ps_up[j][:, m, :], w[:, f], xx[i][:, :], start=p == 0, stop=p == 2),
                            [split[n], w_done[e_]] + free.get(("ps", j), []) if m == 0 and p == 0 else (),
                            "c_up" if m == 1 and p == 2 else None)
                t_g = q.act(lambda e, j=j: e.activation(hid[i][:, 2 * j:2 * j + 2, :], ps_up[j][:, :, :], ACT.Gelu_apprx_tanh),
                            [t_u] + free.get(("hid", i), []), "c_gelu")
                free["ps", j] = [t_g]
            free["up", i] = [t_u]
            made[n] = t_g

        def down(n):
            e_, i = n % NE, n % 2
            for j in range(SB):
                for f in range(NF):
                    t = q.pe(lambda e, j=j, f=f: e.matmul(ps_dn[:, j, :], hid[i][:, f, j * P:(j + 1) * P], w2[:, e_, f, :],
                                                          start=f == 0, stop=f == NF - 1),
                             [made[n], loaded] + free.get("dn", []) if j == 0 and f == 0 else (),
                             "c_dn" if j == SB - 1 and f == NF - 1 else None)
            free["hid", i] = [t]
            t = q.act(lambda e: e.activation(res[i][:, :, :], ps_dn[:, :, :], ACT.Copy), [t] + free.get(("res", i), []), "c_res")
            free["dn"] = [t]
            t = q.dma(slots_out[n // NE][e_ * CAPACITY:(e_ + 1) * CAPACITY, :].rearrange("(s p) n -> p s n", p=P), res[i][:, :, :],
                      f"c_out{i}", [t])
            free["res", i] = [t]

        def results():
            return free["res", 0] + free["res", 1]

        def wide(v):
            return v.rearrange("p (t o) -> p t o", o=1).to_broadcast([P, 4, HID])

        first = {}

        def mix_first(m):
            ts = slice(4 * m, 4 * m + 4)
            t = q.dve(lambda e: e.tensor_tensor(got[:, 0, ts, :], got[:, 0, ts, :], wide(weight[:, 0, ts]), ALU.mult),
                      [(f"gather0_{m}", 4 * 16)], "c_mix")
            first[m] = q.dve(lambda e: e.tensor_tensor(got[:, 0, ts, :], got[:, 0, ts, :],
                                                       bias_bc[:, :, :].to_broadcast([P, 4, HID]), ALU.add), [t, loaded], "c_mix")

        def mix(m):
            ts, b = slice(4 * m, 4 * m + 4), m * 4 // TPB
            t = q.dve(lambda e: e.tensor_tensor(got[:, 1, ts, :], got[:, 1, ts, :], wide(weight[:, 1, ts]), ALU.mult),
                      [(f"gather1_{m}", 4 * 16)], "c_mix")
            t = q.dve(lambda e: e.tensor_tensor(got[:, 1, ts, :], got[:, 1, ts, :], got[:, 0, ts, :], ALU.add), [t, first[m]], "c_mix")
            t = q.dve(lambda e: e.tensor_tensor(got[:, 1, ts, :], got[:, 1, ts, :], gate_bc[:, b:b + 1, :].to_broadcast([P, 4, HID]),
                                                ALU.mult), [t], "c_mix")
            t = q.dve(lambda e: e.tensor_tensor(x[:, ts, :], x[:, ts, :], got[:, 1, ts, :], ALU.add), [t], "c_mix")
            q.dma(out[b, (m * 4 % TPB) * P:(m * 4 % TPB + 4) * P, :].rearrange("(t p) n -> p t n", p=P), x[:, ts, :], "out", [t])

        for n in range(NBUF - 1):
            fetch(n)
        begin(0)
        for n in range(2 * NE):
            if n + NBUF - 1 < 2 * NE:
                fetch(n + NBUF - 1)
            if n + 1 < 2 * NE:
                begin(n + 1)
            up(n)
            if n:
                down(n - 1)
            if n == NE:
                gather(0, results())
            if n > NE + NE // 2:
                for m in range(2 * (n - NE - NE // 2 - 1), 2 * (n - NE - NE // 2)):
                    mix_first(m)
        down(2 * NE - 1)
        for m in range(NE - 2, TILES // 4):
            mix_first(m)
        gather(1, results())
        for m in range(TILES // 4):
            mix(m)
        q.put("sync", lambda e: e.nop(), [("out", q.counts["out"].value)])
        q.run()


def selective_scan(q, nc, a, w_in, x, h_t, gate_bc, stats, mv):
    FG = P // NST
    NG = HID // FG
    with ExitStack() as ctx:
        def sb(n, s=(P, SEQ), dt=F32):
            return ctx.enter_context(nc.sbuf_tensor(f"m_{n}", list(s), dt))

        def pb(n, s):
            return ctx.enter_context(nc.psum_tensor(f"m_{n}", s, F32))
        w_x, w_out = sb("w_x", (P, 2 * NST + 1)), sb("w_out", (P, HID))
        w_b, w_c, w_d = sb("w_b", (P, FG, NST)), sb("w_c", (P, FG, NST)), sb("w_d", (P, P))
        cw, cb, dp = sb("cw", (P, TAPS)), sb("cb", (P, 1)), sb("dp", (P, 1))
        a_neg, log_a = sb("a_neg", (P, NG)), sb("log_a", (P, NG))
        sel_in, sel = sb("sel_in", (P, NG * P // 2)), sb("sel", (P, NG * P), F32R)
        fold = sb("fold", (P, 2 * P - FG))
        xm = [sb(f"xm{i}", (P, SEQ + TAPS - 1)) for i in range(2)]
        z = [sb(f"z{i}") for i in range(2)]
        u, conv = [sb(f"u{i}") for i in range(2)], sb("conv")
        raw, soft, delta, du = sb("raw"), sb("soft"), [sb(f"delta{i}") for i in range(2)], sb("du")
        du_hi, du_lo = ([sb(f"{n}{i}", (P, SEQ), F32R) for i in range(2)] for n in ("du_hi", "du_lo"))
        brep, crep = [sb(f"brep{i}") for i in range(2)], [sb(f"crep{i}") for i in range(2)]
        da, bu, st, hc = ([sb(f"{n}{i}") for i in range(3)] for n in ("da", "bu", "st", "hc"))
        y = sb("y")
        scaled = sb("scaled", (P, 4, HID))
        ps_y = [pb(f"ps_y{i}", [P, BANK]) for i in range(2)]
        ps_x = [pb(f"ps_x{i}", [P, 2 * BANK]) for i in range(2)]
        ps_w = [pb(f"ps_w{i}", [P, BANK]) for i in range(2)]

        for out, in_ in [(w_x[:, :], a["w_xproj"]), (w_out[:, :], a["w_out"]),
                         (cw[:, :], a["conv_w"]), (cb[:, :], a["conv_b"]), (dp[:, :], a["d_param"]),
                         (log_a[:, :], a["log_a"]), (fold[:, :], a["fold"])]:
            loaded = q.dma(out, in_, "mamba_in")
        half = NG * P // 2
        sel_done = []
        for i in range(2):
            sel_done.append(q.dma((sel_in, y)[i][:, :], a["sel"][:, i * half:(i + 1) * half], f"sel_in{i}"))
        q.dve(lambda e: e.tensor_copy(w_b[:, :, :], w_x[:, 0:NST].rearrange("p (o n) -> p o n", o=1).to_broadcast([P, FG, NST])),
              [loaded], "m_const")
        q.dve(lambda e: e.tensor_copy(w_c[:, :, :], w_x[:, NST:2 * NST].rearrange("p (o n) -> p o n", o=1).to_broadcast([P, FG, NST])),
              (), "m_const")
        reps = q.dve(lambda e: e.tensor_copy(w_d[:, :], w_x[:, 2 * NST:2 * NST + 1].to_broadcast([P, P])), (), "m_const")
        t = q.act(lambda e: e.activation(a_neg[:, :], log_a[:, :], ACT.Exp), [loaded], "m_a")
        t_a = q.dve(lambda e: e.tensor_scalar(a_neg[:, :], a_neg[:, :], -1.0, None, ALU.mult), [t], "m_const")
        for i in range(2):
            t_pad = q.pool(lambda e, i=i: e.memset(xm[i][:, 0:TAPS - 1], 0.0), (), "m_pad")

        w_free = [[], []]
        nw = [0]

        def product(lhs, cols, wait):
            i = nw[0] % 2
            nw[0] += 1
            return i, q.pe(lambda e, i=i: e.matmul(ps_w[i][:, :], lhs, cols, start=True, stop=True),
                           wait + w_free[i], "mw_pe")

        old = {}

        def prepare(b):
            k = b % 2
            for c in range(SEQ // BANK):
                cols = h_t[:, b * SEQ + c * BANK:b * SEQ + (c + 1) * BANK]
                i, t = product(w_in[:, 0:HID], cols, [])
                t_x = q.act(lambda e, i=i, c=c: e.activation(xm[k][:, TAPS - 1 + c * BANK:TAPS - 1 + (c + 1) * BANK], ps_w[i][:, :],
                                                             ACT.Copy), [t, t_pad] + old.get(("conv", b - 2), []), "m_act")
                w_free[i] = [t_x]
                yield
            t = q.dve(lambda e: e.tensor_scalar(conv[:, :], xm[k][:, 0:SEQ], cw[:, 0:1], cb[:, 0:1], ALU.mult, ALU.add),
                      [t_x] + old.get(("u", b - 1), []), "m_conv")
            for j in range(1, TAPS):
                t = q.dve(lambda e, j=j: e.scalar_tensor_tensor(conv[:, :], xm[k][:, j:j + SEQ], cw[:, j:j + 1], conv[:, :],
                                                                ALU.mult, ALU.add), [t], "m_conv")
                yield
            old["conv", b] = [t]
            t_u = q.act(lambda e: e.activation(u[k][:, :], conv[:, :], ACT.Silu), [t] + old.get(("y", b - 2), []), "m_act")
            for c in range(SEQ // BANK):
                cols = h_t[:, b * SEQ + c * BANK:b * SEQ + (c + 1) * BANK]
                i, t_z = product(w_in[:, HID:2 * HID], cols, [])
                t_z = q.act(lambda e, i=i, c=c: e.activation(z[k][:, c * BANK:(c + 1) * BANK], ps_w[i][:, :], ACT.Silu),
                            [t_z] + old.get(("y", b - 2), []), "m_act")
                w_free[i] = [t_z]
            old["u", b] = [t_u]
            q.act(lambda e: e.preload_act_table_set("natural_log_exp_and_others"))
            yield
            for c in range(SEQ // BANK):
                i, t = product(w_d[:, :], u[k][:, c * BANK:(c + 1) * BANK], [])
                t = q.act(lambda e, i=i, c=c: e.activation(raw[:, c * BANK:(c + 1) * BANK], ps_w[i][:, :], ACT.Copy),
                          [t] + old.get(("du", b - 1), []), "m_act")
                w_free[i] = [t]
            yield
            t = q.act(lambda e: e.activation(soft[:, :], raw[:, :], ACT.Abs), [t], "m_act")
            t = q.act(lambda e: e.activation(soft[:, :], soft[:, :], ACT.Exp, scale=-1.0), [t], "m_act")
            t = q.act(lambda e: e.activation(soft[:, :], soft[:, :], ACT.Ln, bias=1.0), [t], "m_act")
            yield
            for dst, w in ((brep, w_b), (crep, w_c)):
                for c in range(SEQ // BANK):
                    i, t_b = product(w[:, :, :], u[k][:, c * BANK:(c + 1) * BANK], [t_u, reps])
                    t_b = q.act(lambda e, i=i, c=c, dst=dst: e.activation(dst[k][:, c * BANK:(c + 1) * BANK], ps_w[i][:, :], ACT.Copy),
                              [t_b] + old.get(("scan", b - 2), []), "m_act")
                    w_free[i] = [t_b]
                    yield
            old["bc", b] = [t_b]
            t_d = q.dve(lambda e: e.scalar_tensor_tensor(delta[k][:, :], raw[:, :], 0.0, soft[:, :], ALU.max, ALU.add),
                        [t] + old.get(("scan", b - 2), []), "m_delta")
            yield
            t = q.dve(lambda e: e.tensor_tensor(du[:, :], delta[k][:, :], u[k][:, :], ALU.mult),
                      [t_d, t_u] + old.get(("du", b - 1), []), "m_delta")
            t = q.dve(lambda e: e.tensor_copy(du_hi[k][:, :], du[:, :]), [t] + old.get(("scan", b - 2), []), "m_delta")
            t = q.dve(lambda e: e.tensor_tensor(du_lo[k][:, :], du[:, :], du_hi[k][:, :].bitcast(F32), ALU.subtract), [t], "m_delta")
            old["du", b] = [t]
            yield

        pend = []
        later = []
        added = []

        def gather(b, g, r, t_hc):
            for c in range(SEQ // BANK):
                w0 = P - FG - FG * g
                t = q.pe(lambda e, c=c: e.matmul(ps_y[c][:, :], fold[:, w0:w0 + P], hc[r][:, c * BANK:(c + 1) * BANK],
                                                 start=g == 0, stop=g == NG - 1),
                         [t_hc] + (old.get(("ysum", b - 1), []) if g == 0 else []), "my_pe")
            old["hc", r] = [t]
            if g == NG - 1:
                k = b % 2
                old["scan", b] = [t]
                for c in range(SEQ // BANK):
                    cc = slice(c * BANK, (c + 1) * BANK)
                    t1 = q.dve(lambda e, c=c, cc=cc: e.scalar_tensor_tensor(y[:, cc], u[k][:, cc], dp[:, 0:1], ps_y[c][:, :],
                                                                            ALU.mult, ALU.add), [t] + old.get("out", []), "m_y")
                old["ysum", b] = [t1]
                old["y", b] = [q.dve(lambda e: e.tensor_tensor(y[:, :], y[:, :], z[k][:, :], ALU.mult), [t1], "m_y")]
                later.extend((b, n) for n in range(TPB // 4))

        def output(b, n):
            i = nw[0] % 2
            nw[0] += 1
            for j in range(4):
                blk = slice((n * 4 + j) * P, (n * 4 + j + 1) * P)
                t_o = q.pe(lambda e, j=j, blk=blk: e.matmul(ps_w[i][:, j * HID:(j + 1) * HID], y[:, blk], w_out[:, :],
                                                            start=True, stop=True), old["y", b] + w_free[i], "mo_pe")
            old["out"] = [t_o]
            t_s = q.dve(lambda e: e.tensor_tensor(
                scaled[:, :, :], ps_w[i][:, :].rearrange("p (j n) -> p j n", j=4),
                gate_bc[:, b:b + 1, :].to_broadcast([P, 4, HID]), ALU.mult), [t_o] + old.get("res", []), "mo_dve")
            w_free[i] = [t_s]
            tile = b * TPB + n * 4
            old["res"] = [q.pool(lambda e: e.tensor_tensor(
                x[:, tile:tile + 4, :], x[:, tile:tile + 4, :], scaled[:, :, :], ALU.add), [t_s], "mo_add")]
            added.append((range(tile, tile + 4), old["res"]))

        def group(b, g):
            k, n = b % 2, b * NG + g
            i, r = n % 2, n % 3
            for c in range(SEQ // BANK):
                for part in (du_hi, du_lo):
                    t = q.pe(lambda e, c=c, part=part: e.matmul(
                        ps_x[i][:, c * BANK:(c + 1) * BANK], sel[:, g * P:(g + 1) * P],
                        part[k][:, c * BANK:(c + 1) * BANK], start=part is du_hi, stop=part is du_lo),
                        [t_sel] + old["du", b] + old.get(("px", i), []), "mx_pe")
            t_da = q.act(lambda e: e.activation(da[r][:, :], delta[k][:, :], ACT.Exp, scale=a_neg[:, g:g + 1]),
                         [t_a] + old["du", b] + old.get(("st", r), []), "m_da")
            t_bu = q.dve(lambda e: e.tensor_tensor(bu[r][:, :], ps_x[i][:, :], brep[k][:, :], ALU.mult),
                         [t] + old["bc", b] + old.get(("st", r), []), "m_bu")
            old["px", i] = [t_bu]
            t = q.dve(lambda e: e.tensor_tensor_scan(st[r][:, :], da[r][:, :], bu[r][:, :], 0.0, ALU.mult, ALU.add),
                      [t_bu, t_da] + old.get(("hp", r), []), "m_scan")
            old["st", r] = [t]
            t = q.pool(lambda e: e.tensor_tensor(hc[r][:, :], st[r][:, :], crep[k][:, :], ALU.mult),
                       [t] + old.get(("hc", r), []) + old["bc", b], "m_hc")
            old["hp", r] = [t]
            if len(pend) == LAG:
                gather(*pend.pop(0))
            pend.append((b, g, r, t))

        LAG = 2
        for _ in prepare(0):
            pass
        for i in range(2):
            t_sel = q.dve(lambda e, i=i: e.tensor_copy(sel[:, i * half:(i + 1) * half], (sel_in, y)[i][:, :]), [sel_done[i]], "m_sel")
        for b in range(BATCH):
            ahead = prepare(b + 1) if b + 1 < BATCH else iter(())
            for g in range(NG):
                if added and g > LAG:
                    row_stats(q, x, stats, mv, *added.pop(0))
                if later and g > LAG:
                    output(*later.pop(0))
                elif g > LAG:
                    next(ahead, None)
                    if g % 2:
                        next(ahead, None)
                group(b, g)
            for _ in ahead:
                pass
        for item in pend:
            gather(*item)
        for item in later:
            output(*item)
        for item in added:
            row_stats(q, x, stats, mv, *item)
        q.run()


def program(nc, a, out):
    with ExitStack() as ctx:
        q = Queues(nc, ctx)

        def sb(name, shape, dt=F32):
            return ctx.enter_context(nc.sbuf_tensor(name, shape, dt))
        ident, ident_b = sb("ident", [P, P]), sb("ident_b", [P, P], BF16)
        eps = sb("eps", [P, 1])

        def banks(ctx, name, n):
            ps = ctx.enter_context(nc.psum_tensor(name, [P, n, BANK], F32))
            return ps, [ps[:, i, :] for i in range(n)]

        stats, mv = sb("stats", [P, TILES, 6]), sb("mv", [P, TILES, 2])
        first_h = sb("first_h", [P, TOK])
        mod_t = [sb(f"mod_t{i}", [P, 6, BATCH]) for i in range(2)]
        gates = [[sb(f"gate0{w}", [P, BATCH, HID]) for w in range(2)]]

        slots_in, slots_out = ([nc.dram_tensor(f"{n}{k}", (E1 * CAPACITY, HID), F32, kind="Internal").ap()
                                for k in range(2)] for n in ("slots_in", "slots_out"))
        zeros = sb("zeros", [P, 1, HID])
        t_zero = q.pool(lambda e: e.memset(zeros[:, :, :], 0.0), (), "zeros")

        with ExitStack() as attn:
            with ExitStack() as own:
                q.dma(ident[:, :], a["ident"], "in0")
                weights = attention_tensors(nc, attn)
                x_in = own.enter_context(nc.sbuf_tensor("x_in", [P, TILES, HID], F32))
                t = q.dma(x_in[:, :, :], a["x"].rearrange("b (t p) n -> p (b t) n", p=P), "in0")
                q.dve(lambda e: e.tensor_copy(ident_b[:, :], ident[:, :]), [t], "c0")
                q.dve(lambda e: e.memset(eps[:, :], EPS), (), "c0")
                row_stats(q, x_in, stats, mv, range(TILES), [t])
                with ExitStack() as first:
                    modulation(q, nc, first, banks(first, "ps_mod0", 3)[1], 0, a["c_t0"], a["wmod0"], mod_t[0], gates[0])
                    load_attention(q, a, weights)
                    q.run()
                for k in range(2):
                    t_zero = q.dma(slots_in[k].rearrange("(s p) n -> p s n", p=P),
                                   zeros[:, :, :].to_broadcast([P, E1 * CAPACITY // P, HID]), "slots_zero", [t_zero])
                layernorm_t(q, nc, own, banks(own, "ps_ln0", 4)[1], "0", x_in, mv, (), mod_t[0], 0, 1, first_h, ident, eps)
                q.run()
            q.put("sync", lambda e: e.nop(), [t_zero])
            attention(q, nc, a, weights, first_h, gates[0][0], ident, ident_b, stats, mv)
        x = first_h[:, :].rearrange("p (t n) -> p t n", n=HID)
        h_t = sb("h_t", [P, TOK])
        gates.append([sb(f"gate1{w}", [P, BATCH, HID]) for w in range(2)])
        rows_bc = [sb(f"rows_bc{w}", [P, BATCH, HID]) for w in range(2)]
        w_in = sb("w_in", [P, 2 * HID])
        gate, iota = sb("gate_0", [P, E0]), sb("iota_0", [P, E0])
        with ExitStack() as own:
            def ob(name, shape, dt=F32):
                return own.enter_context(nc.sbuf_tensor(name, shape, dt))
            NC = E0 * F0 // P
            w1 = ob("w1_0", [P, 2 * E0 * F0])
            w1_hi, w1_lo = (ob(f"w1_0{n}", [P, 2 * E0 * F0], F32R) for n in ("hi", "lo"))
            h_hi, h_lo = (ob(f"h_t{n}", [P, TOK], F32R) for n in ("hi", "lo"))
            w2 = ob("w2_0", [P, NC, HID])
            rows_in, rows = ob("rows_in", [2 * E0, E0 * F0]), ob("expert_rows", [P, E0 * F0], F32R)
            q.dma(gate[:, :], a["gate_w"], "in1")
            t_gate = q.dma(iota[:, :], a["iota"], "in1")
            t_w1 = q.dma(w1[:, :].rearrange("h (s e f) -> h s e f", s=2, e=E0)[:, 0, :, :],
                         a["w1_0"].rearrange("e h (s f) -> h s e f", s=2)[:, 0, :, :], "in1_w1")
            t_w1 = q.dma(w1[:, :].rearrange("h (s e f) -> h s e f", s=2, e=E0)[:, 1, :, :],
                         a["w1_0"].rearrange("e h (s f) -> h s e f", s=2)[:, 1, :, :], "in1_w1")
            q.dma(rows_in[:, :], a["expert_rows"], "in1_w2")
            t_w2 = q.dma(w2[:, :, :], a["w2_0"].rearrange("e f n -> (e f) n").rearrange("(c p) n -> p c n", p=P), "in1_w2")
            t = q.pool(lambda e: e.memset(rows[:, :].bitcast(F32), 0.0), (), "rows_zero")
            ps, each = banks(own, "ps_moe0", 7)
            ps_route = own.enter_context(nc.psum_tensor("ps_route0", [P, TILES, E0], F32))
            h_done = layernorm_t(q, nc, own, each[0:4], "1", x, mv, (), mod_t[0], 3, 4, h_t, ident, eps,
                                 use=scores(q, ps_route, h_t, gate, t_gate))
            h_split = split_parts(q, "hs0", h_t, h_hi, h_lo, BANK, (), h_done)
            w_split = split_parts(q, "ws0", w1, w1_hi, w1_lo, E0 * F0, [t_w1])
            combine, picked = route(q, nc, "0", own, ps_route, iota)
            modulation(q, nc, own, each[4:7], 1, a["c_t1"], a["wmod1"], mod_t[1], gates[1], rows_bc)
            t_rows = q.dve(lambda e: e.tensor_copy(rows[0:2 * E0, :], rows_in[:, :]), [t, t_w2], "rows_copy")
            q.run()
            experts(q, nc, ps, x, (h_hi, h_lo, h_split), ((w1_hi, w1_lo, w_split + [t_rows, t_w2]), w2), combine, picked, rows,
                    gates[0][1], ident, stats, mv)

        with ExitStack() as own:
            t = q.dma(w_in[:, :], a["w_in"], "mamba_w_in")
            layernorm_t(q, nc, own, banks(own, "ps_ln2", 4)[1], "2", x, mv, (), mod_t[1], 0, 1, h_t, ident, eps)
            q.put("sync", lambda e: e.nop(), [t])
            q.run()
        selective_scan(q, nc, a, w_in, x, h_t, gates[1][0], stats, mv)
        with ExitStack() as own:
            h = own.enter_context(nc.sbuf_tensor("h_nat", [P, TILES, HID], F32))
            w2 = own.enter_context(nc.sbuf_tensor("w2_1", [P, E1, F1 // P, HID], F32))
            gate = own.enter_context(nc.sbuf_tensor("gate_1", [P, E1], F32))
            tri = own.enter_context(nc.sbuf_tensor("tri", [P, P], F32))
            bias = own.enter_context(nc.sbuf_tensor("bias", [P, 1, HID], F32))
            t_gate = q.dma(gate[:, :], a["router_w"], "in2_gate")
            q.dma(tri[:, :], a["tri"], "in2")
            q.dma(bias[:, :, :], a["bias"].to_broadcast([P, 1, HID]), "in2")
            t = q.dma(w2[:, :, :, :], a["w2_1"].rearrange("e (c f) n -> f e c n", f=P), "in2")
            w1 = own.enter_context(nc.sbuf_tensor("w1_1", [P, E1 * F1], F32))
            w1_hi, w1_lo = (own.enter_context(nc.sbuf_tensor(f"w1_1{n}", [P, E1 * F1], F32R)) for n in ("hi", "lo"))
            t_w1 = q.dma(w1[:, :].rearrange("h (e f) -> h e f", e=E1), a["w1_1"].rearrange("e h f -> h e f"), "in2_w1")
            ps_route = own.enter_context(nc.psum_tensor("ps_route1", [P, TILES, E1], F32))
            with ExitStack() as norm:
                layernorm_t(q, nc, norm, banks(norm, "ps_ln3", 4)[1], "3", x, mv, (), mod_t[1], 3, 4, h_t, ident, eps, rows_bc, h,
                            scores(q, ps_route, h_t, gate, t_gate))
                q.run()
            w_done = split_parts(q, "ws1", w1, w1_hi, w1_lo, F1, [t_w1])
            scattered = []
            slot, weight = route(q, nc, "1", own, ps_route, iota, t, tri, CAPACITY,
                                 lambda slot, k, token: scattered.append(scatter(q, h, slot, k, slots_in, token)))
            capacity_experts(q, nc, t, x, slot, weight, scattered, (w1_hi, w1_lo, w_done), w2, bias, gates[1][1], ident,
                             slots_in, slots_out, out)


def constants():
    inv = (1.0 / THETA ** (np.arange(0, D, 2, dtype=np.float32) / np.float32(D))).astype(np.float32)
    freqs = np.arange(SEQ, dtype=np.float32)[:, None] * inv[None, :]
    emb = np.concatenate([freqs, freqs], axis=-1)[:, 0::2].astype(np.float32)
    cos, sin = np.cos(emb).T, np.sin(emb).T
    cos = np.repeat(cos, 2, axis=0)
    sin = np.repeat(sin, 2, axis=0) * np.tile(np.array([-1.0, 1.0], np.float32), D // 2)[:, None]
    i = np.arange(P)
    later = (i[None, :] > i[:, None]).astype(np.float32)
    fg = P // NST
    j = np.arange(HID // fg * P)
    w = np.arange(2 * P - fg)
    return {
        "cos": np.tile(cos, (2, 1)).astype(np.float32),
        "sin": np.tile(sin, (2, 1)).astype(np.float32),
        "masks": np.stack([later * np.float32(NEG), later.T * np.float32(NEG)], axis=1).astype(np.float32),
        "ident": np.eye(P, dtype=np.float32),
        "tri": later,
        "expert_rows": np.tile(np.arange(E0 * F0)[None, :] // F0 == np.arange(E0)[:, None], (2, 1)).astype(np.float32),
        "iota": np.tile(np.arange(E0, dtype=np.float32), (P, 1)),
        "sel": (i[:, None] == j[None, :] // NST).astype(np.float32),
        "fold": (w[None, :] == P - fg + i[:, None] // NST).astype(np.float32),
    }


def kernel(**inputs):
    import concourse.bacc as bacc
    from concourse.bass_utils import run_bass_kernel_spmd

    arr = {k: np.asarray(v) for k, v in inputs.items()}

    fields = {
        "x": arr["L0_attn_hidden_states"],
        "wq": arr["L0_attn_Wq"], "wk": arr["L0_attn_Wk"], "wv": arr["L0_attn_Wv"], "wo": arr["L0_attn_Wo"],
        "gate_w": arr["L0_ffn_gate_w"].T, "w1_0": arr["L0_ffn_w1"], "w2_0": arr["L0_ffn_w2"],
        "c_t0": arr["L0_c"].T, "wmod0": arr["L0_wmod"],
        "w_in": arr["L1_attn_W_in"], "conv_w": arr["L1_attn_conv_w"].reshape(HID, TAPS),
        "conv_b": arr["L1_attn_conv_b"].reshape(HID, 1), "w_xproj": arr["L1_attn_W_xproj"],
        "log_a": arr["L1_attn_log_A"].reshape(HID * NST // P, P).T,
        "d_param": arr["L1_attn_D_param"].reshape(HID, 1), "w_out": arr["L1_attn_W_out"],
        "router_w": arr["L1_ffn_router_w"], "w1_1": arr["L1_ffn_w1"], "w2_1": arr["L1_ffn_w2"],
        "bias": arr["L1_ffn_bias"].reshape(1, 1, HID),
        "c_t1": arr["L1_c"].T, "wmod1": arr["L1_wmod"],
        **constants(),
    }
    nc = bacc.Bacc("TRN2", target_bir_lowering=False, num_devices=1)
    arrays, aps = {}, {}
    for name, value in fields.items():
        value = np.ascontiguousarray(value)
        arrays[f"in_{name}"] = value
        aps[name] = nc.dram_tensor(f"in_{name}", value.shape, mybir.dt.from_np(value.dtype), kind="ExternalInput").ap()
    out = nc.dram_tensor("out_x", (BATCH, SEQ, HID), F32, kind="ExternalOutput").ap()
    program(nc, aps, out)
    result = run_bass_kernel_spmd(nc, [arrays], core_ids=[0])
    return result.results[0]["out_x"]
```
